# Optimizing a Trainium2 kernel written in Bass

```python
import numpy as np
import jax
import jax.numpy as jnp

def _softmax(x, axis=-1):
    return jax.nn.softmax(x, axis=axis)

def _gelu(x):
    return jax.nn.gelu(x, approximate=True)

def _silu(x):
    return jax.nn.silu(x)

def _sigmoid(x):
    return jax.nn.sigmoid(x)

def _layernorm(x, axis=-1, eps=1e-05):
    m = jnp.mean(x, axis=axis, keepdims=True)
    v = jnp.var(x, axis=axis, keepdims=True)
    return (x - m) / jnp.sqrt(v + eps)

def _scatter_add(tgt, idx, src, axis=0):
    return tgt.at[idx].add(src)

def _segment_sum(src, seg, n):
    return jax.ops.segment_sum(src, seg, n)
kernel_name = 'mk_xattn_ffn_d1_seqx_r4_f1724b'

def setup_inputs(seed: int=0):
    np.random.seed(seed)
    _w = jnp.asarray

    def _rec_inputs():
        import jax
        import jax.numpy as jnp
        _rk = jax.random.key(seed)
        x = 0.0003765 + 1 * jax.random.normal(jax.random.fold_in(_rk, 1), (16, 256, 512), jnp.float32)
        _lenS = 256 - jax.random.randint(jax.random.fold_in(_rk, 7), (16,), 0, max(1, 256 // 4) + 1, jnp.int32)
        _lenS2 = 256 - jax.random.randint(jax.random.fold_in(_rk, 8), (16,), 0, max(1, 256 // 4) + 1, jnp.int32)
        _ctx_2048P = jax.random.normal(jax.random.fold_in(_rk, 11), (16, 16, 512), jnp.float32)
        _ctx_2048c = jax.random.dirichlet(jax.random.fold_in(_rk, 511), 0.3 * jnp.ones((16,), jnp.float32), (16, 256))
        _ctx_2048t = jnp.einsum('bsk,bkd->bsd', _ctx_2048c, _ctx_2048P)
        _ctx_2048t = _ctx_2048t * jax.lax.rsqrt(jnp.mean(jnp.square(_ctx_2048t)) + 1e-12) * 0.953939
        ctx_2048 = -0.000292821 + 1.00034 * (_ctx_2048t + 0.3 * jax.random.normal(jax.random.fold_in(_rk, 611), (16, 256, 512), jnp.float32))
        return (x, ctx_2048)
    x, ctx_2048 = _rec_inputs()

    def _L0_xattn_setup():
        import jax, jax.numpy as jnp
        import numpy as np
        key = jax.random.key(seed)
        k1, k2, k3, k4, k5 = jax.random.split(key, 5)
        B, D_MODEL, L = (2, 256, 512)
        HEAD_DIM = 8
        H = D_MODEL // HEAD_DIM
        return {'k': jax.random.normal(k1, (B, D_MODEL, L), dtype=jnp.float32), 'v': jax.random.normal(k2, (B, D_MODEL, L), dtype=jnp.float32), 'q': jax.random.normal(k3, (B, D_MODEL, L), dtype=jnp.float32), 'ssm_kernel': jax.random.normal(k4, (H, L), dtype=jnp.float32), 'D': jax.random.normal(k5, (H,), dtype=jnp.float32), 'head_dim': HEAD_DIM}
    _L0_xattn_all = _L0_xattn_setup()
    _L0_xattn_in = {k: v for k, v in _L0_xattn_all.items() if k in ('ssm_kernel', 'D')}
    del _L0_xattn_all

    def _L0_ffn_setup():
        import jax, jax.numpy as jnp
        import numpy as np
        DIM = 512
        EXPERT_DIM = 256
        N_EXPERTS = 16
        TOPK = 2
        N_SHARED = 1
        B, T = (4, 512)
        key = jax.random.key(seed)
        ks = jax.random.split(key, 9)
        s = 0.02
        return {'x': jax.random.normal(ks[0], (B, T, DIM), jnp.float32), 'router_w': jax.random.normal(ks[1], (N_EXPERTS, DIM), jnp.float32) * s, 'router_bias': jnp.zeros((N_EXPERTS,), jnp.float32), 'Wu': jax.random.normal(ks[2], (N_EXPERTS, DIM, EXPERT_DIM), jnp.float32) * s, 'Wg': jax.random.normal(ks[3], (N_EXPERTS, DIM, EXPERT_DIM), jnp.float32) * s, 'Wd': jax.random.normal(ks[4], (N_EXPERTS, EXPERT_DIM, DIM), jnp.float32) * s, 'Su': jax.random.normal(ks[5], (N_SHARED, DIM, EXPERT_DIM * TOPK), jnp.float32) * s, 'Sg': jax.random.normal(ks[6], (N_SHARED, DIM, EXPERT_DIM * TOPK), jnp.float32) * s, 'Sd': jax.random.normal(ks[7], (N_SHARED, EXPERT_DIM * TOPK, DIM), jnp.float32) * s}
    _L0_ffn_all = _L0_ffn_setup()
    _L0_ffn_in = {k: v for k, v in _L0_ffn_all.items() if k in ('router_w', 'router_bias', 'Wu', 'Wg', 'Wd', 'Su', 'Sg', 'Sd')}
    del _L0_ffn_all
    return {'x': x, 'ctx_2048': ctx_2048, 'L0_xattn_ssm_kernel': _L0_xattn_in['ssm_kernel'], 'L0_xattn_D': _L0_xattn_in['D'], 'L0_ffn_router_w': _L0_ffn_in['router_w'], 'L0_ffn_router_bias': _L0_ffn_in['router_bias'], 'L0_ffn_Wu': _L0_ffn_in['Wu'], 'L0_ffn_Wg': _L0_ffn_in['Wg'], 'L0_ffn_Wd': _L0_ffn_in['Wd'], 'L0_ffn_Su': _L0_ffn_in['Su'], 'L0_ffn_Sg': _L0_ffn_in['Sg'], 'L0_ffn_Sd': _L0_ffn_in['Sd']}

def reference(x, ctx_2048, L0_xattn_ssm_kernel, L0_xattn_D, L0_ffn_router_w, L0_ffn_router_bias, L0_ffn_Wu, L0_ffn_Wg, L0_ffn_Wd, L0_ffn_Su, L0_ffn_Sg, L0_ffn_Sd):
    import jax
    import jax.numpy as jnp

    def _L0_xattn_ref(k, v, q, ssm_kernel, D, head_dim):
        import jax, jax.numpy as jnp
        import numpy as np
        B, HD, L = k.shape
        H = HD // head_dim
        fft_size = 2 * L
        k_ = k.reshape(B, H, head_dim, L)
        v_ = v.reshape(B, H, head_dim, L)
        q_ = q.reshape(B, H, head_dim, L)
        kv = jnp.einsum('bhil,bhjl->bijhl', k_, v_)
        kv_f = jnp.fft.rfft(kv, n=fft_size)
        kernel_f = jnp.fft.rfft(ssm_kernel, n=fft_size)
        y = jnp.fft.irfft(kv_f * kernel_f, n=fft_size)[..., :L]
        out = y + kv * D[None, None, None, :, None]
        out = jnp.einsum('bijhl,bhil->bjhl', out, q_)
        out = jnp.transpose(out, (0, 2, 1, 3)).reshape(B, H * head_dim, L)
        return out.astype(k.dtype)

    def _L0_ffn_ref(x, router_w, router_bias, Wu, Wg, Wd, Su, Sg, Sd):
        import jax, jax.numpy as jnp
        import numpy as np
        DIM = 512
        EXPERT_DIM = 256
        N_EXPERTS = 16
        TOPK = 2
        N_SHARED = 1
        B, T = (4, 512)
        Bx, Tx, D = x.shape
        flat = x.reshape(Bx * Tx, D)
        logits = flat @ router_w.T
        scores = jax.nn.softmax(logits, axis=-1)
        _, topk_idx = jax.lax.top_k(logits + router_bias, TOPK)
        topk_scores = jnp.take_along_axis(scores, topk_idx, axis=-1)
        topk_scores = topk_scores / topk_scores.sum(-1, keepdims=True)
        combine = jnp.einsum('nk,nke->ne', topk_scores, jax.nn.one_hot(topk_idx, N_EXPERTS, dtype=scores.dtype))
        out = jnp.zeros_like(flat)
        for e in range(N_EXPERTS):
            h = jax.nn.silu(flat @ Wu[e]) * (flat @ Wg[e])
            out = out + combine[:, e:e + 1] * (h @ Wd[e])
        for s in range(N_SHARED):
            out = out + jax.nn.silu(flat @ Su[s]) * (flat @ Sg[s]) @ Sd[s]
        return out.reshape(Bx, Tx, D)
    x = x + _L0_xattn_ref(ctx_2048, ctx_2048, _layernorm(x, axis=-1), L0_xattn_ssm_kernel, L0_xattn_D, 8)
    x = x + _L0_ffn_ref(_layernorm(x, axis=-1), L0_ffn_router_w, L0_ffn_router_bias, L0_ffn_Wu, L0_ffn_Wg, L0_ffn_Wd, L0_ffn_Su, L0_ffn_Sg, L0_ffn_Sd)
    return x

_drawn_inputs = setup_inputs


def setup_inputs(seed=0):
    import zlib

    import numpy as np

    out = dict(_drawn_inputs(seed))
    spreads = {'L0_ffn_router_bias': (0.0, 0.8)}
    factors = {'L0_ffn_router_w': 8.0,
     'L0_ffn_Wu': 8.0,
     'L0_ffn_Wg': 8.0,
     'L0_ffn_Wd': 8.0,
     'L0_ffn_Su': 8.0,
     'L0_ffn_Sg': 8.0,
     'L0_ffn_Sd': 8.0}
    for name, (base, spread) in spreads.items():
        noise = np.random.default_rng([zlib.crc32(name.encode()), seed]).standard_normal(out[name].shape)
        drawn = base * np.exp(spread * noise) if base else spread * noise
        out[name] = jnp.asarray(drawn.astype(out[name].dtype))
    for name, factor in factors.items():
        out[name] = (out[name] * factor).astype(out[name].dtype)
    return out
```

```python
from contextlib import ExitStack, contextmanager

import concourse.bass as bass
from concourse import mybir

ALU = mybir.AluOpType
ACT = mybir.ActivationFunctionType
F32 = mybir.dt.float32
F32R = mybir.dt.float32r
U32 = mybir.dt.uint32
I32 = mybir.dt.int32
AX_X = mybir.AxisListType.X

P = 128
EPS = 1e-5
HALVES = 2



def three_passes(nc, out, w_hi, w_lo, x_hi, x_lo, first, last):
    nc.tensor.matmul(out, w_hi, x_hi, start=first, stop=False)
    nc.tensor.matmul(out, w_lo, x_hi, start=False, stop=False)
    return nc.tensor.matmul(out, w_hi, x_lo, start=False, stop=last)


def f32(ap):
    return ap.bitcast(F32)


@contextmanager
def phase_semaphores(nc):
    taken = []

    def take(name):
        taken.append(nc.alloc_semaphore(name=name))
        return taken[-1]

    yield take
    nc.clear_and_free_semaphores(taken)
    nc.all_engine_barrier()


class Shapes:

    def __init__(self, x, taps, router, wu):
        self.B, self.S, self.L = x.shape
        self.H = taps.shape[0]
        self.C = self.S // self.H
        self.T = self.B * self.S
        self.LC = self.L // P
        self.TT = self.T // P
        self.E = router.shape[0]
        self.F = wu.shape[2]
        self.HB = self.B // HALVES
        self.HT = self.HB * self.S // P
        self.CE = self.C + self.C // 2
        self.ND = self.C // 2 + 1
        self.NP = self.ND * self.C
        self.R = 2 * P
        most = 2 * self.T // self.R + self.E - 1
        self.NT = most + most % 2
        self.RB = self.L + P


def prepare(nc, sh, taps, skip, taps_rev, ident, eps, zero):
    H, L, RB = sh.H, sh.L, sh.RB
    with ExitStack() as ctx:
        take = ctx.enter_context(phase_semaphores(nc))

        raw = ctx.enter_context(nc.sbuf_tensor("taps_raw", [H, L], F32))
        rev = ctx.enter_context(nc.sbuf_tensor("taps_reversed", [H, RB], F32))
        d = ctx.enter_context(nc.sbuf_tensor("skip_weight", [H, 1], F32))
        loaded = take("taps_loaded")
        d_loaded = take("skip_loaded")
        cleared = take("reversed_cleared")
        turned = take("taps_turned")
        added = take("skip_added")
        stored = take("taps_stored")
        blank = take("identity_blank")
        block = ctx.enter_context(nc.Block())

        @block.sync
        def _(sp):
            sp.dma_start(raw[:, :], taps).then_inc(loaded, 16)
            sp.dma_start(d[:, :], skip.rearrange("(h a) -> h a", a=1)).then_inc(d_loaded, 16)
            sp.wait_ge(added, 1)
            sp.dma_start(taps_rev, rev[:, :]).then_inc(stored, 16)
            sp.wait_ge(stored, 16)

        @block.gpsimd
        def _(pool):
            nc.gpsimd.memset(ident[:, :], 0.0).then_inc(blank, 1)
            pool.wait_ge(blank, 1)
            nc.gpsimd.affine_select(out=ident[:, :], in_=ident[:, :], compare_op=ALU.not_equal, fill=1.0,
                                    base=0, pattern=[[-1, P]], channel_multiplier=1)

        @block.vector
        def _(dve):
            nc.vector.memset(eps[:, :], EPS)
            nc.vector.memset(zero[:, :], 0.0)
            nc.vector.memset(rev[:, L:RB], 0.0).then_inc(cleared, 1)
            dve.wait_ge(loaded, 16)
            nc.vector.tensor_copy(rev[:, 0:L], raw[:, ::-1]).then_inc(turned, 1)
            dve.wait_ge(turned, 1)
            dve.wait_ge(cleared, 1)
            dve.wait_ge(d_loaded, 16)
            nc.vector.tensor_tensor(rev[:, L - 1:L], rev[:, L - 1:L], d[:, :], ALU.add).then_inc(added, 1)


def bring_in(nc, sh, half, x, ctx_rows, cT, qT, ident, eps):
    L, LC, HB, H, C, CE = sh.L, sh.LC, sh.HB, sh.H, sh.C, sh.CE
    row0 = half * sh.HT * P
    NK = sh.S // P
    with ExitStack() as ctx:
        take = ctx.enter_context(phase_semaphores(nc))

        def sb(name, shape):
            return ctx.enter_context(nc.sbuf_tensor(f"{name}_in{half}", shape, F32))

        def sem(name):
            return take(f"{name}_in{half}")

        xin = sb("x_rows", [P, NK, L])
        cin = sb("c_rows", [P, NK, L])
        xn = sb("x_normed", [P, NK, L])
        stats = sb("stats", [P, NK, 6])
        mv = sb("mean_var", [P, NK, 2])
        std, rstd = sb("std", [P, NK, 1]), sb("rstd", [P, NK, 1])
        std_done = sem("std_done")
        holds = sem("holds")
        psC = [ctx.enter_context(nc.psum_tensor(f"turned_c{k}_in{half}", [P, L], F32)) for k in range(NK)]
        psX = [ctx.enter_context(nc.psum_tensor(f"turned_x{k}_in{half}", [P, L], F32)) for k in range(NK)]
        x_loaded = [sem(f"x_loaded{k}") for k in range(NK)]
        c_loaded = [sem(f"c_loaded{k}") for k in range(NK)]
        stats_done, mean_done, rstd_done = sem("stats_done"), sem("mean_done"), sem("rstd_done")
        x_normed, c_turned, x_turned = sem("x_normed"), sem("c_turned"), sem("x_turned")
        c_kept, x_kept = sem("c_kept"), sem("x_kept")
        block = ctx.enter_context(nc.Block())

        def keep(engine_copy, dst, src, i, k, done):
            heads = P // C
            d0 = dst[:, :, bass.ds(i * (H * CE) + k * heads * CE, heads * CE)]
            d0 = d0.rearrange("p c (h r) -> p c h r", r=CE)
            s0 = src[:, :].rearrange("p (c h r) -> p c h r", c=LC, r=C)
            engine_copy(d0[:, :, :, 0:C], s0)
            engine_copy(d0[:, :, :, C:CE], s0[:, :, :, 0:CE - C]).then_inc(done, 1)

        cTv = cT[:, :].rearrange("p (c n) -> p c n", c=LC)
        qTv = qT[:, :].rearrange("p (c n) -> p c n", c=LC)

        @block.sync
        def _(sp):
            with sp.Fori(0, HB) as i:
                for k in range(NK):
                    row = i * (NK * P) + (row0 + k * P)
                    sp.wait_ge(x_normed, i * NK + k + 1)
                    sp.dma_start(xin[:, k, :], x[bass.ds(row, P), :]).then_inc(x_loaded[k], 16)
                    sp.wait_ge(c_turned, i * NK + k + 1)
                    sp.dma_start(cin[:, k, :], ctx_rows[bass.ds(row, P), :]).then_inc(c_loaded[k], 16)

        @block.vector
        def _(dve):
            dve.sem_inc(x_normed, NK)
            dve.sem_inc(x_kept, NK)
            with dve.Fori(0, HB) as i:
                for k in range(NK):
                    n = i * NK + k + 1
                    dve.wait_ge(x_loaded[k], i * 16 + 16)
                    nc.vector.bn_stats(stats[:, k, :], xin[:, k, :]).then_inc(stats_done, 1)
                    dve.wait_ge(stats_done, n)
                    dve.sem_inc(holds, 1)
                    nc.vector.bn_aggr(mv[:, k, :], stats[:, k, :]).then_inc(mean_done, 1)
                for k in range(NK):
                    n = i * NK + k + 1
                    dve.wait_ge(std_done, n)
                    nc.vector.reciprocal(rstd[:, k, :], std[:, k, :]).then_inc(rstd_done, 1)
                    dve.wait_ge(rstd_done, n)
                    dve.wait_ge(x_turned, n)
                    nc.vector.tensor_scalar(xn[:, k, :], xin[:, k, :], mv[:, k, 0:1], rstd[:, k, :],
                                            ALU.subtract, ALU.mult).then_inc(x_normed, 1)
                for k in range(NK):
                    dve.wait_ge(x_turned, i * NK + k + 1 + NK)
                    keep(nc.vector.tensor_copy, qTv, psX[k], i, k, x_kept)

        @block.scalar
        def _(act):
            act.sem_inc(c_kept, NK)
            with act.Fori(0, HB) as i:
                for k in range(NK):
                    act.wait_ge(mean_done, i * NK + k + 1)
                    nc.scalar.activation(std[:, k, :], mv[:, k, 1:2], ACT.Sqrt, bias=eps[:, :]).then_inc(std_done, 1)
                for k in range(NK):
                    act.wait_ge(c_turned, i * NK + k + 1 + NK)
                    keep(nc.scalar.copy, cTv, psC[k], i, k, c_kept)

        @block.tensor
        def _(pe):
            pe.sem_inc(c_turned, NK)
            pe.sem_inc(x_turned, NK)
            with pe.Fori(0, HB) as i:
                for k in range(NK):
                    n = i * NK + k + 1
                    pe.wait_ge(c_loaded[k], i * 16 + 16)
                    pe.wait_ge(c_kept, n)
                    for c in range(LC):
                        last = nc.tensor.transpose(psC[k][:, c * P:(c + 1) * P], cin[:, k, c * P:(c + 1) * P], ident[:, :])
                    last.then_inc(c_turned, 1)
                    pe.wait_ge(x_normed, n + NK)
                    pe.wait_ge(x_kept, n)
                    for c in range(LC):
                        last = nc.tensor.transpose(psX[k][:, c * P:(c + 1) * P], xn[:, k, c * P:(c + 1) * P], ident[:, :])
                    last.then_inc(x_turned, 1)


def long_convolution(nc, sh, half, taps_rev, cT, qT, zero, slots, filled):
    L, LC, HB, H, C, CE, ND, NP = sh.L, sh.LC, sh.HB, sh.H, sh.C, sh.CE, sh.ND, sh.NP
    G = LC * HB
    GS = H * CE
    N = HB * NP
    with ExitStack() as ctx:
        take = ctx.enter_context(phase_semaphores(nc))

        def sb(name, shape):
            return [ctx.enter_context(nc.sbuf_tensor(f"{name}{k}_conv{half}", shape, F32)) for k in range(2)]

        def sem(name):
            return take(f"{name}_conv{half}")

        traw, toep = sb("taps_rows", [P, L]), sb("toeplitz", [P, L])
        kv = sb("row_products", [P, G * NP])
        z = sb("terms", [P, G * C * C])
        y = [ctx.enter_context(nc.psum_tensor(f"conv_out{k}_{half}", [P, LC, 512], F32)) for k in range(2)]
        t_loaded = [sem(f"t_loaded{k}") for k in range(2)]
        prod_done = sem("prod_done")
        t_ready, conv_done, terms_done = sem("t_ready"), sem("conv_done"), sem("terms_done")
        folded, summed, holds = sem("folded"), sem("summed"), sem("holds")
        block = ctx.enter_context(nc.Block())

        def head(t, h, pattern):
            v = t[:, bass.ds(h * CE, CE)]
            return bass.AP(tensor=v.tensor, offset=v.offset, ap=[list(v.ap[0])] + pattern)

        def terms(k):
            return z[k][:, :].rearrange("p (g t j) -> p g t j", t=C, j=C)

        @block.sync
        def _(sp):
            with sp.Fori(0, H // 2) as i:
                for k in range(2):
                    sp.wait_ge(t_ready, i * 2 + k + 1)
                    src = bass.AP(tensor=taps_rev.tensor, offset=taps_rev[bass.ds(i * 2 + k, 1), :].offset, ap=[[1, P], [1, L]])
                    sp.dma_start(traw[k][:, :], src).then_inc(t_loaded[k], 16)

        @block.gpsimd
        def _(pool):
            pool.sem_inc(folded, 2)

            def products(h, k):
                pool.wait_ge(conv_done, h + 1)
                nc.gpsimd.tensor_tensor(
                    kv[k][:, :].rearrange("p (g d j) -> p g d j", d=ND, j=C),
                    head(cT, h, [[GS, G], [0, ND], [1, C]]), head(cT, h, [[GS, G], [1, ND], [1, C]]),
                    ALU.mult).then_inc(prod_done, 1)

            def fold(h, k):
                pool.wait_ge(terms_done, h + 3)
                nc.gpsimd.tensor_tensor(terms(k)[:, :, 0:C - ND, :], terms(k)[:, :, 0:C - ND, :],
                                        terms(k)[:, :, ND:C, :], ALU.add).then_inc(folded, 1)

            products(0, 0)
            products(1, 1)
            with pool.Fori(0, H // 2 - 1) as i:
                for k in range(2):
                    products(i * 2 + 2 + k, k)
                    fold(i * 2 + k, k)
            fold(H - 2, 0)
            fold(H - 1, 1)

        @block.scalar
        def _(act):
            act.sem_inc(t_ready, 2)
            for c in range(half * slots.shape[0] // HALVES, (half + 1) * slots.shape[0] // HALVES):
                act.dma_start(slots[c], zero[:, :]).then_inc(filled, 16)
            with act.Fori(0, H // 2) as i:
                for k in range(2):
                    act.wait_ge(t_loaded[k], i * 16 + 16)
                    act.wait_ge(conv_done, i * 2 + k + 1)
                    nc.scalar.activation(toep[k][:, :], traw[k][:, ::-1], ACT.Copy).then_inc(t_ready, 1)

        @block.tensor
        def _(pe):
            pe.sem_inc(conv_done, 2)
            with pe.Fori(0, H // 2) as i:
                for k in range(2):
                    n = i * 2 + k + 1
                    pe.wait_ge(t_ready, n + 2)
                    pe.wait_ge(prod_done, n)
                    pe.wait_ge(terms_done, n)
                    for lc in range(LC):
                        for mc in range(lc + 1):
                            last = nc.tensor.matmul(y[k][:, lc, 0:N], toep[k][:, (lc - mc) * P:(lc - mc + 1) * P],
                                                    kv[k][:, mc * N:(mc + 1) * N], start=mc == 0, stop=mc == lc)
                    last.then_inc(conv_done, 1)

        @block.vector
        def _(dve):
            dve.sem_inc(terms_done, 2)
            dve.sem_inc(summed, 2)

            def multiply(h, k):
                dve.wait_ge(conv_done, h + 3)
                dve.wait_ge(summed, h + 1)
                zt = z[k][:, :].rearrange("p (c b t j) -> p c b t j", c=LC, b=HB, j=C)
                for c in range(LC):
                    src = y[k][:, c, 0:N].rearrange("p (b d j) -> p b d j", d=ND, j=C)
                    v = qT[:, bass.ds(h * CE + c * (HB * GS), CE)]
                    q = bass.AP(tensor=v.tensor, offset=v.offset, ap=[list(v.ap[0]), [GS, HB], [1, ND], [1, C]])
                    nc.vector.tensor_tensor(zt[:, c, :, 0:ND, :], src, q, ALU.mult)
                for d in range(1, ND - 1):
                    for lo, hi, off in ((0, C - d, d), (C - d, C, d - C)):
                        src = y[k][:, :, 0:N].rearrange("p c (b r) -> p c b r", r=NP)[:, :, :, d * C + lo:d * C + hi]
                        v = qT[:, bass.ds(h * CE + lo, CE - lo)]
                        q = bass.AP(tensor=v.tensor, offset=v.offset, ap=[list(v.ap[0]), [HB * GS, LC], [GS, HB], [1, hi - lo]])
                        last = nc.vector.tensor_tensor(zt[:, :, :, ND - 1 + d, lo + off:hi + off], src, q, ALU.mult)
                last.then_inc(terms_done, 1)

            def add_up(h, k):
                dve.wait_ge(folded, h + 3)
                dve.sem_inc(holds, 1)
                nc.vector.tensor_reduce(head(qT, h, [[GS, G], [1, C]]),
                                        terms(k)[:, :, 0:ND, :].rearrange("p g t j -> p g j t"), AX_X, ALU.add).then_inc(summed, 1)

            multiply(0, 0)
            with dve.Fori(0, H // 2 - 1) as i:
                multiply(i * 2 + 1, 1)
                add_up(i * 2, 0)
                multiply(i * 2 + 2, 0)
                add_up(i * 2 + 1, 1)
            multiply(H - 1, 1)
            add_up(H - 2, 0)
            add_up(H - 1, 1)


def close_attention(nc, sh, half, x, oT, x_mid, x_mid_normed, ident, eps):
    L, LC, HB, H, C, CE = sh.L, sh.LC, sh.HB, sh.H, sh.C, sh.CE
    row0 = half * sh.HT * P
    NK = sh.S // P
    heads = P // C
    with ExitStack() as ctx:
        take = ctx.enter_context(phase_semaphores(nc))

        def sb(name, shape):
            return ctx.enter_context(nc.sbuf_tensor(f"{name}_close{half}", shape, F32))

        def sem(name):
            return take(f"{name}_close{half}")

        xin, xm, xn = sb("x_rows", [P, NK, L]), sb("x_mid", [P, NK, L]), sb("x_normed", [P, NK, L])
        packed = sb("packed", [P, NK, L])
        stats, mv = sb("stats", [P, NK, 6]), sb("mean_var", [P, NK, 2])
        std, rstd = sb("std", [P, NK, 1]), sb("rstd", [P, NK, 1])
        std_done = sem("std_done")
        holds = sem("holds")
        ps = [ctx.enter_context(nc.psum_tensor(f"rows{k}_close{half}", [P, L], F32)) for k in range(NK)]
        x_loaded = [sem(f"x_loaded{k}") for k in range(NK)]
        mid_stored = [sem(f"mid_stored{k}") for k in range(NK)]
        normed_stored = [sem(f"normed_stored{k}") for k in range(NK)]
        stats_done, mean_done, rstd_done, normed = sem("stats_done"), sem("mean_done"), sem("rstd_done"), sem("normed")
        turned, added = sem("turned"), sem("added")
        gathered = sem("gathered")
        block = ctx.enter_context(nc.Block())
        oTv = oT[:, :].rearrange("p (c n) -> p c n", c=LC)

        @block.sync
        def _(sp):
            for k in range(NK):
                sp.sem_inc(mid_stored[k], 16)
                sp.sem_inc(normed_stored[k], 16)
            with sp.Fori(0, HB) as i:
                for k in range(NK):
                    n = i * NK + k + 1
                    row = i * (NK * P) + (row0 + k * P)
                    sp.wait_ge(added, n)
                    sp.dma_start(xin[:, k, :], x[bass.ds(row, P), :]).then_inc(x_loaded[k], 16)
                for k in range(NK):
                    n = i * NK + k + 1
                    row = i * (NK * P) + (row0 + k * P)
                    sp.wait_ge(added, n + NK)
                    sp.dma_start(x_mid[bass.ds(row, P), :], xm[:, k, :]).then_inc(mid_stored[k], 16)
                    sp.wait_ge(normed, n)
                    sp.dma_start(x_mid_normed[bass.ds(row, P), :], xn[:, k, :]).then_inc(normed_stored[k], 16)
            for k in range(NK):
                sp.wait_ge(mid_stored[k], 16 * (HB + 1))
                sp.wait_ge(normed_stored[k], 16 * (HB + 1))

        @block.scalar
        def _(act):
            with act.Fori(0, HB) as i:
                for k in range(NK):
                    act.wait_ge(turned, i * NK + k + 1)
                    src = oTv[:, :, bass.ds(i * (H * CE) + k * heads * CE, heads * CE)]
                    nc.scalar.copy(packed[:, k, :].rearrange("p (c h r) -> p c h r", c=LC, r=C),
                                   src.rearrange("p c (h r) -> p c h r", r=CE)[:, :, :, 0:C]).then_inc(gathered, 1)
                for k in range(NK):
                    act.wait_ge(mean_done, i * NK + k + 1)
                    nc.scalar.activation(std[:, k, :], mv[:, k, 1:2], ACT.Sqrt, bias=eps[:, :]).then_inc(std_done, 1)

        @block.tensor
        def _(pe):
            pe.sem_inc(turned, NK)
            with pe.Fori(0, HB) as i:
                for k in range(NK):
                    n = i * NK + k + 1
                    pe.wait_ge(gathered, n)
                    pe.wait_ge(added, n)
                    for c in range(LC):
                        last = nc.tensor.transpose(ps[k][:, c * P:(c + 1) * P], packed[:, k, c * P:(c + 1) * P], ident[:, :])
                    last.then_inc(turned, 1)

        @block.vector
        def _(dve):
            dve.sem_inc(added, NK)
            with dve.Fori(0, HB) as i:
                for k in range(NK):
                    n = i * NK + k + 1
                    dve.wait_ge(turned, n + NK)
                    dve.wait_ge(x_loaded[k], i * 16 + 16)
                    dve.wait_ge(mid_stored[k], i * 16 + 16)
                    nc.vector.tensor_tensor(xm[:, k, :], ps[k][:, :], xin[:, k, :], ALU.add).then_inc(added, 1)
                    dve.wait_ge(added, n + NK)
                    nc.vector.bn_stats(stats[:, k, :], xm[:, k, :]).then_inc(stats_done, 1)
                    dve.wait_ge(stats_done, n)
                    dve.sem_inc(holds, 1)
                    nc.vector.bn_aggr(mv[:, k, :], stats[:, k, :]).then_inc(mean_done, 1)
                for k in range(NK):
                    n = i * NK + k + 1
                    dve.wait_ge(std_done, n)
                    nc.vector.reciprocal(rstd[:, k, :], std[:, k, :]).then_inc(rstd_done, 1)
                    dve.wait_ge(rstd_done, n)
                    dve.wait_ge(normed_stored[k], i * 16 + 16)
                    nc.vector.tensor_scalar(xn[:, k, :], xm[:, k, :], mv[:, k, 0:1], rstd[:, k, :],
                                            ALU.subtract, ALU.mult).then_inc(normed, 1)


def shared_expert(nc, sh, x_mid, x_normed, router, wu, wg, wd, base, logits, ident, filled, stores):
    L, LC, E = sh.L, sh.LC, sh.E
    FS = wu.shape[1]
    FC = FS // P
    GT = 4
    GN = GT * P
    assert L == FS and GT == LC
    NG = sh.T // GN
    with ExitStack() as ctx:
        take = ctx.enter_context(phase_semaphores(nc))

        def sb(name, shape, dt=F32):
            return ctx.enter_context(nc.sbuf_tensor(f"{name}_shared", shape, dt))

        def pair(name, shape, dt=F32):
            return [sb(f"{name}{k}", shape, dt) for k in range(2)]

        def ps(name, shape):
            return ctx.enter_context(nc.psum_tensor(f"{name}_shared", shape, F32))

        def sem(name):
            return take(f"{name}_shared")

        stage = sb("weights", [P, LC, FS])
        whi = [sb(f"w{n}_hi", [P, LC, FS], F32R) for n in "ugd"]
        wlo = [sb(f"w{n}_lo", [P, LC, FS], F32R) for n in "ugd"]
        rraw = sb("router", [P, LC, E])
        rrows = sb("router_rows", [E, L])
        rhi, rlo = sb("router_hi", [P, LC, E], F32R), sb("router_lo", [P, LC, E], F32R)
        xn = pair("x_normed", [P, L])
        xhi, xlo = pair("xT_hi", [P, LC, GN], F32R), pair("xT_lo", [P, LC, GN], F32R)
        gate = pair("gated", [P, GN])
        h = pair("hidden", [P, GN])
        hhi, hlo = sb("hidden_hi", [P, FC, GN], F32R), sb("hidden_lo", [P, FC, GN], F32R)
        xm, out = pair("x_mid", [P, L]), pair("sum", [P, L])
        psT = [ps(f"turned{k}", [P, L]) for k in range(2)]
        psU, psG, psL = ps("up", [P, GN]), ps("gate", [P, GN]), ps("logits", [P, GT, E])
        psY = [ps(f"down{k}", [P, L]) for k in range(2)]
        w_loaded, w_hi, w_lo, r_loaded, r_turned, r_split = (sem("w_loaded"), sem("w_hi"), sem("w_lo"),
                                                             sem("r_loaded"), sem("r_turned"), sem("r_split"))
        xn_loaded = [sem(f"xn_loaded{k}") for k in range(2)]
        xm_loaded = [sem(f"xm_loaded{k}") for k in range(2)]
        stored = [sem(f"stored{k}") for k in range(2)]
        turned, x_hi, x_lo = sem("turned"), sem("x_hi"), sem("x_lo")
        up_done, gate_done, silu_done, h_done, h_hi, h_lo = (sem("up_done"), sem("gate_done"), sem("silu_done"),
                                                             sem("h_done"), sem("h_hi"), sem("h_lo"))
        logits_done, logits_kept, down_done, summed = sem("logits_done"), sem("logits_kept"), sem("down_done"), sem("summed")
        block = ctx.enter_context(nc.Block())

        @block.sync
        def _(sp):
            for k in range(2):
                sp.sem_inc(stored[k], 16)
            sp.wait_ge(filled, 16 * stores)
            sp.dma_start(rrows[:, :], router).then_inc(r_loaded, 16)
            for n, w in enumerate((wu, wg, wd)):
                if n:
                    sp.wait_ge(w_lo, n)
                sp.dma_start(stage[:, :, :], w.rearrange("(p c) n -> p c n", c=LC)).then_inc(w_loaded, 16)

            def rows(g, t):
                return bass.ds(g * GN + t * P, P)

            def load_normed(g):
                for t in range(GT):
                    sp.wait_ge(turned, g * GT + t + 1)
                    sp.dma_start(xn[t % 2][:, :], x_normed[rows(g, t), :]).then_inc(xn_loaded[t % 2], 16)

            def finish(g):
                for t in range(GT + 1):
                    if t < GT:
                        sp.wait_ge(summed, g * GT + t + 1)
                        sp.dma_start(xm[t % 2][:, :], x_mid[rows(g, t), :]).then_inc(xm_loaded[t % 2], 16)
                    if t:
                        sp.wait_ge(summed, g * GT + t + 2)
                        sp.dma_start(base[rows(g, t - 1), :], out[(t - 1) % 2][:, :]).then_inc(stored[(t - 1) % 2], 16)

            load_normed(0)
            with sp.Fori(0, NG - 1) as g:
                load_normed(g + 1)
                finish(g)
            finish(NG - 1)
            for k in range(2):
                sp.wait_ge(stored[k], 16 * (sh.TT // 2 + 1))

        @block.gpsimd
        def _(pool):
            pool.sem_inc(h_lo, 2)
            with pool.Fori(0, NG) as g:
                for fc in range(FC):
                    pool.wait_ge(h_hi, g * FC + fc + 1)
                    nc.gpsimd.tensor_tensor(hlo[:, fc, :], h[fc % 2][:, :], f32(hhi[:, fc, :]), ALU.subtract).then_inc(h_lo, 1)

        @block.scalar
        def _(act):
            act.sem_inc(silu_done, 1)
            act.sem_inc(logits_kept, 1)
            for n in range(3):
                act.wait_ge(w_loaded, 16 * (n + 1))
                nc.scalar.activation(whi[n][:, :, :], stage[:, :, :], ACT.Copy).then_inc(w_hi, 1)
            act.wait_ge(r_turned, 1)
            nc.scalar.activation(rhi[:, :, :], psL[:, :, :], ACT.Copy).then_inc(r_split, 1)

            def high(g, s):
                for t in range(GT):
                    act.wait_ge(turned, g * GT + t + 3)
                    nc.scalar.activation(xhi[s][:, :, t * P:(t + 1) * P],
                                         psT[t % 2][:, :].rearrange("p (c n) -> p c n", c=LC), ACT.Copy).then_inc(x_hi, 1)

            def hidden(g):
                for fc in range(FC):
                    act.wait_ge(up_done, g * FC + fc + 1)
                    act.wait_ge(h_done, g * FC + fc + 1)
                    nc.scalar.activation(gate[fc % 2][:, :], psU[:, :], ACT.Silu).then_inc(silu_done, 1)
                    act.wait_ge(h_done, g * FC + fc + 3)
                    if fc == 0:
                        act.wait_ge(down_done, g * GT + 1)
                    nc.scalar.activation(hhi[:, fc, :], h[fc % 2][:, :], ACT.Copy).then_inc(h_hi, 1)

            def logits_out(g):
                act.wait_ge(logits_done, g + 1)
                nc.scalar.copy(logits[:, bass.ds(g * (GT * E), GT * E)], psL[:, :, :].rearrange("p t e -> p (t e)")).then_inc(logits_kept, 1)

            high(0, 0)

            def body(g, s):
                hidden(g)
                logits_out(g)
                high(g + 1, 1 - s)

            hidden(0)
            logits_out(0)
            high(1, 1)
            with act.Fori(0, (NG - 2) // 2) as i:
                for k in range(2):
                    body(i * 2 + (1 + k), (1 + k) % 2)
            hidden(NG - 1)
            logits_out(NG - 1)

        @block.vector
        def _(dve):
            dve.sem_inc(h_done, 2)
            dve.sem_inc(x_lo, 2)
            dve.sem_inc(summed, 2)
            for n in range(3):
                dve.wait_ge(w_hi, n + 1)
                nc.vector.tensor_tensor(wlo[n][:, :, :], stage[:, :, :], f32(whi[n][:, :, :]), ALU.subtract).then_inc(w_lo, 1)
            dve.wait_ge(r_split, 1)
            nc.vector.tensor_tensor(rlo[:, :, :], psL[:, :, :], f32(rhi[:, :, :]), ALU.subtract).then_inc(r_split, 1)

            def low(g, s):
                for t in range(GT):
                    dve.wait_ge(x_hi, g * GT + t + 1)
                    nc.vector.tensor_tensor(xlo[s][:, :, t * P:(t + 1) * P],
                                            psT[t % 2][:, :].rearrange("p (c n) -> p c n", c=LC),
                                            f32(xhi[s][:, :, t * P:(t + 1) * P]), ALU.subtract).then_inc(x_lo, 1)

            def hidden(g):
                for fc in range(FC):
                    dve.wait_ge(gate_done, g * FC + fc + 1)
                    dve.wait_ge(silu_done, g * FC + fc + 2)
                    dve.wait_ge(h_lo, g * FC + fc + 1)
                    nc.vector.tensor_tensor(h[fc % 2][:, :], psG[:, :], gate[fc % 2][:, :], ALU.mult).then_inc(h_done, 1)

            def sums(g):
                for t in range(GT):
                    dve.wait_ge(down_done, g * GT + t + 2)
                    dve.wait_ge(xm_loaded[t % 2], (g * (GT // 2) + t // 2 + 1) * 16)
                    dve.wait_ge(stored[t % 2], (g * (GT // 2) + t // 2 + 1) * 16)
                    nc.vector.tensor_tensor(out[t % 2][:, :], psY[t % 2][:, :], xm[t % 2][:, :], ALU.add).then_inc(summed, 1)

            low(0, 0)
            with dve.Fori(0, (NG - 2) // 2) as i:
                for k in range(2):
                    g = i * 2 + k
                    hidden(g)
                    low(g + 1, 1 - k)
                    sums(g)
            hidden(NG - 2)
            low(NG - 1, 1)
            sums(NG - 2)
            hidden(NG - 1)
            sums(NG - 1)

        @block.tensor
        def _(pe):
            pe.sem_inc(turned, 2)
            pe.sem_inc(down_done, 1)
            pe.wait_ge(r_loaded, 16)
            for c in range(LC):
                last = nc.tensor.transpose(psL[:, c, :], rrows[:, c::LC], ident[0:E, 0:E])
            last.then_inc(r_turned, 1)

            def turn(g):
                for t in range(GT):
                    pe.wait_ge(xn_loaded[t % 2], (g * (GT // 2) + t // 2 + 1) * 16)
                    pe.wait_ge(x_lo, g * GT + t + 1)
                    for c in range(LC):
                        last = nc.tensor.transpose(psT[t % 2][:, c * P:(c + 1) * P], xn[t % 2][:, c::LC], ident[:, :])
                    last.then_inc(turned, 1)

            def up(g, s):
                pe.wait_ge(x_lo, g * GT + GT + 2)
                for fc in range(FC):
                    f = slice(fc, FS, FC)
                    for n, (bank, done) in enumerate(((psU, up_done), (psG, gate_done))):
                        pe.wait_ge((silu_done, h_done)[n], g * FC + fc + 1 + n)
                        for c in range(LC):
                            last = three_passes(nc, bank[:, :], whi[n][:, c, f], wlo[n][:, c, f],
                                                xhi[s][:, c, :], xlo[s][:, c, :], c == 0, c == LC - 1)
                        last.then_inc(done, 1)

            def route(g, s):
                pe.wait_ge(logits_kept, g + 1)
                for t in range(GT):
                    for c in range(LC):
                        col = slice(t * P, (t + 1) * P)
                        last = three_passes(nc, psL[:, t, :], xhi[s][:, c, col], xlo[s][:, c, col],
                                            rhi[:, c, :], rlo[:, c, :], c == 0, c == LC - 1)
                last.then_inc(logits_done, 1)

            def down(g, s):
                pe.wait_ge(h_lo, g * FC + FC + 2)
                for t in range(GT):
                    pe.wait_ge(summed, g * GT + t + 1)
                    col = slice(t * P, (t + 1) * P)
                    for fc in range(FC):
                        last = three_passes(nc, psY[t % 2][:, :], hhi[:, fc, col], hlo[:, fc, col],
                                            whi[2][:, fc, :], wlo[2][:, fc, :], fc == 0, fc == FC - 1)
                    last.then_inc(down_done, 1)

            turn(0)
            pe.wait_ge(w_lo, 3)
            pe.wait_ge(r_split, 2)
            with pe.Fori(0, (NG - 2) // 2) as i:
                for k in range(2):
                    g = i * 2 + k
                    up(g, k)
                    route(g, k)
                    turn(g + 1)
                    down(g, k)
            up(NG - 2, 0)
            route(NG - 2, 0)
            turn(NG - 1)
            down(NG - 2, 0)
            up(NG - 1, 1)
            route(NG - 1, 1)
            down(NG - 1, 1)


def routing(nc, sh, logits, bias, slots, weights, tile_expert):
    E, TT, NT, R = sh.E, sh.TT, sh.NT, sh.R
    with ExitStack() as ctx:
        take = ctx.enter_context(phase_semaphores(nc))

        def sb(name, shape, dt=F32):
            return ctx.enter_context(nc.sbuf_tensor(f"{name}_route", shape, dt))

        def sem(name):
            return take(f"{name}_route")

        bias_b = sb("bias", [P, E])
        choice = sb("choice", [P, TT, E])
        top = sb("top", [P, TT, 8])
        at = sb("top_at", [P, TT, 8], U32)
        at_f = sb("top_at_f", [P, 2, TT])
        expert_i, expert_id = sb("expert_ids_i", [P, E], I32), sb("expert_ids", [P, E])
        step_i, step_at = sb("tile_steps_i", [P, NT], I32), sb("tile_steps", [P, NT])
        hot = sb("hot", [P, 2, E, TT])
        both = sb("both", [P, E, TT])
        ones, before = sb("ones", [P, P]), sb("before", [P, P])
        ones_row = sb("ones_row", [P, E * TT])
        upto = sb("upto", [P, E, TT])
        counts = sb("counts", [P, E, TT])
        rank = sb("rank", [P, E, TT])
        count, tiles, tiles_upto, origin = sb("count", [P, E]), sb("tiles", [P, E]), sb("tiles_upto", [P, E]), sb("origin", [P, E])
        KT = sh.T // R
        full = sb("full", [P, E, KT])
        picked = sb("picked", [P, 2, E, TT])
        slot_f = sb("slot_f", [P, 2, TT])
        owner = sb("owner", [P, NT, E])
        owner_f = sb("owner_f", [P, NT])
        peak, shifted, expd = sb("peak", [P, TT]), sb("shifted", [P, TT, E]), sb("expd", [P, TT, E])
        total, inverse, score = sb("total", [P, TT]), sb("inverse", [P, TT]), sb("score", [P, TT, E])
        kept, kept_sum, kept_inv = sb("kept", [P, 2, TT]), sb("kept_sum", [P, TT]), sb("kept_inv", [P, TT])
        psB = ctx.enter_context(nc.psum_tensor("before_sum_route", [P, E * TT], F32))
        psC = ctx.enter_context(nc.psum_tensor("counts_sum_route", [P, E * TT], F32))
        bias_loaded, made, both_done, counted, exp_done = (sem("bias_loaded"), sem("made"), sem("both_done"),
                                                           sem("counted"), sem("exp_done"))
        shift_done, step_done = sem("shift_done"), sem("step_done")
        block = ctx.enter_context(nc.Block())
        lg = logits[:, :].rearrange("p (t e) -> p t e", e=E)

        @block.sync
        def _(sp):
            sp.dma_start(bias_b[:, :], bias.rearrange("(a e) -> a e", a=1).partition_broadcast(P).rearrange("p a e -> p (a e)")).then_inc(bias_loaded, 16)

        @block.gpsimd
        def _(pool):
            nc.gpsimd.iota(expert_i[:, :], [[1, E]], base=0, channel_multiplier=0).then_inc(made, 1)
            nc.gpsimd.iota(step_i[:, :], [[1, NT]], base=0, channel_multiplier=0).then_inc(made, 1)
            nc.gpsimd.memset(ones[:, :], 1.0).then_inc(made, 1)
            nc.gpsimd.memset(ones_row[:, :], 1.0).then_inc(made, 1)
            pool.wait_ge(made, 4)
            nc.gpsimd.affine_select(out=before[:, :], in_=ones[:, :], compare_op=ALU.is_gt, fill=0.0,
                                    base=0, pattern=[[1, P]], channel_multiplier=-1).then_inc(made, 1)

        @block.scalar
        def _(act):
            act.wait_ge(shift_done, 1)
            nc.scalar.activation(expd[:, :, :], shifted[:, :, :], ACT.Exp).then_inc(exp_done, 1)

        @block.tensor
        def _(pe):
            pe.wait_ge(made, 5)
            pe.wait_ge(both_done, 1)
            flat = both[:, :, :].rearrange("p e t -> p (e t)")
            nc.tensor.matmul(psB[:, :], before[:, :], flat, start=True, stop=True)
            nc.tensor.matmul(psC[:, :], ones[:, :], flat, start=True, stop=True).then_inc(counted, 1)

        @block.vector
        def _(dve):
            steps = [0]
            done = step_done

            def then(ins):
                steps[0] += 1
                ins.then_inc(done, 1)
                dve.wait_ge(done, steps[0])

            v = nc.vector
            dve.wait_ge(bias_loaded, 16)
            then(v.tensor_tensor(choice[:, :, :], lg, bias_b[:, :].unsqueeze(1).to_broadcast([P, TT, E]), ALU.add))
            for t in range(TT):
                last = v.max(top[:, t, :], choice[:, t, :])
            then(last)
            for t in range(TT):
                last = v.max_index(at[:, t, :], top[:, t, :], choice[:, t, :])
            then(last)
            then(v.tensor_copy(at_f[:, :, :], at[:, :, 0:2].rearrange("p t k -> p k t")))
            dve.wait_ge(made, 5)
            v.tensor_copy(step_at[:, :], step_i[:, :])
            then(v.tensor_copy(expert_id[:, :], expert_i[:, :]))
            for k in range(2):
                last = v.tensor_tensor(hot[:, k, :, :], expert_id[:, :].unsqueeze(2).to_broadcast([P, E, TT]),
                                       at_f[:, k, :].unsqueeze(1).to_broadcast([P, E, TT]), ALU.is_equal)
            then(last)
            v.tensor_tensor(both[:, :, :], hot[:, 0, :, :], hot[:, 1, :, :], ALU.add).then_inc(both_done, 1)

            then(v.tensor_reduce(peak[:, :], lg, AX_X, ALU.max))
            v.tensor_tensor(shifted[:, :, :], lg, peak[:, :].unsqueeze(2).to_broadcast([P, TT, E]), ALU.subtract).then_inc(shift_done, 1)
            dve.wait_ge(exp_done, 1)
            then(v.tensor_reduce(total[:, :], expd[:, :, :], AX_X, ALU.add))
            then(v.reciprocal(inverse[:, :], total[:, :]))
            then(v.tensor_tensor(score[:, :, :], expd[:, :, :], inverse[:, :].unsqueeze(2).to_broadcast([P, TT, E]), ALU.mult))
            for k in range(2):
                last = v.tensor_tensor(picked[:, k, :, :], hot[:, k, :, :], score[:, :, :].rearrange("p t e -> p e t"), ALU.mult)
            then(last)
            for k in range(2):
                last = v.tensor_reduce(kept[:, k, :], picked[:, k, :, :].rearrange("p e t -> p t e"), AX_X, ALU.add)
            then(last)
            then(v.tensor_tensor(kept_sum[:, :], kept[:, 0, :], kept[:, 1, :], ALU.add))
            then(v.reciprocal(kept_inv[:, :], kept_sum[:, :]))
            then(v.tensor_tensor(weights[:, :, :], kept[:, :, :], kept_inv[:, :].unsqueeze(1).to_broadcast([P, 2, TT]), ALU.mult))

            dve.wait_ge(counted, 1)
            then(v.tensor_copy(counts[:, :, :], psC[:, :].rearrange("p (e t) -> p e t", t=TT)))
            then(v.tensor_tensor_scan(upto[:, :, :].rearrange("p e t -> p (e t)"), ones_row[:, :],
                                      counts[:, :, :].rearrange("p e t -> p (e t)"), 0.0, ALU.mult, ALU.add))
            then(v.tensor_tensor(rank[:, :, :], upto[:, :, :], counts[:, :, :], ALU.subtract))
            then(v.tensor_tensor(count[:, :], upto[:, :, TT - 1], rank[:, :, 0], ALU.subtract))
            then(v.tensor_scalar(full[:, :, :], step_at[:, 0:KT].unsqueeze(1).to_broadcast([P, E, KT]), float(R), None, ALU.mult))
            then(v.tensor_tensor(full[:, :, :], count[:, :].unsqueeze(2).to_broadcast([P, E, KT]), full[:, :, :], ALU.is_gt))
            then(v.tensor_reduce(tiles[:, :], full[:, :, :], AX_X, ALU.add))
            then(v.tensor_tensor_scan(tiles_upto[:, :], ones_row[:, 0:E], tiles[:, :], 0.0, ALU.mult, ALU.add))
            then(v.tensor_tensor(origin[:, :], tiles_upto[:, :], tiles[:, :], ALU.subtract))
            then(v.tensor_scalar(origin[:, :], origin[:, :], float(R), None, ALU.mult))
            then(v.tensor_tensor(origin[:, :], origin[:, :], rank[:, :, 0], ALU.subtract))
            then(v.tensor_tensor(rank[:, :, :], rank[:, :, :], psB[:, :].rearrange("p (e t) -> p e t", t=TT), ALU.add))
            then(v.tensor_tensor(rank[:, :, :], rank[:, :, :], origin[:, :].unsqueeze(2).to_broadcast([P, E, TT]), ALU.add))
            for k in range(2):
                last = v.tensor_tensor(picked[:, k, :, :], hot[:, k, :, :], rank[:, :, :], ALU.mult)
            then(last)
            for k in range(2):
                last = v.tensor_reduce(slot_f[:, k, :], picked[:, k, :, :].rearrange("p e t -> p t e"), AX_X, ALU.add)
            then(last)
            then(v.tensor_copy(slots[:, :, :], slot_f[:, :, :]))
            then(v.tensor_tensor(owner[:, :, :], tiles_upto[:, :].unsqueeze(1).to_broadcast([P, NT, E]),
                                 step_at[:, :].unsqueeze(2).to_broadcast([P, NT, E]), ALU.is_le))
            then(v.tensor_reduce(owner_f[:, :], owner[:, :, :], AX_X, ALU.add))
            then(v.tensor_scalar(owner_f[:, :], owner_f[:, :], float(E - 1), None, ALU.min))
            then(v.tensor_copy(tile_expert[:, :], owner_f[0:1, :]))


def dispatch(nc, sh, x_normed, gathered, slots, filled, stores):
    NB = 4
    with ExitStack() as ctx:
        take = ctx.enter_context(phase_semaphores(nc))

        row = [ctx.enter_context(nc.sbuf_tensor(f"row{k}_dispatch", [P, sh.L], F32)) for k in range(NB)]
        loaded = [take(f"loaded{k}_dispatch") for k in range(NB)]
        sent = [take(f"sent{k}_dispatch") for k in range(NB)]
        block = ctx.enter_context(nc.Block())

        @block.sync
        def _(sp):
            for t in range(sh.TT):
                if t >= NB:
                    sp.wait_ge(sent[t % NB], 32 * (t // NB))
                sp.dma_start(row[t % NB][:, :], x_normed[t * P:(t + 1) * P, :]).then_inc(loaded[t % NB], 16)

        @block.gpsimd
        def _(pool):
            pool.wait_ge(filled, 16 * stores)
            for t in range(sh.TT):
                pool.wait_ge(loaded[t % NB], 16 * (t // NB + 1))
                for k in range(2):
                    pool.indirect_dma_start(out=gathered, out_offset=bass.IndirectOffsetOnAxis(ap=slots[:, k, t:t + 1], axis=0),
                                            in_=row[t % NB][:, :], in_offset=None).then_inc(sent[t % NB], 16)
            for k in range(NB):
                pool.wait_ge(sent[k], 32 * (sh.TT // NB))


def experts(nc, sh, gathered, results, tile_expert, wu, wg, wd, ident):
    L, LC, F, R, NT, E = sh.L, sh.LC, sh.F, sh.R, sh.NT, sh.E
    FC = F // P
    RT = R // P
    with ExitStack() as ctx:
        take = ctx.enter_context(phase_semaphores(nc))

        def pair(name, shape, dt=F32):
            return [ctx.enter_context(nc.sbuf_tensor(f"{name}{k}_expert", shape, dt)) for k in range(2)]

        def sem(name):
            return take(f"{name}_expert")

        def sem2(name):
            return [sem(f"{name}{k}") for k in range(2)]

        up_raw, dn_raw = pair("up_raw", [P, 2, LC, F]), pair("down_raw", [P, FC, L])
        up_hi, up_lo = pair("up_hi", [P, 2, LC, F], F32R), pair("up_lo", [P, 2, LC, F], F32R)
        dn_hi, dn_lo = pair("down_hi", [P, FC, L], F32R), pair("down_lo", [P, FC, L], F32R)
        rows = pair("rows", [P, RT, L])
        xhi, xlo = pair("xT_hi", [P, LC, R], F32R), pair("xT_lo", [P, LC, R], F32R)
        gate, h = pair("gated", [P, FC * R]), pair("hidden", [P, FC * R])
        hhi, hlo = pair("hidden_hi", [P, FC * R], F32R), pair("hidden_lo", [P, FC * R], F32R)
        out = pair("out_rows", [P, RT, L])
        psT = ctx.enter_context(nc.psum_tensor("turned_expert", [P, LC, R], F32))
        psU = ctx.enter_context(nc.psum_tensor("up_expert", [P, FC * R], F32))
        psG = ctx.enter_context(nc.psum_tensor("gate_expert", [P, FC * R], F32))
        psY = [ctx.enter_context(nc.psum_tensor(f"down{k}_expert", [P, RT, L], F32)) for k in range(2)]
        rows_loaded, up_loaded, dn_loaded, stored = sem2("rows_loaded"), sem2("up_loaded"), sem2("down_loaded"), sem2("stored")
        turned, x_hi, x_lo = sem("turned"), sem("x_hi"), sem("x_lo")
        up_hi_done, up_lo_done, dn_hi_done, dn_lo_done = sem("up_hi"), sem("up_lo"), sem("down_hi"), sem("down_lo")
        up_done, gate_done, silu_done, h_done, h_hi, h_lo = (sem("up_done"), sem("gate_done"), sem("silu_done"),
                                                             sem("h_done"), sem("h_hi"), sem("h_lo"))
        down_done, copied = sem("down_done"), sem("copied")
        block = ctx.enter_context(nc.Block())
        res = results.rearrange("(j r p) d -> j p r d", r=RT, p=P)
        gat = gathered.rearrange("(j r p) d -> j p r d", r=RT, p=P)
        wuv = wu.rearrange("e (p c) n -> e p (c n)", c=LC)
        wgv = wg.rearrange("e (p c) n -> e p (c n)", c=LC)
        wdv = wd.rearrange("e (p c) n -> e p (c n)", c=FC)

        def tiles(eng, first, last, body):
            with eng.Fori(0, (last - first) // 2) as i:
                for k in range(2):
                    body(i * 2 + (first + k), (first + k) % 2)

        @block.sync
        def _(sp):
            for k in range(2):
                sp.sem_inc(stored[k], 16)

            def load(j, s):
                sp.wait_ge(turned, j + 1)
                sp.dma_start(rows[s][:, :, :], gat[bass.ds(j, 1)].rearrange("j p r d -> (j p) r d")).then_inc(rows_loaded[s], 16)
                e = sp.value_load(tile_expert[0:1, bass.ds(j, 1)], min_val=0, max_val=E - 1)
                sp.wait_ge(up_lo_done, j + 1)
                for n, w in enumerate((wuv, wgv)):
                    sp.dma_start(up_raw[s][:, n, :, :].rearrange("p c n -> p (c n)"),
                                 w[bass.ds(e, 1)].rearrange("e p n -> (e p) n")).then_inc(up_loaded[s], 16)
                sp.wait_ge(dn_lo_done, j + 1)
                sp.dma_start(dn_raw[s][:, :, :].rearrange("p c n -> p (c n)"),
                             wdv[bass.ds(e, 1)].rearrange("e p n -> (e p) n")).then_inc(dn_loaded[s], 16)

            def store(j, s):
                sp.wait_ge(copied, j + 3)
                sp.dma_start(res[bass.ds(j, 1)].rearrange("j p r d -> (j p) r d"), out[s][:, :, :]).then_inc(stored[s], 16)

            load(0, 0)
            load(1, 1)
            load(2, 0)

            def body(j, s):
                load(j + 3, 1 - s)
                store(j, s)

            tiles(sp, 0, NT - 4, body)
            load(NT - 1, 1)
            for j in range(NT - 4, NT):
                store(j, j % 2)
            for k in range(2):
                sp.wait_ge(stored[k], 16 * (NT // 2 + 1))

        @block.scalar
        def _(act):
            act.sem_inc(silu_done, 1)
            act.sem_inc(copied, 2)

            def split_up(j, s):
                act.wait_ge(up_loaded[s], (j - s) * 16 + 32)
                nc.scalar.activation(up_hi[s][:, :, :, :].rearrange("p n c f -> p (n c f)"),
                                     up_raw[s][:, :, :, :].rearrange("p n c f -> p (n c f)"), ACT.Copy).then_inc(up_hi_done, 1)
                act.wait_ge(turned, j + 3)
                nc.scalar.activation(xhi[s][:, :, :], psT[:, :, :], ACT.Copy).then_inc(x_hi, 1)

            def split_down(j, s):
                act.wait_ge(dn_loaded[s], (j - s) * 8 + 16)
                act.wait_ge(down_done, j + 1)
                nc.scalar.activation(dn_hi[s][:, :, :], dn_raw[s][:, :, :], ACT.Copy).then_inc(dn_hi_done, 1)

            def hidden(j, s):
                act.wait_ge(up_done, j + 1)
                nc.scalar.activation(gate[s][:, :], psU[:, :], ACT.Silu).then_inc(silu_done, 1)
                act.wait_ge(h_done, j + 2)
                nc.scalar.activation(hhi[s][:, :], h[s][:, :], ACT.Copy).then_inc(h_hi, 1)

            def copy_out(j, s):
                act.wait_ge(down_done, j + 3)
                act.wait_ge(stored[s], (j - s) * 8 + 16)
                nc.scalar.copy(out[s][:, :, :], psY[s][:, :, :]).then_inc(copied, 1)

            split_up(0, 0)
            split_up(1, 1)
            split_down(0, 0)
            hidden(0, 0)

            def body(j, s, ahead=True):
                if ahead:
                    split_up(j + 2, s)
                split_down(j + 1, 1 - s)
                hidden(j + 1, 1 - s)
                copy_out(j, s)

            tiles(act, 0, NT - 2, body)
            body(NT - 2, 0, False)
            copy_out(NT - 1, 1)

        @block.vector
        def _(dve):
            dve.sem_inc(h_done, 1)
            dve.sem_inc(up_lo_done, 2)
            dve.sem_inc(dn_lo_done, 2)
            dve.sem_inc(x_lo, 1)

            def split_up(j, s):
                dve.wait_ge(up_hi_done, j + 1)
                nc.vector.tensor_tensor(up_lo[s][:, :, :, :].rearrange("p n c f -> p (n c f)"),
                                        up_raw[s][:, :, :, :].rearrange("p n c f -> p (n c f)"),
                                        f32(up_hi[s][:, :, :, :].rearrange("p n c f -> p (n c f)")), ALU.subtract).then_inc(up_lo_done, 1)
                dve.wait_ge(x_hi, j + 1)
                nc.vector.tensor_tensor(xlo[s][:, :, :], psT[:, :, :], f32(xhi[s][:, :, :]), ALU.subtract).then_inc(x_lo, 1)

            def split_down(j, s):
                dve.wait_ge(dn_hi_done, j + 1)
                nc.vector.tensor_tensor(dn_lo[s][:, :, :], dn_raw[s][:, :, :], f32(dn_hi[s][:, :, :]), ALU.subtract).then_inc(dn_lo_done, 1)

            def hidden(j, s):
                dve.wait_ge(silu_done, j + 2)
                dve.wait_ge(gate_done, j + 1)
                nc.vector.tensor_tensor(h[s][:, :], psG[:, :], gate[s][:, :], ALU.mult).then_inc(h_done, 1)

            split_up(0, 0)
            split_up(1, 1)
            split_down(0, 0)
            hidden(0, 0)

            def body(j, s, ahead=True):
                if ahead:
                    split_up(j + 2, s)
                split_down(j + 1, 1 - s)
                hidden(j + 1, 1 - s)

            tiles(dve, 0, NT - 2, body)
            body(NT - 2, 0, False)

        @block.gpsimd
        def _(pool):
            def body(j, s):
                pool.wait_ge(h_hi, j + 1)
                nc.gpsimd.tensor_tensor(hlo[s][:, :], h[s][:, :], f32(hhi[s][:, :]), ALU.subtract).then_inc(h_lo, 1)

            tiles(pool, 0, NT, body)

        @block.tensor
        def _(pe):
            pe.sem_inc(turned, 2)
            pe.sem_inc(down_done, 2)

            def turn(j, s):
                pe.wait_ge(rows_loaded[s], (j - s) * 8 + 16)
                pe.wait_ge(x_lo, j + 1)
                for r in range(RT):
                    for c in range(LC):
                        last = nc.tensor.transpose(psT[:, c, r * P:(r + 1) * P], rows[s][:, r, c::LC], ident[:, :])
                last.then_inc(turned, 1)

            def up(j, s):
                pe.wait_ge(up_lo_done, j + 3)
                pe.wait_ge(x_lo, j + 2)
                for n, (bank, done) in enumerate(((psU, up_done), (psG, gate_done))):
                    pe.wait_ge((silu_done, h_done)[n], j + 1)
                    for fc in range(FC):
                        for c in range(LC):
                            last = three_passes(nc, bank[:, fc * R:(fc + 1) * R], up_hi[s][:, n, c, fc::FC],
                                                up_lo[s][:, n, c, fc::FC], xhi[s][:, c, :], xlo[s][:, c, :], c == 0, c == LC - 1)
                    last.then_inc(done, 1)

            def down(j, s):
                pe.wait_ge(dn_lo_done, j + 3)
                pe.wait_ge(h_lo, j + 1)
                pe.wait_ge(copied, j + 1)
                for r in range(RT):
                    for fc in range(FC):
                        col = slice(fc * R + r * P, fc * R + (r + 1) * P)
                        last = three_passes(nc, psY[s][:, r, :], hhi[s][:, col], hlo[s][:, col],
                                            dn_hi[s][:, fc, :], dn_lo[s][:, fc, :], fc == 0, fc == FC - 1)
                last.then_inc(down_done, 1)

            turn(0, 0)
            turn(1, 1)
            up(0, 0)

            def body(j, s, ahead=True):
                if ahead:
                    turn(j + 2, s)
                up(j + 1, 1 - s)
                down(j, s)

            tiles(pe, 0, NT - 2, body)
            body(NT - 2, 0, False)
            down(NT - 1, 1)


def combine(nc, sh, base, results, slots, weights, out):
    NB = 4
    with ExitStack() as ctx:
        take = ctx.enter_context(phase_semaphores(nc))

        def tiles(name):
            return [ctx.enter_context(nc.sbuf_tensor(f"{name}{k}_combine", [P, sh.L], F32)) for k in range(NB)]

        def sems(name, n=NB):
            return [take(f"{name}{k}_combine") for k in range(n)]

        b, y0, y1, part, o = tiles("base"), tiles("first"), tiles("second"), tiles("partial"), tiles("sum")
        b_loaded, y_loaded, stored = sems("b_loaded"), sems("y_loaded"), sems("stored")
        first_added, added = sems("added", 2)
        block = ctx.enter_context(nc.Block())

        @block.sync
        def _(sp):
            for t in range(sh.TT):
                s = t % NB
                if t >= NB:
                    sp.wait_ge(added, t - NB + 1)
                sp.dma_start(b[s][:, :], base[t * P:(t + 1) * P, :]).then_inc(b_loaded[s], 16)

        @block.gpsimd
        def _(pool):
            for t in range(sh.TT):
                s = t % NB
                if t >= NB:
                    pool.wait_ge(added, t - NB + 1)
                for k, y in enumerate((y0, y1)):
                    pool.indirect_dma_start(out=y[s][:, :], out_offset=None, in_=results,
                                            in_offset=bass.IndirectOffsetOnAxis(ap=slots[:, k, t:t + 1], axis=0)).then_inc(y_loaded[s], 16)

        @block.vector
        def _(dve):
            for t in range(sh.TT):
                s = t % NB
                dve.wait_ge(b_loaded[s], 16 * (t // NB + 1))
                dve.wait_ge(y_loaded[s], 32 * (t // NB + 1))
                nc.vector.scalar_tensor_tensor(out=part[s][:, :], in0=y0[s][:, :], scalar=weights[:, 0, t:t + 1], in1=b[s][:, :],
                                               op0=ALU.mult, op1=ALU.add).then_inc(first_added, 1)
                dve.wait_ge(first_added, t + 1)
                if t >= NB:
                    dve.wait_ge(stored[s], 16 * (t // NB))
                nc.vector.scalar_tensor_tensor(out=o[s][:, :], in0=y1[s][:, :], scalar=weights[:, 1, t:t + 1], in1=part[s][:, :],
                                               op0=ALU.mult, op1=ALU.add).then_inc(added, 1)

        @block.scalar
        def _(act):
            for t in range(sh.TT):
                act.wait_ge(added, t + 1)
                act.dma_start(out[t * P:(t + 1) * P, :], o[t % NB][:, :]).then_inc(stored[t % NB], 16)
            for s in range(NB):
                act.wait_ge(stored[s], 16 * (sh.TT // NB))


def program(nc, x, context, taps, skip, router, bias, wu, wg, wd, su, sg, sd, out):
    sh = Shapes(x, taps, router, wu)
    rows, context_rows = x.rearrange("b s l -> (b s) l"), context.rearrange("b s l -> (b s) l")

    def dram(name, shape):
        return nc.dram_tensor(name, shape, F32).ap()

    taps_rev = dram("taps_rev", (sh.H, sh.RB))
    x_mid, x_normed, base = dram("x_mid", (sh.T, sh.L)), dram("x_mid_normed", (sh.T, sh.L)), dram("base", (sh.T, sh.L))
    gathered, results = dram("gathered", (sh.NT * sh.R, sh.L)), dram("results", (sh.NT * sh.R, sh.L))
    ZR = 4
    slot_rows = gathered.rearrange("(c p r) d -> c p (r d)", p=P, r=ZR)
    with ExitStack() as ctx:
        def sb(name, shape, dt=F32):
            return ctx.enter_context(nc.sbuf_tensor(name, shape, dt))

        ident, eps = sb("identity", [P, P]), sb("eps", [P, 1])
        filled = ctx.enter_context(nc.semaphore("slots_zeroed"))
        with ExitStack() as attention:
            zero = attention.enter_context(nc.sbuf_tensor("zero_rows", [P, ZR * sh.L], F32))
            prepare(nc, sh, taps, skip, taps_rev, ident, eps, zero)
            for half in range(HALVES):
                with ExitStack() as turned:
                    cT, qT = (turned.enter_context(nc.sbuf_tensor(f"{n}T{half}", [P, sh.LC * sh.HB * sh.H * sh.CE], F32)) for n in "cq")
                    bring_in(nc, sh, half, rows, context_rows, cT, qT, ident, eps)
                    long_convolution(nc, sh, half, taps_rev, cT, qT, zero, slot_rows, filled)
                    close_attention(nc, sh, half, rows, qT, x_mid, x_normed, ident, eps)
        logits = sb("logits", [P, sh.TT * sh.E])
        slots, weights, tile_expert = sb("slots", [P, 2, sh.TT], U32), sb("weights", [P, 2, sh.TT]), sb("tile_expert", [1, sh.NT], I32)
        shared_expert(nc, sh, x_mid, x_normed, router, su[0], sg[0], sd[0], base, logits, ident, filled, slot_rows.shape[0])
        routing(nc, sh, logits, bias, slots, weights, tile_expert)
        dispatch(nc, sh, x_normed, gathered, slots, filled, slot_rows.shape[0])
        experts(nc, sh, gathered, results, tile_expert, wu, wg, wd, ident)
        combine(nc, sh, base, results, slots, weights, out.rearrange("b s l -> (b s) l"))


_INS = ['x', 'ctx_2048', 'L0_xattn_ssm_kernel', 'L0_xattn_D', 'L0_ffn_router_w', 'L0_ffn_router_bias',
        'L0_ffn_Wu', 'L0_ffn_Wg', 'L0_ffn_Wd', 'L0_ffn_Su', 'L0_ffn_Sg', 'L0_ffn_Sd']


def kernel(**inputs):
    import numpy as _np
    import concourse.bacc as _bacc
    from concourse import mybir as _mybir
    from concourse.bass_utils import run_bass_kernel_spmd as _run

    nc = _bacc.Bacc("TRN2", target_bir_lowering=False, num_devices=1)
    arrays, args = {}, []
    for name in _INS:
        a = _np.ascontiguousarray(inputs[name])
        arrays[f"in_{name}"] = a
        args.append(nc.dram_tensor(f"in_{name}", a.shape, _mybir.dt.from_np(a.dtype), kind="ExternalInput").ap())
    out = nc.dram_tensor("out", inputs["x"].shape, _mybir.dt.from_np(_np.dtype("float32")), kind="ExternalOutput").ap()
    program(nc, *args, out)
    r = _run(nc, [arrays], core_ids=[0])
    return r.results[0]["out"]
```

```python
from contextlib import ExitStack, contextmanager

import concourse.bass as bass
from concourse import mybir

ALU = mybir.AluOpType
ACT = mybir.ActivationFunctionType
F32 = mybir.dt.float32
F32R = mybir.dt.float32r
U32 = mybir.dt.uint32
I32 = mybir.dt.int32
AX_X = mybir.AxisListType.X

P = 128
EPS = 1e-5
HALVES = 2



def three_passes(nc, out, w_hi, w_lo, x_hi, x_lo, first, last):
    nc.tensor.matmul(out, w_hi, x_hi, start=first, stop=False)
    nc.tensor.matmul(out, w_lo, x_hi, start=False, stop=False)
    return nc.tensor.matmul(out, w_hi, x_lo, start=False, stop=last)


def f32(ap):
    return ap.bitcast(F32)


@contextmanager
def phase_semaphores(nc):
    taken = []

    def take(name):
        taken.append(nc.alloc_semaphore(name=name))
        return taken[-1]

    yield take
    nc.clear_and_free_semaphores(taken)
    nc.all_engine_barrier()


class Shapes:

    def __init__(self, x, taps, router, wu):
        self.B, self.S, self.L = x.shape
        self.H = taps.shape[0]
        self.C = self.S // self.H
        self.T = self.B * self.S
        self.LC = self.L // P
        self.TT = self.T // P
        self.E = router.shape[0]
        self.F = wu.shape[2]
        self.HB = self.B // HALVES
        self.HT = self.HB * self.S // P
        self.CE = self.C + self.C // 2
        self.ND = self.C // 2 + 1
        self.NP = self.C * (self.C + 1) // 2
        self.R = 2 * P
        most = 2 * self.T // self.R + self.E - 1
        self.NT = most + most % 2
        self.RB = self.L + P


def prepare(nc, sh, taps, skip, router, taps_rev, router_T, ident, eps):
    H, L, LC, RB, E = sh.H, sh.L, sh.LC, sh.RB, sh.E
    with ExitStack() as ctx:
        take = ctx.enter_context(phase_semaphores(nc))

        raw = ctx.enter_context(nc.sbuf_tensor("taps_raw", [H, L], F32))
        rev = ctx.enter_context(nc.sbuf_tensor("taps_reversed", [H, RB], F32))
        d = ctx.enter_context(nc.sbuf_tensor("skip_weight", [H, 1], F32))
        loaded = take("taps_loaded")
        d_loaded = take("skip_loaded")
        cleared = take("reversed_cleared")
        turned = take("taps_turned")
        added = take("skip_added")
        stored = take("taps_stored")
        blank = take("identity_blank")
        ident_made, router_loaded, router_turned = take("identity_made"), take("router_loaded"), take("router_turned")
        router_rows = ctx.enter_context(nc.sbuf_tensor("router_rows", [E, L], F32))
        ps = ctx.enter_context(nc.psum_tensor("router_turned", [P, LC, E], F32))
        block = ctx.enter_context(nc.Block())

        @block.sync
        def _(sp):
            sp.dma_start(raw[:, :], taps).then_inc(loaded, 16)
            sp.dma_start(d[:, :], skip.rearrange("(h a) -> h a", a=1)).then_inc(d_loaded, 16)
            sp.dma_start(router_rows[:, :], router).then_inc(router_loaded, 16)
            sp.wait_ge(added, 1)
            sp.dma_start(taps_rev, rev[:, :]).then_inc(stored, 16)
            sp.wait_ge(stored, 16)

        @block.gpsimd
        def _(pool):
            nc.gpsimd.memset(ident[:, :], 0.0).then_inc(blank, 1)
            pool.wait_ge(blank, 1)
            nc.gpsimd.affine_select(out=ident[:, :], in_=ident[:, :], compare_op=ALU.not_equal, fill=1.0,
                                    base=0, pattern=[[-1, P]], channel_multiplier=1).then_inc(ident_made, 1)

        @block.tensor
        def _(pe):
            pe.wait_ge(ident_made, 1)
            pe.wait_ge(router_loaded, 16)
            for c in range(LC):
                last = nc.tensor.transpose(ps[:, c, :], router_rows[:, c::LC], ident[0:E, 0:E])
            last.then_inc(router_turned, 1)

        @block.vector
        def _(dve):
            nc.vector.memset(eps[:, :], EPS)
            nc.vector.memset(rev[:, L:RB], 0.0).then_inc(cleared, 1)
            dve.wait_ge(loaded, 16)
            nc.vector.tensor_copy(rev[:, 0:L], raw[:, ::-1]).then_inc(turned, 1)
            dve.wait_ge(turned, 1)
            dve.wait_ge(cleared, 1)
            dve.wait_ge(d_loaded, 16)
            nc.vector.tensor_tensor(rev[:, L - 1:L], rev[:, L - 1:L], d[:, :], ALU.add).then_inc(added, 1)
            dve.wait_ge(router_turned, 1)
            nc.vector.tensor_copy(router_T[:, :, :], ps[:, :, :])


def change_rows(nc, sh, leaving, entering, x, ctx_rows, cT, qT, oT, x_mid, x_mid_normed, router_T, logits, ident, eps):
    L, LC, HB, H, C, CE, E = sh.L, sh.LC, sh.HB, sh.H, sh.C, sh.CE, sh.E
    U = 4
    NK = sh.S // P
    heads = P // C
    STEPS = sh.HT // U
    here = f"rows{leaving}{entering}"
    with ExitStack() as ctx:
        take = ctx.enter_context(phase_semaphores(nc))

        def sb(name, shape):
            return ctx.enter_context(nc.sbuf_tensor(f"{name}_{here}", shape, F32))

        def ps(name, shape=(P, L)):
            return ctx.enter_context(nc.psum_tensor(f"{name}_{here}", list(shape), F32))

        def sem(name):
            return take(f"{name}_{here}")

        def sems(name):
            return [sem(f"{name}{u}") for u in range(U)]

        if entering is not None:
            xin, cin, xn = sb("x_in", [P, U, L]), sb("c_in", [P, U, L]), sb("x_in_normed", [P, U, L])
            stats, mv, std, rstd = (sb("in_stats", [P, U, 6]), sb("in_mean_var", [P, U, 2]),
                                    sb("in_std", [P, U, 1]), sb("in_rstd", [P, U, 1]))
            psC, psX = [ps(f"turned_c{k}") for k in range(2)], [ps(f"turned_x{k}") for k in range(2)]
            x_loaded, c_loaded = sems("x_loaded"), sems("c_loaded")
            stats_done, mean_done, std_done, rstd_done = sem("stats"), sem("mean"), sem("std"), sem("rstd")
            x_normed, c_turned, x_turned = sem("x_normed"), sem("c_turned"), sem("x_turned")
            c_kept, x_kept = sem("c_kept"), sem("x_kept")
        if leaving is not None:
            l_x, l_mid, l_xn, packed = sb("x_out", [P, U, L]), sb("x_mid", [P, U, L]), sb("mid_normed", [P, U, L]), sb("packed", [P, 2, L])
            l_stats, l_mv, l_std, l_rstd = (sb("out_stats", [P, U, 6]), sb("out_mean_var", [P, U, 2]),
                                            sb("out_std", [P, U, 1]), sb("out_rstd", [P, U, 1]))
            xT = sb("mid_T", [P, 2, LC * P])
            psO = [ps(f"rows{k}") for k in range(2)]
            psT, psL = ps("mid_turned"), ps("logits", (P, U * E))
            l_loaded, mid_stored, normed_stored = sems("l_loaded"), sems("mid_stored"), sems("normed_stored")
            pack_done, o_turned, added = sem("pack"), sem("o_turned"), sem("added")
            l_stats_done, l_mean_done, l_std_done, l_rstd_done = sem("l_stats"), sem("l_mean"), sem("l_std"), sem("l_rstd")
            normed, l_turned = sem("normed"), sem("l_turned")
            xT_kept, logits_done, logits_kept = sem("xT_kept"), sem("logits"), sem("logits_kept")
        holds = sem("holds")
        block = ctx.enter_context(nc.Block())

        def rows(half, i, u):
            return bass.ds(i * (U * P) + (half * sh.HT + u) * P, P)

        def place(t, i, u):
            v = t[:, :].rearrange("p (c n) -> p c n", c=LC)
            v = v[:, :, bass.ds(i * (U // NK * H * CE) + (u // NK * H + u % NK * heads) * CE, heads * CE)]
            return v.rearrange("p c (h r) -> p c h r", r=CE)

        def keep(copy, t, src, i, u, done):
            d, s = place(t, i, u), src[:, :].rearrange("p (c h r) -> p c h r", c=LC, r=C)
            copy(d[:, :, :, 0:C], s)
            copy(d[:, :, :, C:CE], s[:, :, :, 0:CE - C]).then_inc(done, 1)

        @block.sync
        def _(sp):
            def load(i):
                for u in range(U):
                    n = i * U + u
                    if leaving is not None:
                        sp.wait_ge(added, n + 1)
                        sp.dma_start(l_x[:, u, :], x[rows(leaving, i, u), :]).then_inc(l_loaded[u], 16)
                    if entering is not None:
                        sp.wait_ge(x_normed, n + 1)
                        sp.dma_start(xin[:, u, :], x[rows(entering, i, u), :]).then_inc(x_loaded[u], 16)
                        sp.wait_ge(c_turned, n + 1)
                        sp.dma_start(cin[:, u, :], ctx_rows[rows(entering, i, u), :]).then_inc(c_loaded[u], 16)

            def store(i):
                for u in range(U):
                    sp.wait_ge(added, i * U + u + 1 + U)
                    sp.dma_start(x_mid[rows(leaving, i, u), :], l_mid[:, u, :]).then_inc(mid_stored[u], 16)
                for u in range(U):
                    sp.wait_ge(normed, i * U + u + 1)
                    sp.dma_start(x_mid_normed[rows(leaving, i, u), :], l_xn[:, u, :]).then_inc(normed_stored[u], 16)

            if leaving is None:
                with sp.Fori(0, STEPS) as i:
                    load(i)
            else:
                for u in range(U):
                    sp.sem_inc(mid_stored[u], 16)
                    sp.sem_inc(normed_stored[u], 16)
                load(0)
                with sp.Fori(0, STEPS - 1) as i:
                    load(i + 1)
                    store(i)
                store(STEPS - 1)
                for u in range(U):
                    sp.wait_ge(mid_stored[u], 16 * (STEPS + 1))
                    sp.wait_ge(normed_stored[u], 16 * (STEPS + 1))

        @block.scalar
        def _(act):
            if entering is not None:
                act.sem_inc(c_kept, 2)
            if leaving is not None:
                act.sem_inc(xT_kept, 1)
                act.sem_inc(logits_kept, 1)
            with act.Fori(0, STEPS) as i:
                for u in range(U):
                    n = i * U + u
                    if leaving is not None:
                        act.wait_ge(o_turned, n - 1 + U)
                        nc.scalar.copy(packed[:, u % 2, :].rearrange("p (c h r) -> p c h r", c=LC, r=C),
                                       place(oT, i, u)[:, :, :, 0:C]).then_inc(pack_done, 1)
                    if entering is not None:
                        act.wait_ge(c_turned, n + 1 + U)
                        keep(nc.scalar.copy, cT, psC[u % 2], i, u, c_kept)
                if entering is not None:
                    act.wait_ge(mean_done, i + 1)
                    nc.scalar.activation(std[:, :, :], mv[:, :, 1:2], ACT.Sqrt, bias=eps[:, :]).then_inc(std_done, 1)
                if leaving is not None:
                    act.wait_ge(l_mean_done, i + 1)
                    nc.scalar.activation(l_std[:, :, :], l_mv[:, :, 1:2], ACT.Sqrt, bias=eps[:, :]).then_inc(l_std_done, 1)
                if leaving is not None:
                    for u in range(U):
                        act.wait_ge(l_turned, i * U + u + 1 + U)
                        nc.scalar.copy(xT[:, u % 2, :], psT[:, :]).then_inc(xT_kept, 1)
                    act.wait_ge(logits_done, i + 1)
                    nc.scalar.copy(logits[:, bass.ds(i * (U * E) + leaving * sh.HT * E, U * E)], psL[:, :]).then_inc(logits_kept, 1)

        @block.vector
        def _(dve):
            if entering is not None:
                dve.sem_inc(x_normed, U)
                dve.sem_inc(x_kept, 2)
            if leaving is not None:
                dve.sem_inc(added, U)
            def statistics(src, st, m, seen, out, i):
                for u in range(U):
                    last = nc.vector.bn_stats(st[:, u, :], src(u))
                last.then_inc(seen, 1)
                dve.wait_ge(seen, i + 1)
                dve.sem_inc(holds, 1)
                for u in range(U):
                    last = nc.vector.bn_aggr(m[:, u, :], st[:, u, :])
                last.then_inc(out, 1)

            with dve.Fori(0, STEPS) as i:
                if entering is not None:
                    for u in range(U):
                        dve.wait_ge(x_loaded[u], i * 16 + 16)
                    statistics(lambda u: xin[:, u, :], stats, mv, stats_done, mean_done, i)
                if leaving is not None:
                    for u in range(U):
                        n = i * U + u
                        dve.wait_ge(o_turned, n + 1 + U)
                        dve.wait_ge(l_loaded[u], i * 16 + 16)
                        dve.wait_ge(mid_stored[u], i * 16 + 16)
                        nc.vector.tensor_tensor(l_mid[:, u, :], psO[u % 2][:, :], l_x[:, u, :], ALU.add).then_inc(added, 1)
                    dve.wait_ge(added, i * U + 2 * U)
                    statistics(lambda u: l_mid[:, u, :], l_stats, l_mv, l_stats_done, l_mean_done, i)
                if entering is not None:
                    dve.wait_ge(std_done, i + 1)
                    nc.vector.reciprocal(rstd[:, :, :], std[:, :, :]).then_inc(rstd_done, 1)
                if leaving is not None:
                    dve.wait_ge(l_std_done, i + 1)
                    nc.vector.reciprocal(l_rstd[:, :, :], l_std[:, :, :]).then_inc(l_rstd_done, 1)
                for u in range(U):
                    n = i * U + u
                    if entering is not None:
                        dve.wait_ge(rstd_done, i + 1)
                        dve.wait_ge(x_turned, n + 1)
                        nc.vector.tensor_scalar(xn[:, u, :], xin[:, u, :], mv[:, u, 0:1], rstd[:, u, :],
                                                ALU.subtract, ALU.mult).then_inc(x_normed, 1)
                    if leaving is not None:
                        dve.wait_ge(l_rstd_done, i + 1)
                        dve.wait_ge(l_turned, n + 1)
                        dve.wait_ge(normed_stored[u], i * 16 + 16)
                        nc.vector.tensor_scalar(l_xn[:, u, :], l_mid[:, u, :], l_mv[:, u, 0:1], l_rstd[:, u, :],
                                                ALU.subtract, ALU.mult).then_inc(normed, 1)
                if entering is not None:
                    for u in range(U):
                        dve.wait_ge(x_turned, i * U + u + 1 + U)
                        keep(nc.vector.tensor_copy, qT, psX[u % 2], i, u, x_kept)

        @block.tensor
        def _(pe):
            def turn(out, src, done):
                for c in range(LC):
                    last = nc.tensor.transpose(out[:, c * P:(c + 1) * P], src(c), ident[:, :])
                last.then_inc(done, 1)

            if entering is not None:
                pe.sem_inc(c_turned, U)
                pe.sem_inc(x_turned, U)
            if leaving is not None:
                pe.sem_inc(o_turned, U)
                pe.sem_inc(l_turned, U)
            with pe.Fori(0, STEPS) as i:
                for u in range(U):
                    n = i * U + u
                    if leaving is not None:
                        pe.wait_ge(pack_done, n + 1)
                        pe.wait_ge(added, n - 1 + U)
                        turn(psO[u % 2], lambda c: packed[:, u % 2, c * P:(c + 1) * P], o_turned)
                    if entering is not None:
                        pe.wait_ge(c_loaded[u], i * 16 + 16)
                        pe.wait_ge(c_kept, n + 1)
                        turn(psC[u % 2], lambda c: cin[:, u, c * P:(c + 1) * P], c_turned)
                if entering is not None:
                    for u in range(U):
                        n = i * U + u
                        pe.wait_ge(x_normed, n + 1 + U)
                        pe.wait_ge(x_kept, n + 1)
                        turn(psX[u % 2], lambda c: xn[:, u, c * P:(c + 1) * P], x_turned)
                if leaving is not None:
                    def route(u):
                        pe.wait_ge(xT_kept, i * U + u + 2)
                        for c in range(LC):
                            last = nc.tensor.matmul(psL[:, u * E:(u + 1) * E], xT[:, u % 2, c * P:(c + 1) * P],
                                                    router_T[:, c, :], start=c == 0, stop=c == LC - 1)
                        return last

                    pe.wait_ge(logits_kept, i + 1)
                    for u in range(U):
                        pe.wait_ge(normed, i * U + u + 1)
                        pe.wait_ge(xT_kept, i * U + u + 1)
                        turn(psT, lambda c: l_xn[:, u, c::LC], l_turned)
                        if u:
                            route(u - 1)
                    route(U - 1).then_inc(logits_done, 1)


def long_convolution(nc, sh, half, taps_rev, cT, qT, gathered):
    L, LC, HB, H, C, CE, ND, NP = sh.L, sh.LC, sh.HB, sh.H, sh.C, sh.CE, sh.ND, sh.NP
    G = LC * HB
    GS = H * CE
    N = HB * NP
    ZR = gathered.shape[0] // (HALVES * (H // 2) * P)
    with ExitStack() as ctx:
        take = ctx.enter_context(phase_semaphores(nc))

        def sb(name, shape):
            return [ctx.enter_context(nc.sbuf_tensor(f"{name}{k}_conv{half}", shape, F32)) for k in range(2)]

        def sem(name):
            return take(f"{name}_conv{half}")

        traw, toep = sb("taps_rows", [P, L]), sb("toeplitz", [P, L])
        kv = sb("row_products", [P, G * NP])
        z = sb("terms", [P, G * C * C])
        y = [ctx.enter_context(nc.psum_tensor(f"conv_out{k}_{half}", [P, LC, 512], F32)) for k in range(2)]
        t_loaded = [sem(f"t_loaded{k}") for k in range(2)]
        prod_done = sem("prod_done")
        t_ready, conv_done, terms_done = sem("t_ready"), sem("conv_done"), sem("terms_done")
        folded, summed, holds = sem("folded"), sem("summed"), sem("holds")
        cleared, filled = sem("cleared"), sem("filled")
        ZERO_ROWS = gathered.shape[0] // (HALVES * (H // 2) * ZR)
        slots = gathered.rearrange("(n z) d -> n (z d)", z=ZR)
        zero = ctx.enter_context(nc.sbuf_tensor(f"zeros_conv{half}", [ZERO_ROWS, ZR * L], F32))
        block = ctx.enter_context(nc.Block())

        FULL = (ND - 1) * C

        def head(t, h, pattern, row=0, chunk=0):
            v = t[:, bass.ds(h * CE + (row + chunk * HB * GS), CE - row)]
            return bass.AP(tensor=v.tensor, offset=v.offset, ap=[list(v.ap[0])] + pattern)

        def terms(k):
            return z[k][:, :].rearrange("p (g t j) -> p g t j", t=C, j=C)

        @block.sync
        def _(sp):
            with sp.Fori(0, H // 2) as i:
                for k in range(2):
                    sp.wait_ge(t_ready, i * 2 + k + 1)
                    src = bass.AP(tensor=taps_rev.tensor, offset=taps_rev[bass.ds(i * 2 + k, 1), :].offset, ap=[[1, P], [1, L]])
                    sp.dma_start(traw[k][:, :], src).then_inc(t_loaded[k], 16)

        @block.gpsimd
        def _(pool):
            pool.sem_inc(folded, 2)

            def products(h, k):
                pool.wait_ge(conv_done, h + 1)
                each = kv[k][:, :].rearrange("p (g r) -> p g r", r=NP)
                nc.gpsimd.tensor_tensor(
                    each[:, :, 0:FULL].rearrange("p g (d j) -> p g d j", j=C),
                    head(cT, h, [[GS, G], [0, ND - 1], [1, C]]), head(cT, h, [[GS, G], [1, ND - 1], [1, C]]), ALU.mult)
                nc.gpsimd.tensor_tensor(each[:, :, FULL:NP], head(cT, h, [[GS, G], [1, C // 2]]),
                                        head(cT, h, [[GS, G], [1, C // 2]], C // 2), ALU.mult).then_inc(prod_done, 1)

            def fold(h, k):
                pool.wait_ge(terms_done, h + 3)
                nc.gpsimd.tensor_tensor(terms(k)[:, :, 0:C - ND, :], terms(k)[:, :, 0:C - ND, :],
                                        terms(k)[:, :, ND:C, :], ALU.add).then_inc(folded, 1)

            products(0, 0)
            products(1, 1)
            with pool.Fori(0, H // 2 - 1) as i:
                for k in range(2):
                    products(i * 2 + 2 + k, k)
                    fold(i * 2 + k, k)
            fold(H - 2, 0)
            fold(H - 1, 1)

        @block.scalar
        def _(act):
            act.sem_inc(t_ready, 2)
            act.wait_ge(cleared, 1)
            with act.Fori(0, H // 2) as i:
                for k in range(2):
                    act.wait_ge(t_loaded[k], i * 16 + 16)
                    act.wait_ge(conv_done, i * 2 + k + 1)
                    nc.scalar.activation(toep[k][:, :], traw[k][:, ::-1], ACT.Copy).then_inc(t_ready, 1)
                act.dma_start(slots[bass.ds(i * ZERO_ROWS + half * (H // 2) * ZERO_ROWS, ZERO_ROWS), :],
                              zero[:, :]).then_inc(filled, 16)
            act.wait_ge(filled, 16 * (H // 2))

        @block.tensor
        def _(pe):
            pe.sem_inc(conv_done, 2)
            with pe.Fori(0, H // 2) as i:
                for k in range(2):
                    n = i * 2 + k + 1
                    pe.wait_ge(t_ready, n + 2)
                    pe.wait_ge(prod_done, n)
                    pe.wait_ge(terms_done, n)
                    for lc in range(LC):
                        for mc in range(lc + 1):
                            last = nc.tensor.matmul(y[k][:, lc, 0:N], toep[k][:, (lc - mc) * P:(lc - mc + 1) * P],
                                                    kv[k][:, mc * N:(mc + 1) * N], start=mc == 0, stop=mc == lc)
                    last.then_inc(conv_done, 1)

        @block.vector
        def _(dve):
            dve.sem_inc(terms_done, 2)
            nc.vector.memset(zero[:, :], 0.0).then_inc(cleared, 1)
            dve.sem_inc(summed, 2)

            def multiply(h, k):
                dve.wait_ge(conv_done, h + 3)
                dve.wait_ge(summed, h + 1)
                zt = z[k][:, :].rearrange("p (c b t j) -> p c b t j", c=LC, b=HB, j=C)
                each = y[k][:, :, 0:N].rearrange("p c (b r) -> p c b r", r=NP)
                for c in range(LC):
                    q = head(qT, h, [[GS, HB], [1, ND - 1], [1, C]], 0, c)
                    nc.vector.tensor_tensor(zt[:, c, :, 0:ND - 1, :], each[:, c, :, 0:FULL].rearrange("p b (d j) -> p b d j", j=C), q, ALU.mult)
                for row, other in ((0, C // 2), (C // 2, 0)):
                    q = head(qT, h, [[HB * GS, LC], [GS, HB], [1, C // 2]], other)
                    nc.vector.tensor_tensor(zt[:, :, :, ND - 1, row:row + C // 2], each[:, :, :, FULL:NP], q, ALU.mult)
                for d in range(1, ND - 1):
                    for lo, hi, off in ((0, C - d, d), (C - d, C, d - C)):
                        q = head(qT, h, [[HB * GS, LC], [GS, HB], [1, hi - lo]], lo)
                        last = nc.vector.tensor_tensor(zt[:, :, :, ND - 1 + d, lo + off:hi + off], each[:, :, :, d * C + lo:d * C + hi], q, ALU.mult)
                last.then_inc(terms_done, 1)

            def add_up(h, k):
                dve.wait_ge(folded, h + 3)
                dve.sem_inc(holds, 1)
                nc.vector.tensor_reduce(head(qT, h, [[GS, G], [1, C]]),
                                        terms(k)[:, :, 0:ND, :].rearrange("p g t j -> p g j t"), AX_X, ALU.add).then_inc(summed, 1)

            multiply(0, 0)
            with dve.Fori(0, H // 2 - 1) as i:
                multiply(i * 2 + 1, 1)
                add_up(i * 2, 0)
                multiply(i * 2 + 2, 0)
                add_up(i * 2 + 1, 1)
            multiply(H - 1, 1)
            add_up(H - 2, 0)
            add_up(H - 1, 1)


def routing(nc, sh, logits, bias, slots, weights, tile_expert, shared, s_hi, s_lo):
    E, TT, NT, R = sh.E, sh.TT, sh.NT, sh.R
    with ExitStack() as ctx:
        take = ctx.enter_context(phase_semaphores(nc))

        def sb(name, shape, dt=F32):
            return ctx.enter_context(nc.sbuf_tensor(f"{name}_route", shape, dt))

        def sem(name):
            return take(f"{name}_route")

        bias_b = sb("bias", [P, E])
        choice = sb("choice", [P, TT, E])
        top = sb("top", [P, TT, 8])
        at = sb("top_at", [P, TT, 8], U32)
        at_f = sb("top_at_f", [P, 2, TT])
        expert_i, expert_id = sb("expert_ids_i", [P, E], I32), sb("expert_ids", [P, E])
        step_i, step_at = sb("tile_steps_i", [P, NT], I32), sb("tile_steps", [P, NT])
        hot = sb("hot", [P, 2, E, TT])
        both = sb("both", [P, E, TT])
        ones, before = sb("ones", [P, P]), sb("before", [P, P])
        ones_row = sb("ones_row", [P, E * TT])
        upto = sb("upto", [P, E, TT])
        counts = sb("counts", [P, E, TT])
        rank = sb("rank", [P, E, TT])
        count, tiles, tiles_upto, origin = sb("count", [P, E]), sb("tiles", [P, E]), sb("tiles_upto", [P, E]), sb("origin", [P, E])
        KT = sh.T // R
        full = sb("full", [P, E, KT])
        picked = sb("picked", [P, 2, E, TT])
        slot_f = sb("slot_f", [P, 2, TT])
        owner = sb("owner", [P, NT, E])
        owner_f = sb("owner_f", [P, NT])
        peak, shifted, expd = sb("peak", [P, TT]), sb("shifted", [P, TT, E]), sb("expd", [P, TT, E])
        total, inverse, score = sb("total", [P, TT]), sb("inverse", [P, TT]), sb("score", [P, TT, E])
        kept, kept_sum, kept_inv = sb("kept", [P, 2, TT]), sb("kept_sum", [P, TT]), sb("kept_inv", [P, TT])
        psB = ctx.enter_context(nc.psum_tensor("before_sum_route", [P, E * TT], F32))
        psC = ctx.enter_context(nc.psum_tensor("counts_sum_route", [P, E * TT], F32))
        bias_loaded, made, both_done, counted, exp_done = (sem("bias_loaded"), sem("made"), sem("both_done"),
                                                           sem("counted"), sem("exp_done"))
        shift_done, step_done = sem("shift_done"), sem("step_done")
        stage = [sb(f"shared_weights{n}", list(w.shape)) for n, w in enumerate(s_hi)]
        w_loaded, w_hi_done = [sem(f"w_loaded{n}") for n in range(len(shared))], sem("w_hi_done")
        block = ctx.enter_context(nc.Block())
        lg = logits[:, :].rearrange("p (t e) -> p t e", e=E)

        @block.sync
        def _(sp):
            sp.dma_start(bias_b[:, :], bias.rearrange("(a e) -> a e", a=1).partition_broadcast(P).rearrange("p a e -> p (a e)")).then_inc(bias_loaded, 16)
            for n, w in enumerate(shared):
                sp.dma_start(stage[n][:, :, :], w.rearrange("(p c) n -> p c n", p=P)).then_inc(w_loaded[n], 16)

        @block.gpsimd
        def _(pool):
            nc.gpsimd.iota(expert_i[:, :], [[1, E]], base=0, channel_multiplier=0).then_inc(made, 1)
            nc.gpsimd.iota(step_i[:, :], [[1, NT]], base=0, channel_multiplier=0).then_inc(made, 1)
            nc.gpsimd.memset(ones[:, :], 1.0).then_inc(made, 1)
            nc.gpsimd.memset(ones_row[:, :], 1.0).then_inc(made, 1)
            pool.wait_ge(made, 4)
            nc.gpsimd.affine_select(out=before[:, :], in_=ones[:, :], compare_op=ALU.is_gt, fill=0.0,
                                    base=0, pattern=[[1, P]], channel_multiplier=-1).then_inc(made, 1)
            for n in range(len(shared)):
                pool.wait_ge(w_hi_done, n + 1)
                nc.gpsimd.tensor_tensor(s_lo[n][:, :, :], stage[n][:, :, :], f32(s_hi[n][:, :, :]), ALU.subtract)

        @block.scalar
        def _(act):
            for n in range(len(shared)):
                act.wait_ge(w_loaded[n], 16)
                nc.scalar.activation(s_hi[n][:, :, :], stage[n][:, :, :], ACT.Copy).then_inc(w_hi_done, 1)
            act.wait_ge(shift_done, 1)
            nc.scalar.activation(expd[:, :, :], shifted[:, :, :], ACT.Exp).then_inc(exp_done, 1)

        @block.tensor
        def _(pe):
            pe.wait_ge(made, 5)
            pe.wait_ge(both_done, 1)
            flat = both[:, :, :].rearrange("p e t -> p (e t)")
            nc.tensor.matmul(psB[:, :], before[:, :], flat, start=True, stop=True)
            nc.tensor.matmul(psC[:, :], ones[:, :], flat, start=True, stop=True).then_inc(counted, 1)

        @block.vector
        def _(dve):
            steps = [0]
            done = step_done

            def then(ins):
                steps[0] += 1
                ins.then_inc(done, 1)
                dve.wait_ge(done, steps[0])

            v = nc.vector
            dve.wait_ge(bias_loaded, 16)
            then(v.tensor_tensor(choice[:, :, :], lg, bias_b[:, :].unsqueeze(1).to_broadcast([P, TT, E]), ALU.add))
            for t in range(TT):
                last = v.max(top[:, t, :], choice[:, t, :])
            then(last)
            for t in range(TT):
                last = v.max_index(at[:, t, :], top[:, t, :], choice[:, t, :])
            then(last)
            then(v.tensor_copy(at_f[:, :, :], at[:, :, 0:2].rearrange("p t k -> p k t")))
            dve.wait_ge(made, 5)
            v.tensor_copy(step_at[:, :], step_i[:, :])
            then(v.tensor_copy(expert_id[:, :], expert_i[:, :]))
            for k in range(2):
                last = v.tensor_tensor(hot[:, k, :, :], expert_id[:, :].unsqueeze(2).to_broadcast([P, E, TT]),
                                       at_f[:, k, :].unsqueeze(1).to_broadcast([P, E, TT]), ALU.is_equal)
            then(last)
            v.tensor_tensor(both[:, :, :], hot[:, 0, :, :], hot[:, 1, :, :], ALU.add).then_inc(both_done, 1)

            then(v.tensor_reduce(peak[:, :], lg, AX_X, ALU.max))
            v.tensor_tensor(shifted[:, :, :], lg, peak[:, :].unsqueeze(2).to_broadcast([P, TT, E]), ALU.subtract).then_inc(shift_done, 1)
            dve.wait_ge(exp_done, 1)
            then(v.tensor_reduce(total[:, :], expd[:, :, :], AX_X, ALU.add))
            then(v.reciprocal(inverse[:, :], total[:, :]))
            then(v.tensor_tensor(score[:, :, :], expd[:, :, :], inverse[:, :].unsqueeze(2).to_broadcast([P, TT, E]), ALU.mult))
            for k in range(2):
                last = v.tensor_tensor(picked[:, k, :, :], hot[:, k, :, :], score[:, :, :].rearrange("p t e -> p e t"), ALU.mult)
            then(last)
            for k in range(2):
                last = v.tensor_reduce(kept[:, k, :], picked[:, k, :, :].rearrange("p e t -> p t e"), AX_X, ALU.add)
            then(last)
            then(v.tensor_tensor(kept_sum[:, :], kept[:, 0, :], kept[:, 1, :], ALU.add))
            then(v.reciprocal(kept_inv[:, :], kept_sum[:, :]))
            then(v.tensor_tensor(weights[:, :, :], kept[:, :, :], kept_inv[:, :].unsqueeze(1).to_broadcast([P, 2, TT]), ALU.mult))

            dve.wait_ge(counted, 1)
            then(v.tensor_copy(counts[:, :, :], psC[:, :].rearrange("p (e t) -> p e t", t=TT)))
            then(v.tensor_tensor_scan(upto[:, :, :].rearrange("p e t -> p (e t)"), ones_row[:, :],
                                      counts[:, :, :].rearrange("p e t -> p (e t)"), 0.0, ALU.mult, ALU.add))
            then(v.tensor_tensor(rank[:, :, :], upto[:, :, :], counts[:, :, :], ALU.subtract))
            then(v.tensor_tensor(count[:, :], upto[:, :, TT - 1], rank[:, :, 0], ALU.subtract))
            then(v.tensor_scalar(full[:, :, :], step_at[:, 0:KT].unsqueeze(1).to_broadcast([P, E, KT]), float(R), None, ALU.mult))
            then(v.tensor_tensor(full[:, :, :], count[:, :].unsqueeze(2).to_broadcast([P, E, KT]), full[:, :, :], ALU.is_gt))
            then(v.tensor_reduce(tiles[:, :], full[:, :, :], AX_X, ALU.add))
            then(v.tensor_tensor_scan(tiles_upto[:, :], ones_row[:, 0:E], tiles[:, :], 0.0, ALU.mult, ALU.add))
            then(v.tensor_tensor(origin[:, :], tiles_upto[:, :], tiles[:, :], ALU.subtract))
            then(v.tensor_scalar(origin[:, :], origin[:, :], float(R), None, ALU.mult))
            then(v.tensor_tensor(origin[:, :], origin[:, :], rank[:, :, 0], ALU.subtract))
            then(v.tensor_tensor(rank[:, :, :], rank[:, :, :], psB[:, :].rearrange("p (e t) -> p e t", t=TT), ALU.add))
            then(v.tensor_tensor(rank[:, :, :], rank[:, :, :], origin[:, :].unsqueeze(2).to_broadcast([P, E, TT]), ALU.add))
            for k in range(2):
                last = v.tensor_tensor(picked[:, k, :, :], hot[:, k, :, :], rank[:, :, :], ALU.mult)
            then(last)
            for k in range(2):
                last = v.tensor_reduce(slot_f[:, k, :], picked[:, k, :, :].rearrange("p e t -> p t e"), AX_X, ALU.add)
            then(last)
            then(v.tensor_copy(slots[:, :, :], slot_f[:, :, :]))
            then(v.tensor_tensor(owner[:, :, :], tiles_upto[:, :].unsqueeze(1).to_broadcast([P, NT, E]),
                                 step_at[:, :].unsqueeze(2).to_broadcast([P, NT, E]), ALU.is_le))
            then(v.tensor_reduce(owner_f[:, :], owner[:, :, :], AX_X, ALU.add))
            then(v.tensor_scalar(owner_f[:, :], owner_f[:, :], float(E - 1), None, ALU.min))
            then(v.tensor_copy(tile_expert[:, :], owner_f[0:1, :]))


def experts(nc, sh, gathered, results, tile_expert, wu, wg, wd, ident):
    L, LC, F, R, NT, E = sh.L, sh.LC, sh.F, sh.R, sh.NT, sh.E
    FC = F // P
    RT = R // P
    with ExitStack() as ctx:
        take = ctx.enter_context(phase_semaphores(nc))

        def pair(name, shape, dt=F32):
            return [ctx.enter_context(nc.sbuf_tensor(f"{name}{k}_expert", shape, dt)) for k in range(2)]

        def sem(name):
            return take(f"{name}_expert")

        def sem2(name):
            return [sem(f"{name}{k}") for k in range(2)]

        up_raw, dn_raw = pair("up_raw", [P, 2, LC, F]), pair("down_raw", [P, FC, L])
        up_hi, up_lo = pair("up_hi", [P, 2, LC, F], F32R), pair("up_lo", [P, 2, LC, F], F32R)
        dn_hi, dn_lo = pair("down_hi", [P, FC, L], F32R), pair("down_lo", [P, FC, L], F32R)
        rows = pair("rows", [P, RT, L])
        xhi, xlo = pair("xT_hi", [P, LC, R], F32R), pair("xT_lo", [P, LC, R], F32R)
        gate, h = pair("gated", [P, FC * R]), pair("hidden", [P, FC * R])
        hhi, hlo = pair("hidden_hi", [P, FC * R], F32R), pair("hidden_lo", [P, FC * R], F32R)
        out = pair("out_rows", [P, RT, L])
        psT = ctx.enter_context(nc.psum_tensor("turned_expert", [P, LC, R], F32))
        psU = ctx.enter_context(nc.psum_tensor("up_expert", [P, FC * R], F32))
        psG = ctx.enter_context(nc.psum_tensor("gate_expert", [P, FC * R], F32))
        psY = [ctx.enter_context(nc.psum_tensor(f"down{k}_expert", [P, RT, L], F32)) for k in range(2)]
        rows_loaded, up_loaded, dn_loaded, stored = sem2("rows_loaded"), sem2("up_loaded"), sem2("down_loaded"), sem2("stored")
        turned, x_hi, x_lo = sem("turned"), sem("x_hi"), sem("x_lo")
        up_hi_done, up_lo_done, dn_hi_done, dn_lo_done = sem("up_hi"), sem("up_lo"), sem("down_hi"), sem("down_lo")
        up_done, gate_done, silu_done, h_done, h_hi, h_lo = (sem("up_done"), sem("gate_done"), sem("silu_done"),
                                                             sem("h_done"), sem("h_hi"), sem("h_lo"))
        down_done, copied = sem("down_done"), sem("copied")
        block = ctx.enter_context(nc.Block())
        res = results.rearrange("(j r p) d -> j p r d", r=RT, p=P)
        gat = gathered.rearrange("(j r p) d -> j p r d", r=RT, p=P)
        wuv = wu.rearrange("e (p c) n -> e p (c n)", c=LC)
        wgv = wg.rearrange("e (p c) n -> e p (c n)", c=LC)
        wdv = wd.rearrange("e (p c) n -> e p (c n)", c=FC)

        def tiles(eng, first, last, body):
            with eng.Fori(0, (last - first) // 2) as i:
                for k in range(2):
                    body(i * 2 + (first + k), (first + k) % 2)

        @block.sync
        def _(sp):
            for k in range(2):
                sp.sem_inc(stored[k], 16)

            def load(j, s):
                sp.wait_ge(turned, j + 1)
                sp.dma_start(rows[s][:, :, :], gat[bass.ds(j, 1)].rearrange("j p r d -> (j p) r d")).then_inc(rows_loaded[s], 16)
                e = sp.value_load(tile_expert[0:1, bass.ds(j, 1)], min_val=0, max_val=E - 1)
                sp.wait_ge(up_lo_done, j + 1)
                for n, w in enumerate((wuv, wgv)):
                    sp.dma_start(up_raw[s][:, n, :, :].rearrange("p c n -> p (c n)"),
                                 w[bass.ds(e, 1)].rearrange("e p n -> (e p) n")).then_inc(up_loaded[s], 16)
                sp.wait_ge(dn_lo_done, j + 1)
                sp.dma_start(dn_raw[s][:, :, :].rearrange("p c n -> p (c n)"),
                             wdv[bass.ds(e, 1)].rearrange("e p n -> (e p) n")).then_inc(dn_loaded[s], 16)

            def store(j, s):
                sp.wait_ge(copied, j + 3)
                sp.dma_start(res[bass.ds(j, 1)].rearrange("j p r d -> (j p) r d"), out[s][:, :, :]).then_inc(stored[s], 16)

            load(0, 0)
            load(1, 1)
            load(2, 0)

            def body(j, s):
                load(j + 3, 1 - s)
                store(j, s)

            tiles(sp, 0, NT - 4, body)
            load(NT - 1, 1)
            for j in range(NT - 4, NT):
                store(j, j % 2)
            for k in range(2):
                sp.wait_ge(stored[k], 16 * (NT // 2 + 1))

        @block.scalar
        def _(act):
            act.sem_inc(silu_done, 1)
            act.sem_inc(copied, 2)

            def split_up(j, s):
                act.wait_ge(up_loaded[s], (j - s) * 16 + 32)
                nc.scalar.activation(up_hi[s][:, :, :, :].rearrange("p n c f -> p (n c f)"),
                                     up_raw[s][:, :, :, :].rearrange("p n c f -> p (n c f)"), ACT.Copy).then_inc(up_hi_done, 1)
                act.wait_ge(turned, j + 3)
                nc.scalar.activation(xhi[s][:, :, :], psT[:, :, :], ACT.Copy).then_inc(x_hi, 1)

            def split_down(j, s):
                act.wait_ge(dn_loaded[s], (j - s) * 8 + 16)
                act.wait_ge(down_done, j + 1)
                nc.scalar.activation(dn_hi[s][:, :, :], dn_raw[s][:, :, :], ACT.Copy).then_inc(dn_hi_done, 1)

            def hidden(j, s):
                act.wait_ge(up_done, j + 1)
                nc.scalar.activation(gate[s][:, :], psU[:, :], ACT.Silu).then_inc(silu_done, 1)
                act.wait_ge(h_done, j + 2)
                nc.scalar.activation(hhi[s][:, :], h[s][:, :], ACT.Copy).then_inc(h_hi, 1)

            def copy_out(j, s):
                act.wait_ge(down_done, j + 3)
                act.wait_ge(stored[s], (j - s) * 8 + 16)
                nc.scalar.copy(out[s][:, :, :], psY[s][:, :, :]).then_inc(copied, 1)

            split_up(0, 0)
            split_up(1, 1)
            split_down(0, 0)
            hidden(0, 0)

            def body(j, s, ahead=True):
                if ahead:
                    split_up(j + 2, s)
                split_down(j + 1, 1 - s)
                hidden(j + 1, 1 - s)
                copy_out(j, s)

            tiles(act, 0, NT - 2, body)
            body(NT - 2, 0, False)
            copy_out(NT - 1, 1)

        @block.vector
        def _(dve):
            dve.sem_inc(h_done, 1)
            dve.sem_inc(up_lo_done, 2)
            dve.sem_inc(dn_lo_done, 2)
            dve.sem_inc(x_lo, 1)

            def split_up(j, s):
                dve.wait_ge(up_hi_done, j + 1)
                nc.vector.tensor_tensor(up_lo[s][:, :, :, :].rearrange("p n c f -> p (n c f)"),
                                        up_raw[s][:, :, :, :].rearrange("p n c f -> p (n c f)"),
                                        f32(up_hi[s][:, :, :, :].rearrange("p n c f -> p (n c f)")), ALU.subtract).then_inc(up_lo_done, 1)
                dve.wait_ge(x_hi, j + 1)
                nc.vector.tensor_tensor(xlo[s][:, :, :], psT[:, :, :], f32(xhi[s][:, :, :]), ALU.subtract).then_inc(x_lo, 1)

            def split_down(j, s):
                dve.wait_ge(dn_hi_done, j + 1)
                nc.vector.tensor_tensor(dn_lo[s][:, :, :], dn_raw[s][:, :, :], f32(dn_hi[s][:, :, :]), ALU.subtract).then_inc(dn_lo_done, 1)

            def hidden(j, s):
                dve.wait_ge(silu_done, j + 2)
                dve.wait_ge(gate_done, j + 1)
                nc.vector.tensor_tensor(h[s][:, :], psG[:, :], gate[s][:, :], ALU.mult).then_inc(h_done, 1)

            split_up(0, 0)
            split_up(1, 1)
            split_down(0, 0)
            hidden(0, 0)

            def body(j, s, ahead=True):
                if ahead:
                    split_up(j + 2, s)
                split_down(j + 1, 1 - s)
                hidden(j + 1, 1 - s)

            tiles(dve, 0, NT - 2, body)
            body(NT - 2, 0, False)

        @block.gpsimd
        def _(pool):
            def body(j, s):
                pool.wait_ge(h_hi, j + 1)
                nc.gpsimd.tensor_tensor(hlo[s][:, :], h[s][:, :], f32(hhi[s][:, :]), ALU.subtract).then_inc(h_lo, 1)

            tiles(pool, 0, NT, body)

        @block.tensor
        def _(pe):
            pe.sem_inc(turned, 2)
            pe.sem_inc(down_done, 2)

            def turn(j, s):
                pe.wait_ge(rows_loaded[s], (j - s) * 8 + 16)
                pe.wait_ge(x_lo, j + 1)
                for r in range(RT):
                    for c in range(LC):
                        last = nc.tensor.transpose(psT[:, c, r * P:(r + 1) * P], rows[s][:, r, c::LC], ident[:, :])
                last.then_inc(turned, 1)

            def up(j, s):
                pe.wait_ge(up_lo_done, j + 3)
                pe.wait_ge(x_lo, j + 2)
                for n, (bank, done) in enumerate(((psU, up_done), (psG, gate_done))):
                    pe.wait_ge((silu_done, h_done)[n], j + 1)
                    for fc in range(FC):
                        for c in range(LC):
                            last = three_passes(nc, bank[:, fc * R:(fc + 1) * R], up_hi[s][:, n, c, fc::FC],
                                                up_lo[s][:, n, c, fc::FC], xhi[s][:, c, :], xlo[s][:, c, :], c == 0, c == LC - 1)
                    last.then_inc(done, 1)

            def down(j, s):
                pe.wait_ge(dn_lo_done, j + 3)
                pe.wait_ge(h_lo, j + 1)
                pe.wait_ge(copied, j + 1)
                for r in range(RT):
                    for fc in range(FC):
                        col = slice(fc * R + r * P, fc * R + (r + 1) * P)
                        last = three_passes(nc, psY[s][:, r, :], hhi[s][:, col], hlo[s][:, col],
                                            dn_hi[s][:, fc, :], dn_lo[s][:, fc, :], fc == 0, fc == FC - 1)
                last.then_inc(down_done, 1)

            turn(0, 0)
            turn(1, 1)
            up(0, 0)

            def body(j, s, ahead=True):
                if ahead:
                    turn(j + 2, s)
                up(j + 1, 1 - s)
                down(j, s)

            tiles(pe, 0, NT - 2, body)
            body(NT - 2, 0, False)
            down(NT - 1, 1)


def shared_half(nc, sh, half, x_mid, x_normed, w_hi, w_lo, base, gathered, results, slots, weights, out, ident):
    L, LC, R = sh.L, sh.LC, sh.R
    FS = w_hi[0].shape[2]
    FC = FS // P
    RT = R // P
    NT = sh.T // 2 // R
    TH = sh.TT // 2
    last_half = half == 1
    with ExitStack() as ctx:
        take = ctx.enter_context(phase_semaphores(nc))

        def one(name, shape, dt=F32):
            return ctx.enter_context(nc.sbuf_tensor(f"{name}_sh{half}", shape, dt))

        def pair(name, shape, dt=F32):
            return [one(f"{name}{k}", shape, dt) for k in range(2)]

        def ps(name, shape):
            return ctx.enter_context(nc.psum_tensor(f"{name}_sh{half}", shape, F32))

        def sem(name):
            return take(f"{name}_sh{half}")

        def sem2(name):
            return [sem(f"{name}{k}") for k in range(2)]

        rows = pair("rows", [P, RT, L])
        xhi, xlo = pair("xT_hi", [P, LC, R], F32R), pair("xT_lo", [P, LC, R], F32R)
        gate, h = pair("gated", [P, FC * R]), pair("hidden", [P, FC * R])
        hhi, hlo = pair("hidden_hi", [P, FC * R], F32R), pair("hidden_lo", [P, FC * R], F32R)
        xm, total = pair("x_mid", [P, RT, L]), pair("sum", [P, RT, L])
        psT, psU, psG = ps("turned", [P, LC, R]), ps("up", [P, FC * R]), ps("gate", [P, FC * R])
        psY = ps("down", [P, RT, L])
        rows_loaded, xm_loaded, stored = sem2("rows_loaded"), sem2("xm_loaded"), sem2("stored")
        turned, x_hi, x_lo = sem("turned"), sem("x_hi"), sem("x_lo")
        up_done, gate_done, silu_done, h_done, h_hi, h_lo = (sem("up_done"), sem("gate_done"), sem("silu_done"),
                                                             sem("h_done"), sem("h_hi"), sem("h_lo"))
        down_done, summed, finished = sem("down_done"), sem("summed"), sem("finished")
        if last_half:
            res, old_res = pair("results", [P, 2 * RT, L]), pair("old_results", [P, 2 * RT, L])
            acc, old_acc = one("partial", [P, RT, L]), one("old_partial", [P, RT, L])
            old_base, old_total = pair("old_base", [P, RT, L]), pair("old_sum", [P, RT, L])
            res_loaded, old_loaded, old_stored = sem2("res_loaded"), sem2("old_loaded"), sem2("old_stored")
            base_loaded = sem2("base_loaded")
            partial, old_partial, old_finished = sem("partial"), sem("old_partial"), sem("old_finished")
        else:
            NB = 4
            row = [one(f"dispatched{k}", [P, L]) for k in range(NB)]
            row_loaded, sent = [sem(f"row_loaded{k}") for k in range(NB)], [sem(f"sent{k}") for k in range(NB)]
        block = ctx.enter_context(nc.Block())

        def tiles(eng, first, last, body):
            with eng.Fori(0, (last - first) // 2) as i:
                for k in range(2):
                    body(i * 2 + (first + k), (first + k) % 2)

        def rows_of(t, j, which=half):
            return t[bass.ds(j * R + which * NT * R, R), :].rearrange("(r p) d -> p r d", p=P)

        @block.sync
        def _(sp):
            for k in range(2):
                sp.sem_inc(stored[k], 16)
                if last_half:
                    sp.sem_inc(old_stored[k], 16)

            def load(j, s):
                sp.wait_ge(turned, j + 1)
                sp.dma_start(rows[s][:, :, :], rows_of(x_normed, j)).then_inc(rows_loaded[s], 16)

            def load_late(j, s):
                sp.wait_ge(summed, j + 1)
                sp.dma_start(xm[s][:, :, :], rows_of(x_mid, j)).then_inc(xm_loaded[s], 16)
                if last_half:
                    sp.wait_ge(old_partial, j + 1)
                    sp.dma_start(old_base[s][:, :, :], rows_of(base, j, 0)).then_inc(base_loaded[s], 16)

            def store(j, s):
                if last_half:
                    sp.wait_ge(old_finished, j + 1)
                    sp.dma_start(rows_of(out, j, 0), old_total[s][:, :, :]).then_inc(old_stored[s], 16)
                    sp.wait_ge(finished, j + 1)
                else:
                    sp.wait_ge(summed, j + 3)
                sp.dma_start(rows_of(out if last_half else base, j), total[s][:, :, :]).then_inc(stored[s], 16)

            load(0, 0)
            load(1, 1)
            load_late(0, 0)
            load(2, 0)

            def body(j, s):
                load(j + 3, 1 - s)
                load_late(j + 1, 1 - s)
                store(j, s)

            tiles(sp, 0, NT - 4, body)
            load(NT - 1, 1)
            for j in range(NT - 4, NT):
                if j + 1 < NT:
                    load_late(j + 1, (j + 1) % 2)
                store(j, j % 2)
            for k in range(2):
                sp.wait_ge(stored[k], 16 * (NT // 2 + 1))
                if last_half:
                    sp.wait_ge(old_stored[k], 16 * (NT // 2 + 1))

        @block.gpsimd
        def _(pool):
            if not last_half:
                def fetch(t):
                    if t >= NB:
                        pool.wait_ge(sent[t % NB], 32 * (t // NB))
                    pool.dma_start(row[t % NB][:, :], x_normed[t * P:(t + 1) * P, :]).then_inc(row_loaded[t % NB], 16)

                for t in range(2):
                    fetch(t)
                for t in range(sh.TT):
                    if t + 2 < sh.TT:
                        fetch(t + 2)
                    pool.wait_ge(row_loaded[t % NB], 16 * (t // NB + 1))
                    for k in range(2):
                        pool.indirect_dma_start(out=gathered, out_offset=bass.IndirectOffsetOnAxis(ap=slots[:, k, t:t + 1], axis=0),
                                                in_=row[t % NB][:, :], in_offset=None).then_inc(sent[t % NB], 16)
                for k in range(NB):
                    pool.wait_ge(sent[k], 32 * (sh.TT // NB))
            else:
                for j in range(NT):
                    for y, loaded, read, t0 in ((old_res, old_loaded, old_finished, 0), (res, res_loaded, finished, TH)):
                        if j >= 2:
                            pool.wait_ge(read, j - 1)
                        for r in range(RT):
                            for k in range(2):
                                at = slots[:, k, t0 + j * RT + r:t0 + j * RT + r + 1]
                                pool.indirect_dma_start(out=y[j % 2][:, 2 * r + k, :], out_offset=None, in_=results,
                                                        in_offset=bass.IndirectOffsetOnAxis(ap=at, axis=0)).then_inc(loaded[j % 2], 16)

        @block.scalar
        def _(act):
            act.sem_inc(silu_done, 1)

            def high(j, s):
                act.wait_ge(turned, j + 3)
                nc.scalar.activation(xhi[s][:, :, :], psT[:, :, :], ACT.Copy).then_inc(x_hi, 1)

            def hidden(j, s):
                act.wait_ge(up_done, j + 1)
                nc.scalar.activation(gate[s][:, :], psU[:, :], ACT.Silu).then_inc(silu_done, 1)
                act.wait_ge(h_done, j + 2)
                nc.scalar.activation(hhi[s][:, :], h[s][:, :], ACT.Copy).then_inc(h_hi, 1)

            high(0, 0)
            high(1, 1)
            hidden(0, 0)

            def body(j, s):
                high(j + 2, s)
                hidden(j + 1, 1 - s)

            tiles(act, 0, NT - 2, body)
            hidden(NT - 1, 1)

        @block.vector
        def _(dve):
            dve.sem_inc(h_done, 1)
            dve.sem_inc(x_lo, 1)
            dve.sem_inc(summed, 2)
            if last_half:
                dve.sem_inc(old_partial, 2)

            def low(j, s):
                dve.wait_ge(x_hi, j + 1)
                nc.vector.tensor_tensor(xlo[s][:, :, :], psT[:, :, :], f32(xhi[s][:, :, :]), ALU.subtract).then_inc(x_lo, 1)

            def hidden(j, s):
                dve.wait_ge(silu_done, j + 2)
                dve.wait_ge(gate_done, j + 1)
                nc.vector.tensor_tensor(h[s][:, :], psG[:, :], gate[s][:, :], ALU.mult).then_inc(h_done, 1)
                dve.wait_ge(h_hi, j + 1)
                nc.vector.tensor_tensor(hlo[s][:, :], h[s][:, :], f32(hhi[s][:, :]), ALU.subtract).then_inc(h_lo, 1)

            def add_result(dst, src, y, k, t, done):
                for r in range(RT):
                    last = nc.vector.scalar_tensor_tensor(out=dst[:, r, :], in0=y[:, 2 * r + k, :], scalar=weights[:, k, bass.ds(t + r, 1)],
                                                          in1=src[:, r, :], op0=ALU.mult, op1=ALU.add)
                last.then_inc(done, 1)

            def old_rows(j, s):
                dve.wait_ge(base_loaded[s], (j - s) * 8 + 16)
                dve.wait_ge(old_loaded[s], (j - s) * (8 * 2 * RT) + 16 * 2 * RT)
                add_result(old_acc, old_base[s], old_res[s], 0, j * RT, old_partial)
                dve.wait_ge(old_partial, j + 3)
                dve.wait_ge(old_stored[s], (j - s) * 8 + 16)
                add_result(old_total[s], old_acc, old_res[s], 1, j * RT, old_finished)

            def sums(j, s):
                dve.wait_ge(down_done, j + 1)
                dve.wait_ge(xm_loaded[s], (j - s) * 8 + 16)
                if last_half:
                    nc.vector.tensor_tensor(acc[:, :, :], psY[:, :, :], xm[s][:, :, :], ALU.add).then_inc(summed, 1)
                    dve.wait_ge(summed, j + 3)
                    dve.wait_ge(res_loaded[s], (j - s) * (8 * 2 * RT) + 16 * 2 * RT)
                    add_result(acc, acc, res[s], 0, j * RT + TH, partial)
                    dve.wait_ge(partial, j + 1)
                    dve.wait_ge(stored[s], (j - s) * 8 + 16)
                    add_result(total[s], acc, res[s], 1, j * RT + TH, finished)
                else:
                    dve.wait_ge(stored[s], (j - s) * 8 + 16)
                    nc.vector.tensor_tensor(total[s][:, :, :], psY[:, :, :], xm[s][:, :, :], ALU.add).then_inc(summed, 1)

            low(0, 0)
            low(1, 1)
            hidden(0, 0)

            def body(j, s):
                low(j + 2, s)
                hidden(j + 1, 1 - s)
                if last_half:
                    old_rows(j, s)
                sums(j, s)

            tiles(dve, 0, NT - 2, body)
            hidden(NT - 1, 1)
            for j in (NT - 2, NT - 1):
                if last_half:
                    old_rows(j, j % 2)
                sums(j, j % 2)

        @block.tensor
        def _(pe):
            pe.sem_inc(turned, 2)

            def turn(j, s):
                pe.wait_ge(rows_loaded[s], (j - s) * 8 + 16)
                pe.wait_ge(x_lo, j + 1)
                for r in range(RT):
                    for c in range(LC):
                        last = nc.tensor.transpose(psT[:, c, r * P:(r + 1) * P], rows[s][:, r, c::LC], ident[:, :])
                last.then_inc(turned, 1)

            def up(j, s):
                pe.wait_ge(x_lo, j + 2)
                for n, (bank, done) in enumerate(((psU, up_done), (psG, gate_done))):
                    pe.wait_ge((silu_done, h_done)[n], j + 1)
                    for fc in range(FC):
                        f = slice(fc, FS, FC)
                        for c in range(LC):
                            last = three_passes(nc, bank[:, fc * R:(fc + 1) * R], w_hi[n][:, c, f], w_lo[n][:, c, f],
                                                xhi[s][:, c, :], xlo[s][:, c, :], c == 0, c == LC - 1)
                    last.then_inc(done, 1)

            def down(j, s):
                pe.wait_ge(h_lo, j + 1)
                pe.wait_ge(summed, j + 2)
                for r in range(RT):
                    for fc in range(FC):
                        col = slice(fc * R + r * P, fc * R + (r + 1) * P)
                        last = three_passes(nc, psY[:, r, :], hhi[s][:, col], hlo[s][:, col],
                                            w_hi[2][:, fc, :], w_lo[2][:, fc, :], fc == 0, fc == FC - 1)
                last.then_inc(down_done, 1)

            turn(0, 0)
            turn(1, 1)
            up(0, 0)

            def body(j, s):
                turn(j + 2, s)
                up(j + 1, 1 - s)
                down(j, s)

            tiles(pe, 0, NT - 2, body)
            up(NT - 1, 1)
            down(NT - 2, 0)
            down(NT - 1, 1)


def program(nc, x, context, taps, skip, router, bias, wu, wg, wd, su, sg, sd, out):
    sh = Shapes(x, taps, router, wu)
    rows, context_rows = x.rearrange("b s l -> (b s) l"), context.rearrange("b s l -> (b s) l")

    out = out.rearrange("b s l -> (b s) l")

    def dram(name, shape):
        return nc.dram_tensor(name, shape, F32).ap()

    taps_rev = dram("taps_rev", (sh.H, sh.RB))
    x_mid, x_normed, base = dram("x_mid", (sh.T, sh.L)), dram("x_mid_normed", (sh.T, sh.L)), dram("base", (sh.T // 2, sh.L))
    gathered, results = dram("gathered", (sh.NT * sh.R, sh.L)), dram("results", (sh.NT * sh.R, sh.L))
    with ExitStack() as ctx:
        def sb(name, shape, dt=F32, scope=ctx):
            return scope.enter_context(nc.sbuf_tensor(name, shape, dt))

        ident, eps, router_T = sb("identity", [P, P]), sb("eps", [P, 1]), sb("router_T", [P, sh.LC, sh.E])
        logits = sb("logits", [P, sh.TT * sh.E])
        prepare(nc, sh, taps, skip, router, taps_rev, router_T, ident, eps)
        with ExitStack() as attention:
            cT, qT0, qT1 = (sb(name, [P, sh.LC * sh.HB * sh.H * sh.CE], F32, attention) for name in ("cT", "qT0", "qT1"))
            for leaving, entering, oT, qT in ((None, 0, None, qT0), (0, 1, qT0, qT1), (1, None, qT1, None)):
                change_rows(nc, sh, leaving, entering, rows, context_rows, cT, qT, oT, x_mid, x_normed, router_T, logits, ident, eps)
                if entering is not None:
                    long_convolution(nc, sh, entering, taps_rev, cT, qT, gathered)
        slots, weights, tile_expert = sb("slots", [P, 2, sh.TT], U32), sb("weights", [P, 2, sh.TT]), sb("tile_expert", [1, sh.NT], I32)
        shared = (su[0], sg[0], sd[0])
        s_hi, s_lo = ([sb(f"shared_{part}{n}", [P, w.shape[0] // P, w.shape[1]], F32R) for n, w in enumerate(shared)] for part in ("hi", "lo"))
        routing(nc, sh, logits, bias, slots, weights, tile_expert, shared, s_hi, s_lo)
        for half in range(2):
            shared_half(nc, sh, half, x_mid, x_normed, s_hi, s_lo, base, gathered, results, slots, weights, out, ident)
            if half == 0:
                experts(nc, sh, gathered, results, tile_expert, wu, wg, wd, ident)


_INS = ['x', 'ctx_2048', 'L0_xattn_ssm_kernel', 'L0_xattn_D', 'L0_ffn_router_w', 'L0_ffn_router_bias',
        'L0_ffn_Wu', 'L0_ffn_Wg', 'L0_ffn_Wd', 'L0_ffn_Su', 'L0_ffn_Sg', 'L0_ffn_Sd']


def kernel(**inputs):
    import numpy as _np
    import concourse.bacc as _bacc
    from concourse import mybir as _mybir
    from concourse.bass_utils import run_bass_kernel_spmd as _run

    nc = _bacc.Bacc("TRN2", target_bir_lowering=False, num_devices=1)
    arrays, args = {}, []
    for name in _INS:
        a = _np.ascontiguousarray(inputs[name])
        arrays[f"in_{name}"] = a
        args.append(nc.dram_tensor(f"in_{name}", a.shape, _mybir.dt.from_np(a.dtype), kind="ExternalInput").ap())
    out = nc.dram_tensor("out", inputs["x"].shape, _mybir.dt.from_np(_np.dtype("float32")), kind="ExternalOutput").ap()
    program(nc, *args, out)
    r = _run(nc, [arrays], core_ids=[0])
    return r.results[0]["out"]
```

```python
from contextlib import ExitStack, contextmanager

import concourse.bass as bass
from concourse import mybir

ALU = mybir.AluOpType
ACT = mybir.ActivationFunctionType
F32 = mybir.dt.float32
F32R = mybir.dt.float32r
U32 = mybir.dt.uint32
I32 = mybir.dt.int32
AX_X = mybir.AxisListType.X

P = 128
EPS = 1e-5
HALVES = 2



def three_passes(nc, out, w_hi, w_lo, x_hi, x_lo, first, last):
    nc.tensor.matmul(out, w_hi, x_hi, start=first, stop=False)
    nc.tensor.matmul(out, w_lo, x_hi, start=False, stop=False)
    return nc.tensor.matmul(out, w_hi, x_lo, start=False, stop=last)


def f32(ap):
    return ap.bitcast(F32)


@contextmanager
def phase_semaphores(nc):
    taken = []

    def take(name):
        taken.append(nc.alloc_semaphore(name=name))
        return taken[-1]

    yield take
    nc.clear_and_free_semaphores(taken)
    nc.all_engine_barrier()


class Shapes:

    def __init__(self, x, taps, router, wu):
        self.B, self.S, self.L = x.shape
        self.H = taps.shape[0]
        self.C = self.S // self.H
        self.T = self.B * self.S
        self.LC = self.L // P
        self.TT = self.T // P
        self.E = router.shape[0]
        self.F = wu.shape[2]
        self.HB = self.B // HALVES
        self.HT = self.HB * self.S // P
        self.CE = self.C + self.C // 2
        self.ND = self.C // 2 + 1
        self.NP = self.C * (self.C + 1) // 2
        self.R = 2 * P
        self.NT = (2 * self.T + self.E * (P - 1)) // P
        store = HALVES * (self.H // 2) * P
        self.GR = -(-self.NT * P // store) * store
        self.RB = self.L + P


def prepare(nc, sh, taps, skip, router, taps_rev, router_T, ident, eps):
    H, L, LC, RB, E = sh.H, sh.L, sh.LC, sh.RB, sh.E
    with ExitStack() as ctx:
        take = ctx.enter_context(phase_semaphores(nc))

        raw = ctx.enter_context(nc.sbuf_tensor("taps_raw", [H, L], F32))
        rev = ctx.enter_context(nc.sbuf_tensor("taps_reversed", [H, RB], F32))
        d = ctx.enter_context(nc.sbuf_tensor("skip_weight", [H, 1], F32))
        loaded = take("taps_loaded")
        d_loaded = take("skip_loaded")
        cleared = take("reversed_cleared")
        turned = take("taps_turned")
        added = take("skip_added")
        stored = take("taps_stored")
        blank = take("identity_blank")
        ident_made, router_loaded, router_turned = take("identity_made"), take("router_loaded"), take("router_turned")
        router_rows = ctx.enter_context(nc.sbuf_tensor("router_rows", [E, L], F32))
        ps = ctx.enter_context(nc.psum_tensor("router_turned", [P, LC, E], F32))
        block = ctx.enter_context(nc.Block())

        @block.sync
        def _(sp):
            sp.dma_start(raw[:, :], taps).then_inc(loaded, 16)
            sp.dma_start(d[:, :], skip.rearrange("(h a) -> h a", a=1)).then_inc(d_loaded, 16)
            sp.dma_start(router_rows[:, :], router).then_inc(router_loaded, 16)
            sp.wait_ge(added, 1)
            sp.dma_start(taps_rev, rev[:, :]).then_inc(stored, 16)
            sp.wait_ge(stored, 16)

        @block.gpsimd
        def _(pool):
            nc.gpsimd.memset(ident[:, :], 0.0).then_inc(blank, 1)
            pool.wait_ge(blank, 1)
            nc.gpsimd.affine_select(out=ident[:, :], in_=ident[:, :], compare_op=ALU.not_equal, fill=1.0,
                                    base=0, pattern=[[-1, P]], channel_multiplier=1).then_inc(ident_made, 1)

        @block.tensor
        def _(pe):
            pe.wait_ge(ident_made, 1)
            pe.wait_ge(router_loaded, 16)
            for c in range(LC):
                last = nc.tensor.transpose(ps[:, c, :], router_rows[:, c::LC], ident[0:E, 0:E])
            last.then_inc(router_turned, 1)

        @block.vector
        def _(dve):
            nc.vector.memset(eps[:, :], EPS)
            nc.vector.memset(rev[:, L:RB], 0.0).then_inc(cleared, 1)
            dve.wait_ge(loaded, 16)
            nc.vector.tensor_copy(rev[:, 0:L], raw[:, ::-1]).then_inc(turned, 1)
            dve.wait_ge(turned, 1)
            dve.wait_ge(cleared, 1)
            dve.wait_ge(d_loaded, 16)
            nc.vector.tensor_tensor(rev[:, L - 1:L], rev[:, L - 1:L], d[:, :], ALU.add).then_inc(added, 1)
            dve.wait_ge(router_turned, 1)
            nc.vector.tensor_copy(router_T[:, :, :], ps[:, :, :])


def change_rows(nc, sh, leaving, entering, x, ctx_rows, cT, qT, oT, x_mid, x_mid_normed, router_T, logits, ident, eps):
    L, LC, HB, H, C, CE, E = sh.L, sh.LC, sh.HB, sh.H, sh.C, sh.CE, sh.E
    U = 4
    NK = sh.S // P
    heads = P // C
    STEPS = sh.HT // U
    here = f"rows{leaving}{entering}"
    with ExitStack() as ctx:
        take = ctx.enter_context(phase_semaphores(nc))

        def sb(name, shape):
            return ctx.enter_context(nc.sbuf_tensor(f"{name}_{here}", shape, F32))

        def ps(name, shape=(P, L)):
            return ctx.enter_context(nc.psum_tensor(f"{name}_{here}", list(shape), F32))

        def sem(name):
            return take(f"{name}_{here}")

        def sems(name):
            return [sem(f"{name}{u}") for u in range(U)]

        if entering is not None:
            xin, cin, xn = sb("x_in", [P, U, L]), sb("c_in", [P, U, L]), sb("x_in_normed", [P, U, L])
            stats, mv, std, rstd = (sb("in_stats", [P, U, 6]), sb("in_mean_var", [P, U, 2]),
                                    sb("in_std", [P, U, 1]), sb("in_rstd", [P, U, 1]))
            psC, psX = [ps(f"turned_c{k}") for k in range(2)], [ps(f"turned_x{k}") for k in range(2)]
            x_loaded, c_loaded = sems("x_loaded"), sems("c_loaded")
            stats_done, mean_done, std_done, rstd_done = sem("stats"), sem("mean"), sem("std"), sem("rstd")
            x_normed, c_turned, x_turned = sem("x_normed"), sem("c_turned"), sem("x_turned")
            c_kept, x_kept = sem("c_kept"), sem("x_kept")
        if leaving is not None:
            l_x, l_mid, l_xn, packed = sb("x_out", [P, U, L]), sb("x_mid", [P, U, L]), sb("mid_normed", [P, U, L]), sb("packed", [P, 2, L])
            l_stats, l_mv, l_std, l_rstd = (sb("out_stats", [P, U, 6]), sb("out_mean_var", [P, U, 2]),
                                            sb("out_std", [P, U, 1]), sb("out_rstd", [P, U, 1]))
            xT = sb("mid_T", [P, 2, LC * P])
            psO = [ps(f"rows{k}") for k in range(2)]
            psT, psL = ps("mid_turned"), ps("logits", (P, U * E))
            l_loaded, mid_stored, normed_stored = sems("l_loaded"), sems("mid_stored"), sems("normed_stored")
            pack_done, o_turned, added = sem("pack"), sem("o_turned"), sem("added")
            l_stats_done, l_mean_done, l_std_done, l_rstd_done = sem("l_stats"), sem("l_mean"), sem("l_std"), sem("l_rstd")
            normed, l_turned = sem("normed"), sem("l_turned")
            xT_kept, logits_done, logits_kept = sem("xT_kept"), sem("logits"), sem("logits_kept")
        holds = sem("holds")
        block = ctx.enter_context(nc.Block())

        def rows(half, i, u):
            return bass.ds(i * (U * P) + (half * sh.HT + u) * P, P)

        def place(t, i, u):
            v = t[:, :].rearrange("p (c n) -> p c n", c=LC)
            v = v[:, :, bass.ds(i * (U // NK * H * CE) + (u // NK * H + u % NK * heads) * CE, heads * CE)]
            return v.rearrange("p c (h r) -> p c h r", r=CE)

        def keep(copy, t, src, i, u, done):
            d, s = place(t, i, u), src[:, :].rearrange("p (c h r) -> p c h r", c=LC, r=C)
            copy(d[:, :, :, 0:C], s)
            copy(d[:, :, :, C:CE], s[:, :, :, 0:CE - C]).then_inc(done, 1)

        @block.sync
        def _(sp):
            def body(a, b):
                if a is not None:
                    for u in range(U):
                        if leaving is not None:
                            sp.wait_ge(added, a * U + u + 1)
                            sp.dma_start(l_x[:, u, :], x[rows(leaving, a, u), :]).then_inc(l_loaded[u], 16)
                    for u in range(U):
                        if entering is not None:
                            sp.wait_ge(c_turned, a * U + u + 1)
                            sp.dma_start(cin[:, u, :], ctx_rows[rows(entering, a, u), :]).then_inc(c_loaded[u], 16)
                for u in range(U):
                    if a is not None and entering is not None:
                        sp.wait_ge(x_normed, a * U + u + 1)
                        sp.dma_start(xin[:, u, :], x[rows(entering, a, u), :]).then_inc(x_loaded[u], 16)
                    if b is not None and leaving is not None:
                        sp.wait_ge(normed, b * U + u + 1)
                        sp.dma_start(x_mid_normed[rows(leaving, b, u), :], l_xn[:, u, :]).then_inc(normed_stored[u], 16)
                if a is not None and leaving is not None:
                    for u in range(U):
                        sp.wait_ge(added, a * U + u + 1 + U)
                        sp.dma_start(x_mid[rows(leaving, a, u), :], l_mid[:, u, :]).then_inc(mid_stored[u], 16)

            if leaving is not None:
                for u in range(U):
                    sp.sem_inc(mid_stored[u], 16)
                    sp.sem_inc(normed_stored[u], 16)
            body(0, None)
            with sp.Fori(0, STEPS - 1) as i:
                body(i + 1, i)
            if leaving is not None:
                body(None, STEPS - 1)
                for u in range(U):
                    sp.wait_ge(mid_stored[u], 16 * (STEPS + 1))
                    sp.wait_ge(normed_stored[u], 16 * (STEPS + 1))

        @block.scalar
        def _(act):
            def pack(a, u):
                act.wait_ge(o_turned, a * U + u - 1 + U)
                nc.scalar.copy(packed[:, u % 2, :].rearrange("p (c h r) -> p c h r", c=LC, r=C),
                               place(oT, a, u)[:, :, :, 0:C]).then_inc(pack_done, 1)

            def body(a, b):
                if a is not None and leaving is not None:
                    pack(a, 0)
                    pack(a, 1)
                for u in range(U):
                    if a is not None and leaving is not None and u + 2 < U:
                        pack(a, u + 2)
                    if b is not None and leaving is not None:
                        act.wait_ge(l_turned, b * U + u + 1 + U)
                        nc.scalar.copy(xT[:, u % 2, :], psT[:, :]).then_inc(xT_kept, 1)
                    if a is not None and entering is not None:
                        act.wait_ge(c_turned, a * U + u + 1 + U)
                        keep(nc.scalar.copy, cT, psC[u % 2], a, u, c_kept)
                    if b is not None and entering is not None:
                        act.wait_ge(x_turned, b * U + u + 1 + U)
                        keep(nc.scalar.copy, qT, psX[u % 2], b, u, x_kept)
                if b is not None and leaving is not None:
                    act.wait_ge(logits_done, b + 1)
                    nc.scalar.copy(logits[:, bass.ds(b * (U * E) + leaving * sh.HT * E, U * E)], psL[:, :]).then_inc(logits_kept, 1)
                if a is not None and leaving is not None:
                    act.wait_ge(l_mean_done, a + 1)
                    nc.scalar.activation(l_std[:, :, :], l_mv[:, :, 1:2], ACT.Sqrt, bias=eps[:, :]).then_inc(l_std_done, 1)
                if a is not None and entering is not None:
                    act.wait_ge(mean_done, a + 1)
                    nc.scalar.activation(std[:, :, :], mv[:, :, 1:2], ACT.Sqrt, bias=eps[:, :]).then_inc(std_done, 1)

            if entering is not None:
                act.sem_inc(c_kept, 2)
                act.sem_inc(x_kept, 2)
            if leaving is not None:
                act.sem_inc(xT_kept, 1)
                act.sem_inc(logits_kept, 1)
            body(0, None)
            with act.Fori(0, STEPS - 1) as i:
                body(i + 1, i)
            body(None, STEPS - 1)

        @block.vector
        def _(dve):
            def aggregate(st, m, seen, out, a):
                dve.wait_ge(seen, a + 1)
                dve.sem_inc(holds, 1)
                for u in range(U):
                    last = nc.vector.bn_aggr(m[:, u, :], st[:, u, :])
                last.then_inc(out, 1)

            def norms(b):
                if leaving is not None:
                    dve.wait_ge(l_std_done, b + 1)
                    nc.vector.reciprocal(l_rstd[:, :, :], l_std[:, :, :]).then_inc(l_rstd_done, 1)
                if entering is not None:
                    dve.wait_ge(std_done, b + 1)
                    nc.vector.reciprocal(rstd[:, :, :], std[:, :, :]).then_inc(rstd_done, 1)
                for u in range(U):
                    n = b * U + u
                    if leaving is not None:
                        dve.wait_ge(l_rstd_done, b + 1)
                        dve.wait_ge(l_turned, n + 1)
                        dve.wait_ge(normed_stored[u], b * 16 + 16)
                        nc.vector.tensor_scalar(l_xn[:, u, :], l_mid[:, u, :], l_mv[:, u, 0:1], l_rstd[:, u, :],
                                                ALU.subtract, ALU.mult).then_inc(normed, 1)
                    if entering is not None:
                        dve.wait_ge(rstd_done, b + 1)
                        dve.wait_ge(x_turned, n + 1)
                        nc.vector.tensor_scalar(xn[:, u, :], xin[:, u, :], mv[:, u, 0:1], rstd[:, u, :],
                                                ALU.subtract, ALU.mult).then_inc(x_normed, 1)

            def body(a, b):
                if b is not None:
                    norms(b)
                if a is not None and leaving is not None:
                    for u in range(U):
                        dve.wait_ge(o_turned, a * U + u + 1 + U)
                        dve.wait_ge(l_loaded[u], a * 16 + 16)
                        dve.wait_ge(mid_stored[u], a * 16 + 16)
                        if b is not None:
                            dve.wait_ge(normed, b * U + u + 1)
                        nc.vector.tensor_tensor(l_mid[:, u, :], psO[u % 2][:, :], l_x[:, u, :], ALU.add).then_inc(added, 1)
                        if u:
                            dve.wait_ge(added, a * U + u + U)
                            nc.vector.bn_stats(l_stats[:, u - 1, :], l_mid[:, u - 1, :])
                    dve.wait_ge(added, a * U + 2 * U)
                    nc.vector.bn_stats(l_stats[:, U - 1, :], l_mid[:, U - 1, :]).then_inc(l_stats_done, 1)
                    aggregate(l_stats, l_mv, l_stats_done, l_mean_done, a)
                if a is not None and entering is not None:
                    if b is not None:
                        dve.wait_ge(x_normed, b * U + 2 * U)
                    for u in range(U):
                        dve.wait_ge(x_loaded[u], a * 16 + 16)
                        last = nc.vector.bn_stats(stats[:, u, :], xin[:, u, :])
                    last.then_inc(stats_done, 1)
                    aggregate(stats, mv, stats_done, mean_done, a)

            if entering is not None:
                dve.sem_inc(x_normed, U)
            if leaving is not None:
                dve.sem_inc(added, U)
            body(0, None)
            with dve.Fori(0, STEPS - 1) as i:
                body(i + 1, i)
            body(None, STEPS - 1)

        @block.tensor
        def _(pe):
            def turn(out, src, done):
                for c in range(LC):
                    last = nc.tensor.transpose(out[:, c * P:(c + 1) * P], src(c), ident[:, :])
                last.then_inc(done, 1)

            def route(b, u):
                pe.wait_ge(xT_kept, b * U + u + 2)
                for c in range(LC):
                    last = nc.tensor.matmul(psL[:, u * E:(u + 1) * E], xT[:, u % 2, c * P:(c + 1) * P],
                                            router_T[:, c, :], start=c == 0, stop=c == LC - 1)
                return last

            def body(a, b):
                if b is not None and leaving is not None:
                    pe.wait_ge(logits_kept, b + 1)
                def turn_output(u):
                    pe.wait_ge(pack_done, a * U + u + 1)
                    pe.wait_ge(added, a * U + u - 1 + U)
                    turn(psO[u % 2], lambda c: packed[:, u % 2, c * P:(c + 1) * P], o_turned)

                if a is not None and leaving is not None:
                    turn_output(0)
                    turn_output(1)
                for u in range(U):
                    if b is not None and leaving is not None:
                        pe.wait_ge(normed, b * U + u + 1)
                        pe.wait_ge(xT_kept, b * U + u + 1)
                        turn(psT, lambda c: l_xn[:, u, c::LC], l_turned)
                        if u:
                            route(b, u - 1)
                    if a is not None and entering is not None:
                        pe.wait_ge(c_loaded[u], a * 16 + 16)
                        pe.wait_ge(c_kept, a * U + u + 1)
                        turn(psC[u % 2], lambda c: cin[:, u, c * P:(c + 1) * P], c_turned)
                    if a is not None and leaving is not None and u + 2 < U:
                        turn_output(u + 2)
                    if b is not None and leaving is not None and u == U - 1:
                        route(b, u).then_inc(logits_done, 1)
                    if b is not None and entering is not None:
                        pe.wait_ge(x_normed, b * U + u + 1 + U)
                        pe.wait_ge(x_kept, b * U + u + 1)
                        turn(psX[u % 2], lambda c: xn[:, u, c * P:(c + 1) * P], x_turned)

            if entering is not None:
                pe.sem_inc(c_turned, U)
                pe.sem_inc(x_turned, U)
            if leaving is not None:
                pe.sem_inc(o_turned, U)
                pe.sem_inc(l_turned, U)
            body(0, None)
            with pe.Fori(0, STEPS - 1) as i:
                body(i + 1, i)
            body(None, STEPS - 1)


def long_convolution(nc, sh, half, taps_rev, cT, qT, gathered):
    L, LC, HB, H, C, CE, ND, NP = sh.L, sh.LC, sh.HB, sh.H, sh.C, sh.CE, sh.ND, sh.NP
    G = LC * HB
    GS = H * CE
    N = HB * NP
    ZR = gathered.shape[0] // (HALVES * (H // 2) * P)
    with ExitStack() as ctx:
        take = ctx.enter_context(phase_semaphores(nc))

        def sb(name, shape):
            return [ctx.enter_context(nc.sbuf_tensor(f"{name}{k}_conv{half}", shape, F32)) for k in range(2)]

        def sem(name):
            return take(f"{name}_conv{half}")

        traw, toep = sb("taps_rows", [P, L]), sb("toeplitz", [P, L])
        kv = sb("row_products", [P, G * NP])
        z = sb("terms", [P, G * C * C])
        y = [ctx.enter_context(nc.psum_tensor(f"conv_out{k}_{half}", [P, LC, 512], F32)) for k in range(2)]
        t_loaded = [sem(f"t_loaded{k}") for k in range(2)]
        prod_done = sem("prod_done")
        t_ready, conv_done, terms_done = sem("t_ready"), sem("conv_done"), sem("terms_done")
        folded, summed, holds = sem("folded"), sem("summed"), sem("holds")
        cleared, filled = sem("cleared"), sem("filled")
        ZERO_ROWS = gathered.shape[0] // (HALVES * (H // 2) * ZR)
        slots = gathered.rearrange("(n z) d -> n (z d)", z=ZR)
        zero = ctx.enter_context(nc.sbuf_tensor(f"zeros_conv{half}", [ZERO_ROWS, ZR * L], F32))
        block = ctx.enter_context(nc.Block())

        FULL = (ND - 1) * C

        def head(t, h, pattern, row=0, chunk=0):
            v = t[:, bass.ds(h * CE + (row + chunk * HB * GS), CE - row)]
            return bass.AP(tensor=v.tensor, offset=v.offset, ap=[list(v.ap[0])] + pattern)

        def terms(k):
            return z[k][:, :].rearrange("p (g t j) -> p g t j", t=C, j=C)

        @block.sync
        def _(sp):
            with sp.Fori(0, H // 2) as i:
                for k in range(2):
                    sp.wait_ge(t_ready, i * 2 + k + 1)
                    src = bass.AP(tensor=taps_rev.tensor, offset=taps_rev[bass.ds(i * 2 + k, 1), :].offset, ap=[[1, P], [1, L]])
                    sp.dma_start(traw[k][:, :], src).then_inc(t_loaded[k], 16)

        @block.gpsimd
        def _(pool):
            pool.sem_inc(folded, 2)

            def products(h, k):
                pool.wait_ge(conv_done, h + 1)
                each = kv[k][:, :].rearrange("p (g r) -> p g r", r=NP)
                nc.gpsimd.tensor_tensor(
                    each[:, :, 0:FULL].rearrange("p g (d j) -> p g d j", j=C),
                    head(cT, h, [[GS, G], [0, ND - 1], [1, C]]), head(cT, h, [[GS, G], [1, ND - 1], [1, C]]), ALU.mult)
                nc.gpsimd.tensor_tensor(each[:, :, FULL:NP], head(cT, h, [[GS, G], [1, C // 2]]),
                                        head(cT, h, [[GS, G], [1, C // 2]], C // 2), ALU.mult).then_inc(prod_done, 1)

            def fold(h, k):
                pool.wait_ge(terms_done, h + 3)
                nc.gpsimd.tensor_tensor(terms(k)[:, :, 0:C - ND, :], terms(k)[:, :, 0:C - ND, :],
                                        terms(k)[:, :, ND:C, :], ALU.add).then_inc(folded, 1)

            products(0, 0)
            products(1, 1)
            with pool.Fori(0, H // 2 - 1) as i:
                for k in range(2):
                    products(i * 2 + 2 + k, k)
                    fold(i * 2 + k, k)
            fold(H - 2, 0)
            fold(H - 1, 1)

        @block.scalar
        def _(act):
            act.sem_inc(t_ready, 2)
            act.wait_ge(cleared, 1)
            with act.Fori(0, H // 2) as i:
                for k in range(2):
                    act.wait_ge(t_loaded[k], i * 16 + 16)
                    act.wait_ge(conv_done, i * 2 + k + 1)
                    nc.scalar.activation(toep[k][:, :], traw[k][:, ::-1], ACT.Copy).then_inc(t_ready, 1)
                act.dma_start(slots[bass.ds(i * ZERO_ROWS + half * (H // 2) * ZERO_ROWS, ZERO_ROWS), :],
                              zero[:, :]).then_inc(filled, 16)
            act.wait_ge(filled, 16 * (H // 2))

        @block.tensor
        def _(pe):
            pe.sem_inc(conv_done, 2)
            with pe.Fori(0, H // 2) as i:
                for k in range(2):
                    n = i * 2 + k + 1
                    pe.wait_ge(t_ready, n + 2)
                    pe.wait_ge(prod_done, n)
                    pe.wait_ge(terms_done, n)
                    for lc in range(LC):
                        for mc in range(lc + 1):
                            last = nc.tensor.matmul(y[k][:, lc, 0:N], toep[k][:, (lc - mc) * P:(lc - mc + 1) * P],
                                                    kv[k][:, mc * N:(mc + 1) * N], start=mc == 0, stop=mc == lc)
                    last.then_inc(conv_done, 1)

        @block.vector
        def _(dve):
            dve.sem_inc(terms_done, 2)
            nc.vector.memset(zero[:, :], 0.0).then_inc(cleared, 1)
            dve.sem_inc(summed, 2)

            def multiply(h, k):
                dve.wait_ge(conv_done, h + 3)
                dve.wait_ge(summed, h + 1)
                zt = z[k][:, :].rearrange("p (c b t j) -> p c b t j", c=LC, b=HB, j=C)
                each = y[k][:, :, 0:N].rearrange("p c (b r) -> p c b r", r=NP)
                for c in range(LC):
                    q = head(qT, h, [[GS, HB], [1, ND - 1], [1, C]], 0, c)
                    nc.vector.tensor_tensor(zt[:, c, :, 0:ND - 1, :], each[:, c, :, 0:FULL].rearrange("p b (d j) -> p b d j", j=C), q, ALU.mult)
                for row, other in ((0, C // 2), (C // 2, 0)):
                    q = head(qT, h, [[HB * GS, LC], [GS, HB], [1, C // 2]], other)
                    nc.vector.tensor_tensor(zt[:, :, :, ND - 1, row:row + C // 2], each[:, :, :, FULL:NP], q, ALU.mult)
                for d in range(1, ND - 1):
                    for lo, hi, off in ((0, C - d, d), (C - d, C, d - C)):
                        q = head(qT, h, [[HB * GS, LC], [GS, HB], [1, hi - lo]], lo)
                        last = nc.vector.tensor_tensor(zt[:, :, :, ND - 1 + d, lo + off:hi + off], each[:, :, :, d * C + lo:d * C + hi], q, ALU.mult)
                last.then_inc(terms_done, 1)

            def add_up(h, k):
                dve.wait_ge(folded, h + 3)
                dve.sem_inc(holds, 1)
                nc.vector.tensor_reduce(head(qT, h, [[GS, G], [1, C]]),
                                        terms(k)[:, :, 0:ND, :].rearrange("p g t j -> p g j t"), AX_X, ALU.add).then_inc(summed, 1)

            multiply(0, 0)
            with dve.Fori(0, H // 2 - 1) as i:
                multiply(i * 2 + 1, 1)
                add_up(i * 2, 0)
                multiply(i * 2 + 2, 0)
                add_up(i * 2 + 1, 1)
            multiply(H - 1, 1)
            add_up(H - 2, 0)
            add_up(H - 1, 1)


def experts(nc, sh, gathered, results, tile_turn, turn_expert, turn_end, wu, wg, wd, ident):
    L, LC, F, NT, E = sh.L, sh.LC, sh.F, sh.NT, sh.E
    FC = F // P
    W = LC * 2 * F + FC * L
    WS = 4
    UP = LC * 2 * F
    with ExitStack() as ctx:
        take = ctx.enter_context(phase_semaphores(nc))

        def one(name, shape, dt=F32):
            return ctx.enter_context(nc.sbuf_tensor(f"{name}_expert", shape, dt))

        def pair(name, shape, dt=F32):
            return [one(f"{name}{k}", shape, dt) for k in range(2)]

        def bank2(name):
            return [ctx.enter_context(nc.psum_tensor(f"{name}{k}_expert", [P, L], F32)) for k in range(2)]

        def sem(name):
            return take(f"{name}_expert")

        def sem2(name):
            return [sem(f"{name}{k}") for k in range(2)]

        raw = pair("raw_weights", [P, W])
        w_hi, w_lo = one("weights_hi", [P, WS * W], F32R), one("weights_lo", [P, WS * W], F32R)
        rows = [one(f"rows{k}", [P, L]) for k in range(4)]
        xhi, xlo = pair("xT_hi", [P, LC * P], F32R), pair("xT_lo", [P, LC * P], F32R)
        gate, h = pair("gated", [P, F]), pair("hidden", [P, F])
        hhi, hlo = pair("hiddenT_hi", [P, F], F32R), pair("hiddenT_lo", [P, F], F32R)
        out = pair("out_rows", [P, L])
        psT, psU, psH, psY = bank2("turned"), bank2("up"), bank2("hidden_turned"), bank2("down")
        rows_loaded, stored, w_loaded = [sem(f"rows_loaded{k}") for k in range(4)], sem2("stored"), sem2("w_loaded")
        first_loaded, first_hi, first_split = sem2("first_loaded"), sem("first_hi"), sem("first_split")
        first_down_loaded = sem2("first_down_loaded")
        turned, x_hi, x_lo = sem("turned"), sem("x_hi"), sem("x_lo")
        up_done, silu_done, h_done, h_turned, h_hi, h_lo = (sem("up_done"), sem("silu_done"), sem("h_done"),
                                                            sem("h_turned"), sem("h_hi"), sem("h_lo"))
        down_done, copied = sem("down_done"), sem("copied")
        w_hi_done, w_ready, holds = sem("w_hi"), sem("w_ready"), sem("holds")
        block = ctx.enter_context(nc.Block())

        def tiles(eng, first, last, body):
            with eng.Fori(0, (last - first) // 4) as i:
                for k in range(4):
                    body(i * 4 + (first + k), (first + k) % 4)

        def run(eng, body, after_first=None):
            body(-2, 2)
            if after_first:
                after_first()
            for j in (-1, 0, 1):
                body(j, j % 4)
            tiles(eng, 2, 2 + (NT - 4) // 4 * 4, body)
            for j in range(2 + (NT - 4) // 4 * 4, NT + 1):
                body(j, j % 4)

        def there(j, ahead):
            return not isinstance(j, int) or 0 <= j + ahead < NT

        FIRST = ((0, 0, UP // 2, False), (0, UP // 2, UP // 2, False), (1, 0, UP, False),
                 (0, UP, W - UP, True), (1, UP, W - UP, True))

        def load_weights(eng, t, s, done, down_loaded):
            e = eng.value_load(turn_expert[0:1, bass.ds(t, 1)], min_val=0, max_val=E - 1)
            up = raw[s][:, 0:UP].rearrange("p (c n) -> p c n", c=LC)
            for n, w in enumerate((wu, wg)):
                eng.dma_start(up[:, :, n * F:(n + 1) * F],
                          w[bass.ds(e, 1)].rearrange("e (p c) n -> (e p) c n", c=LC)).then_inc(done, 16)
            eng.dma_start(raw[s][:, UP:W].rearrange("p (c n) -> p c n", c=FC),
                      wd[bass.ds(e, 1)].rearrange("e (p c) n -> (e p) c n", c=FC)).then_inc(down_loaded, 16)

        @block.sync
        def _(sp):
            for k in range(2):
                sp.sem_inc(stored[k], 16)

            def load(j, s):
                sp.wait_ge(turned, j + 1)
                sp.dma_start(rows[s][:, :], gathered[bass.ds(j * P, P), :]).then_inc(rows_loaded[s], 16)

            def body(j, s):
                if there(j, 5):
                    load(j + 5, (s + 5) % 4)
                if there(j, -1):
                    sp.wait_ge(copied, j + 2)
                    sp.dma_start(results[bass.ds((j - 1) * P, P), :], out[(s - 1) % 2][:, :]).then_inc(stored[(s - 1) % 2], 16)

            load(0, 0)
            load_weights(sp, 0, 0, first_loaded[0], first_down_loaded[0])
            load(1, 1)
            load(2, 2)
            load_weights(sp, 1, 1, first_loaded[1], first_down_loaded[1])
            run(sp, body)
            for k in range(2):
                sp.wait_ge(stored[k], 16 * ((NT + 1 - k) // 2 + 1))

        @block.scalar
        def _(act):
            act.sem_inc(copied, 2)

            def body(j, s):
                k = s % 2
                if there(j, 2):
                    act.wait_ge(turned, j + 2 + 5)
                    act.wait_ge(up_done, j + 2 + 1)
                    nc.scalar.activation(xhi[k][:, :], psT[k][:, :], ACT.Copy).then_inc(x_hi, 1)
                if there(j, 1):
                    act.wait_ge(up_done, j + 1 + 3)
                    nc.scalar.activation(gate[1 - k][:, :], psU[1 - k][:, 0:F], ACT.Silu).then_inc(silu_done, 1)
                if there(j, 0):
                    act.wait_ge(h_turned, j + 3)
                    act.wait_ge(down_done, j + 1)
                    nc.scalar.activation(hhi[k][:, :], psH[k][:, 0:F], ACT.Copy).then_inc(h_hi, 1)
                if there(j, -1):
                    act.wait_ge(down_done, j - 1 + 3)
                    act.wait_ge(stored[1 - k], (j - 1 - (1 - k)) * 8 + 16)
                    nc.scalar.copy(out[1 - k][:, :], psY[1 - k][:, :]).then_inc(copied, 1)

            def split(pieces):
                for e, start, size, down in pieces:
                    act.wait_ge((first_loaded, first_down_loaded)[down][e], (32, 16)[down])
                    nc.scalar.activation(w_hi[:, e * W + start:e * W + start + size], raw[e][:, start:start + size], ACT.Copy).then_inc(first_hi, 1)

            split(FIRST[:2])
            run(act, body, lambda: split(FIRST[2:]))

        @block.vector
        def _(dve):
            dve.sem_inc(x_lo, 2)
            dve.sem_inc(h_done, 2)
            dve.sem_inc(h_lo, 2)

            def body(j, s):
                k = s % 2
                if there(j, 2):
                    dve.wait_ge(x_hi, j + 2 + 1)
                    nc.vector.tensor_tensor(xlo[k][:, :], psT[k][:, :], f32(xhi[k][:, :]), ALU.subtract).then_inc(x_lo, 1)
                if there(j, 1):
                    dve.wait_ge(silu_done, j + 1 + 1)
                    dve.wait_ge(h_turned, j + 1 + 1)
                    nc.vector.tensor_tensor(h[1 - k][:, :], psU[1 - k][:, F:2 * F], gate[1 - k][:, :], ALU.mult).then_inc(h_done, 1)
                if there(j, 0):
                    dve.wait_ge(h_hi, j + 1)
                    nc.vector.tensor_tensor(hlo[k][:, :], psH[k][:, 0:F], f32(hhi[k][:, :]), ALU.subtract).then_inc(h_lo, 1)

            def split(pieces):
                for n in pieces:
                    e, start, size, down = FIRST[n]
                    to = slice(e * W + start, e * W + start + size)
                    dve.wait_ge(first_hi, n + 1)
                    part = nc.vector.tensor_tensor(w_lo[:, to], raw[e][:, start:start + size], f32(w_hi[:, to]), ALU.subtract)
                    if down:
                        part.then_inc(first_split, 1)
                    elif start + size == UP:
                        part.then_inc(w_ready, 1)

            split((0, 1))
            run(dve, body, lambda: split(range(2, len(FIRST))))

        @block.gpsimd
        def _(pool):
            def load(e, s):
                if isinstance(e, int) and e < WS:
                    pool.wait_ge(first_split, e - 1)
                else:
                    pool.wait_ge(w_ready, e - 1)
                pool.sem_inc(holds, 1)
                load_weights(pool, e, s % 2, w_loaded[s % 2], w_loaded[s % 2])

            def split(e, s, wait_tiles):
                if wait_tiles:
                    end = pool.value_load(turn_end[0:1, bass.ds(e - WS, 1)], min_val=0, max_val=NT)
                    pool.wait_ge(down_done, end + 2)
                    pool.sem_inc(holds, 1)
                pool.wait_ge(w_loaded[s % 2], (e - s % 2) * 24)
                pool.sem_inc(holds, 1)
                to = slice(s * W, (s + 1) * W)
                nc.gpsimd.tensor_scalar(w_hi[:, to], raw[s % 2][:, :], 1.0, None, ALU.mult).then_inc(w_hi_done, 1)
                pool.wait_ge(w_hi_done, e - 1)
                nc.gpsimd.tensor_tensor(w_lo[:, to], raw[s % 2][:, :], f32(w_hi[:, to]), ALU.subtract).then_inc(w_ready, 1)

            def body(e, s, wait_tiles=True):
                split(e, s, wait_tiles)
                load(e + 2, s)

            load(2, 2)
            load(3, 3)
            body(2, 2, False)
            body(3, 3, False)
            with pool.Fori(0, (E - 2 * WS) // WS) as i:
                for k in range(WS):
                    body(i * WS + (WS + k), k)
            for k in range(WS):
                e = E - WS + k
                split(e, k, True)
                if e + 2 < E:
                    load(e + 2, k)

        @block.tensor
        def _(pe):
            pe.sem_inc(turned, 4)
            pe.sem_inc(up_done, 2)
            pe.sem_inc(h_turned, 2)
            pe.sem_inc(down_done, 2)

            def turn(bank, src, done):
                for c, columns in enumerate(src):
                    last = nc.tensor.transpose(bank[:, c * P:(c + 1) * P], columns, ident[:, :])
                last.then_inc(done, 1)

            def products(bank, hi, lo, chunks, e, start, done):
                at = (e & (WS - 1)) * W + start
                for c in range(chunks):
                    part = slice(c * P, (c + 1) * P)
                    w = bass.ds(at + c * L, L)
                    nc.tensor.matmul(bank[:, :], hi[:, part], w_hi[:, w], start=c == 0, stop=False)
                    nc.tensor.matmul(bank[:, :], lo[:, part], w_hi[:, w], start=False, stop=False)
                    last = nc.tensor.matmul(bank[:, :], hi[:, part], w_lo[:, w], start=False, stop=c == chunks - 1)
                last.then_inc(done, 1)

            def turn_of(j):
                return pe.value_load(tile_turn[0:1, bass.ds(j, 1)], min_val=0, max_val=E - 1)

            def body(j, s):
                k = s % 2
                if there(j, 2):
                    pe.wait_ge(rows_loaded[(s + 2) % 4], (j + 2 - (s + 2) % 4) * 4 + 16)
                    pe.wait_ge(x_lo, j + 2 + 1)
                    turn(psT[k], [rows[(s + 2) % 4][:, c::LC] for c in range(LC)], turned)
                if there(j, 1):
                    e = turn_of(j + 1)
                    pe.wait_ge(w_ready, e + 1)
                    pe.wait_ge(x_lo, j + 1 + 3)
                    pe.wait_ge(h_done, j + 1 + 1)
                    products(psU[1 - k], xhi[1 - k], xlo[1 - k], LC, e, 0, up_done)
                if there(j, 0):
                    pe.wait_ge(h_done, j + 3)
                    pe.wait_ge(h_lo, j + 1)
                    turn(psH[k], [h[k][:, c::FC] for c in range(FC)], h_turned)
                if there(j, -1):
                    e = turn_of(j - 1)
                    if isinstance(j, int) and j < 2:
                        pe.wait_ge(first_split, 2)
                    pe.wait_ge(h_lo, j - 1 + 3)
                    pe.wait_ge(copied, j - 1 + 1)
                    products(psY[1 - k], hhi[1 - k], hlo[1 - k], FC, e, UP, down_done)

            run(pe, body)


def routing(nc, sh, sb, sem, logits, bias, slots, weights, tile_turn, turn_expert, turn_end, sums):
    E, TT, NT, R = sh.E, sh.TT, sh.NT, P
    bias_b = sb("bias", [P, E])
    choice = sb("choice", [P, TT, E])
    top = sb("top", [P, TT, 8])
    at = sb("top_at", [P, TT, 8], U32)
    at_f = sb("top_at_f", [P, 2, TT])
    expert_i, expert_id = sb("expert_ids_i", [P, E], I32), sb("expert_ids", [P, E])
    step_i, step_at = sb("tile_steps_i", [P, NT], I32), sb("tile_steps", [P, NT])
    hot = sb("hot", [P, 2, E, TT])
    both = sb("both", [P, E, TT])
    ones, before = sb("ones", [P, P]), sb("before", [P, P])
    ones_row = sb("ones_row", [P, E * TT])
    upto = sb("upto", [P, E, TT])
    counts = sb("counts", [P, E, TT])
    rank = sb("rank", [P, E, TT])
    count, tiles, tiles_upto, origin = sb("count", [P, E]), sb("tiles", [P, E]), sb("tiles_upto", [P, E]), sb("origin", [P, E])
    KT = sh.T // R
    full = sb("full", [P, E, KT])
    picked = sb("picked", [P, 2, E, TT])
    slot_f = sb("slot_f", [P, 2, TT])
    owner, owned = sb("owner", [P, NT, E]), sb("owned", [P, NT, E])
    some, turns_upto, turn_of = sb("some", [P, E]), sb("turns_upto", [P, E]), sb("turn_of", [P, E])
    passed, passed_tiles = sb("passed", [P, E, E]), sb("passed_tiles", [P, E, E])
    turn_expert_f, turn_end_f, over = sb("turn_expert_f", [P, E]), sb("turn_end_f", [P, E]), sb("over", [P, E])
    owner_f = sb("owner_f", [P, NT])
    peak, shifted, expd = sb("peak", [P, TT]), sb("shifted", [P, TT, E]), sb("expd", [P, TT, E])
    total, inverse, score = sb("total", [P, TT]), sb("inverse", [P, TT]), sb("score", [P, TT, E])
    kept, kept_sum, kept_inv = sb("kept", [P, 2, TT]), sb("kept_sum", [P, TT]), sb("kept_inv", [P, TT])
    bank = [s[:, 0:E * TT] for s in sums]
    before_part = sb("before_part", [P, E, TT])
    bias_loaded, made, both_done, counted, exp_done = (sem("bias_loaded"), sem("made"), sem("both_done"),
                                                       sem("counted"), sem("exp_done"))
    shift_done, step_done = sem("shift_done"), sem("step_done")
    counts_read, slots_ready = sem("counts_read"), sem("slots_ready")
    lg = logits[:, :].rearrange("p (t e) -> p t e", e=E)

    def load_bias(sp):
        sp.dma_start(bias_b[:, :], bias.rearrange("(a e) -> a e", a=1).partition_broadcast(P).rearrange("p a e -> p (a e)")).then_inc(bias_loaded, 16)

    def constants(pool):
        nc.gpsimd.iota(expert_i[:, :], [[1, E]], base=0, channel_multiplier=0).then_inc(made, 1)
        nc.gpsimd.iota(step_i[:, :], [[1, NT]], base=0, channel_multiplier=0).then_inc(made, 1)
        nc.gpsimd.memset(ones[:, :], 1.0).then_inc(made, 1)
        nc.gpsimd.memset(ones_row[:, :], 1.0).then_inc(made, 1)
        pool.wait_ge(made, 4)
        nc.gpsimd.affine_select(out=before[:, :], in_=ones[:, :], compare_op=ALU.is_gt, fill=0.0,
                                base=0, pattern=[[1, P]], channel_multiplier=-1).then_inc(made, 1)

    def exponentials(act):
        act.wait_ge(shift_done, 1)
        nc.scalar.activation(expd[:, :, :], shifted[:, :, :], ACT.Exp).then_inc(exp_done, 1)

    def count_tokens(pe):
        pe.wait_ge(made, 5)
        pe.wait_ge(both_done, 1)
        flat = both[:, :, :].rearrange("p e t -> p (e t)")
        nc.tensor.matmul(bank[0], before[:, :], flat, start=True, stop=True)
        nc.tensor.matmul(bank[1], ones[:, :], flat, start=True, stop=True).then_inc(counted, 1)

    steps = [0]
    v = nc.vector

    def then(ins):
        steps[0] += 1
        ins.then_inc(step_done, 1)
        nc.vector.wait_ge(step_done, steps[0])

    def choose(dve):
        dve.wait_ge(bias_loaded, 16)
        then(v.tensor_tensor(choice[:, :, :], lg, bias_b[:, :].unsqueeze(1).to_broadcast([P, TT, E]), ALU.add))
        for t in range(TT):
            last = v.max(top[:, t, :], choice[:, t, :])
        then(last)
        for t in range(TT):
            last = v.max_index(at[:, t, :], top[:, t, :], choice[:, t, :])
        then(last)
        then(v.tensor_copy(at_f[:, :, :], at[:, :, 0:2].rearrange("p t k -> p k t")))
        dve.wait_ge(made, 5)
        v.tensor_copy(step_at[:, :], step_i[:, :])
        then(v.tensor_copy(expert_id[:, :], expert_i[:, :]))
        for k in range(2):
            last = v.tensor_tensor(hot[:, k, :, :], expert_id[:, :].unsqueeze(2).to_broadcast([P, E, TT]),
                                   at_f[:, k, :].unsqueeze(1).to_broadcast([P, E, TT]), ALU.is_equal)
        then(last)
        v.tensor_tensor(both[:, :, :], hot[:, 0, :, :], hot[:, 1, :, :], ALU.add).then_inc(both_done, 1)

    def read_counts(dve):
        dve.wait_ge(counted, 1)
        v.tensor_copy(before_part[:, :, :], bank[0].rearrange("p (e t) -> p e t", t=TT)).then_inc(counts_read, 1)
        v.tensor_copy(counts[:, :, :], bank[1].rearrange("p (e t) -> p e t", t=TT)).then_inc(counts_read, 1)

    def rank_tokens(dve):
        dve.wait_ge(counts_read, 2)
        then(v.tensor_tensor_scan(upto[:, :, :].rearrange("p e t -> p (e t)"), ones_row[:, :],
                                  counts[:, :, :].rearrange("p e t -> p (e t)"), 0.0, ALU.mult, ALU.add))
        then(v.tensor_tensor(rank[:, :, :], upto[:, :, :], counts[:, :, :], ALU.subtract))
        then(v.tensor_tensor(count[:, :], upto[:, :, TT - 1], rank[:, :, 0], ALU.subtract))
        then(v.tensor_scalar(full[:, :, :], step_at[:, 0:KT].unsqueeze(1).to_broadcast([P, E, KT]), float(R), None, ALU.mult))
        then(v.tensor_tensor(full[:, :, :], count[:, :].unsqueeze(2).to_broadcast([P, E, KT]), full[:, :, :], ALU.is_gt))
        then(v.tensor_reduce(tiles[:, :], full[:, :, :], AX_X, ALU.add))
        then(v.tensor_tensor_scan(tiles_upto[:, :], ones_row[:, 0:E], tiles[:, :], 0.0, ALU.mult, ALU.add))
        then(v.tensor_tensor(origin[:, :], tiles_upto[:, :], tiles[:, :], ALU.subtract))
        then(v.tensor_scalar(origin[:, :], origin[:, :], float(R), None, ALU.mult))
        then(v.tensor_tensor(origin[:, :], origin[:, :], rank[:, :, 0], ALU.subtract))
        then(v.tensor_tensor(rank[:, :, :], rank[:, :, :], before_part[:, :, :], ALU.add))
        then(v.tensor_tensor(rank[:, :, :], rank[:, :, :], origin[:, :].unsqueeze(2).to_broadcast([P, E, TT]), ALU.add))
        for k in range(2):
            last = v.tensor_tensor(picked[:, k, :, :], hot[:, k, :, :], rank[:, :, :], ALU.mult)
        then(last)
        for k in range(2):
            last = v.tensor_reduce(slot_f[:, k, :], picked[:, k, :, :].rearrange("p e t -> p t e"), AX_X, ALU.add)
        then(last)
        v.tensor_copy(slots[:, :, :], slot_f[:, :, :]).then_inc(slots_ready, 1)

    def name_tiles(dve):
        then(v.tensor_scalar(some[:, :], tiles[:, :], 0.0, None, ALU.is_gt))
        then(v.tensor_tensor_scan(turns_upto[:, :], ones_row[:, 0:E], some[:, :], 0.0, ALU.mult, ALU.add))
        v.tensor_scalar(turn_of[:, :], turns_upto[:, :], 1.0, None, ALU.subtract)
        then(v.tensor_tensor(owner[:, :, :], tiles_upto[:, :].unsqueeze(1).to_broadcast([P, NT, E]),
                             step_at[:, :].unsqueeze(2).to_broadcast([P, NT, E]), ALU.is_le))
        then(v.tensor_tensor(owned[:, :, :], owner[:, :, :], some[:, :].unsqueeze(1).to_broadcast([P, NT, E]), ALU.mult))
        then(v.tensor_reduce(owner_f[:, :], owned[:, :, :], AX_X, ALU.add))
        then(v.tensor_scalar(owner_f[:, :], owner_f[:, :], float(E - 1), None, ALU.min))
        v.tensor_copy(tile_turn[:, :], owner_f[0:1, :])
        turn_at = step_at[:, 0:E].unsqueeze(2).to_broadcast([P, E, E])
        then(v.tensor_tensor(passed[:, :, :], turns_upto[:, :].unsqueeze(1).to_broadcast([P, E, E]), turn_at, ALU.is_le))
        then(v.tensor_reduce(turn_expert_f[:, :], passed[:, :, :], AX_X, ALU.add))
        then(v.tensor_scalar(turn_expert_f[:, :], turn_expert_f[:, :], float(E - 1), None, ALU.min))
        v.tensor_copy(turn_expert[:, :], turn_expert_f[0:1, :])
        then(v.tensor_tensor(passed[:, :, :], turn_of[:, :].unsqueeze(1).to_broadcast([P, E, E]), turn_at, ALU.is_le))
        then(v.tensor_tensor(passed_tiles[:, :, :], passed[:, :, :], tiles[:, :].unsqueeze(1).to_broadcast([P, E, E]), ALU.mult))
        then(v.tensor_reduce(turn_end_f[:, :], passed_tiles[:, :, :], AX_X, ALU.add))
        then(v.tensor_tensor(over[:, :], turns_upto[:, E - 1:E].to_broadcast([P, E]), step_at[:, 0:E], ALU.is_le))
        then(v.tensor_scalar(over[:, :], over[:, :], float(NT), None, ALU.mult))
        then(v.tensor_tensor(turn_end_f[:, :], turn_end_f[:, :], over[:, :], ALU.max))
        then(v.tensor_copy(turn_end[:, :], turn_end_f[0:1, :]))

    def weigh(dve):
        then(v.tensor_reduce(peak[:, :], lg, AX_X, ALU.max))
        v.tensor_tensor(shifted[:, :, :], lg, peak[:, :].unsqueeze(2).to_broadcast([P, TT, E]), ALU.subtract).then_inc(shift_done, 1)
        dve.wait_ge(exp_done, 1)
        then(v.tensor_reduce(total[:, :], expd[:, :, :], AX_X, ALU.add))
        then(v.reciprocal(inverse[:, :], total[:, :]))
        then(v.tensor_tensor(score[:, :, :], expd[:, :, :], inverse[:, :].unsqueeze(2).to_broadcast([P, TT, E]), ALU.mult))
        for k in range(2):
            last = v.tensor_tensor(picked[:, k, :, :], hot[:, k, :, :], score[:, :, :].rearrange("p t e -> p e t"), ALU.mult)
        then(last)
        for k in range(2):
            last = v.tensor_reduce(kept[:, k, :], picked[:, k, :, :].rearrange("p e t -> p t e"), AX_X, ALU.add)
        then(last)
        then(v.tensor_tensor(kept_sum[:, :], kept[:, 0, :], kept[:, 1, :], ALU.add))
        then(v.reciprocal(kept_inv[:, :], kept_sum[:, :]))
        then(v.tensor_tensor(weights[:, :, :], kept[:, :, :], kept_inv[:, :].unsqueeze(1).to_broadcast([P, 2, TT]), ALU.mult))

    return {"load_bias": load_bias, "constants": constants, "exponentials": exponentials, "count_tokens": count_tokens,
            "choose": choose, "read_counts": read_counts, "rank_tokens": rank_tokens, "name_tiles": name_tiles,
            "weigh": weigh}, counts_read, slots_ready


def shared_half(nc, sh, half, x_mid, x_normed, w, w_hi, w_lo, base, gathered, results, logits, bias,
                slots, weights, tile_turn, turn_expert, turn_end, out, ident):
    L, LC, R = sh.L, sh.LC, sh.R
    FS = w_hi[0].shape[2]
    FC = FS // P
    RT = R // P
    NT = sh.T // 2 // R
    TH = sh.TT // 2
    last_half = half == 1
    with ExitStack() as ctx:
        take = ctx.enter_context(phase_semaphores(nc))

        def one(name, shape, dt=F32):
            return ctx.enter_context(nc.sbuf_tensor(f"{name}_sh{half}", shape, dt))

        def pair(name, shape, dt=F32):
            return [one(f"{name}{k}", shape, dt) for k in range(2)]

        def ps(name, shape):
            return ctx.enter_context(nc.psum_tensor(f"{name}_sh{half}", shape, F32))

        def sem(name):
            return take(f"{name}_sh{half}")

        def sem2(name):
            return [sem(f"{name}{k}") for k in range(2)]

        rows = pair("rows", [P, RT, L])
        xhi, xlo = pair("xT_hi", [P, LC, R], F32R), pair("xT_lo", [P, LC, R], F32R)
        gate, h = pair("gated", [P, FC * R]), pair("hidden", [P, FC * R])
        hhi, hlo = pair("hidden_hi", [P, FC * R], F32R), pair("hidden_lo", [P, FC * R], F32R)
        xm, total = pair("x_mid", [P, RT, L]), pair("sum", [P, RT, L])
        psT, psU, psG = ps("turned", [P, LC, R]), ps("up", [P, FC * R]), ps("gate", [P, FC * R])
        psY = ps("down", [P, RT, L])
        rows_loaded, xm_loaded, stored = sem2("rows_loaded"), sem2("xm_loaded"), sem2("stored")
        turned, x_hi, x_lo = sem("turned"), sem("x_hi"), sem("x_lo")
        up_done, gate_done, silu_done, h_done, h_hi, h_lo = (sem("up_done"), sem("gate_done"), sem("silu_done"),
                                                             sem("h_done"), sem("h_hi"), sem("h_lo"))
        down_done, summed, finished = sem("down_done"), sem("summed"), sem("finished")
        if last_half:
            res, old_res = pair("results", [P, 2 * RT, L]), pair("old_results", [P, 2 * RT, L])
            acc, old_acc = one("partial", [P, RT, L]), one("old_partial", [P, RT, L])
            old_base, old_total = pair("old_base", [P, RT, L]), pair("old_sum", [P, RT, L])
            res_loaded, old_loaded, old_stored = sem2("res_loaded"), sem2("old_loaded"), sem2("old_stored")
            base_loaded = sem2("base_loaded")
            partial, both_added, old_partial, old_finished = sem("partial"), sem("both_added"), sem("old_partial"), sem("old_finished")
        else:
            NB = 4
            row = [one(f"dispatched{k}", [P, L]) for k in range(NB)]
            row_loaded, sent = [sem(f"row_loaded{k}") for k in range(NB)], [sem(f"sent{k}") for k in range(NB)]
            stage = [one(f"weights{n}", list(t.shape)) for n, t in enumerate(w_hi)]
            w_loaded = [sem(f"w_loaded{n}") for n in range(len(w))]
            w_hi_done, w_lo_done = sem("w_hi_done"), [sem(f"w_lo_done{n}") for n in range(len(w))]
            route, counts_read, slots_ready = routing(nc, sh, one, sem, logits, bias, slots, weights, tile_turn, turn_expert, turn_end, [psY[:, r, :] for r in range(2)])
        block = ctx.enter_context(nc.Block())

        def tiles(eng, first, last, body):
            with eng.Fori(0, (last - first) // 2) as i:
                for k in range(2):
                    body(i * 2 + (first + k), (first + k) % 2)

        def rows_of(t, j, which=half):
            return t[bass.ds(j * R + which * NT * R, R), :].rearrange("(r p) d -> p r d", p=P)

        @block.sync
        def _(sp):
            for k in range(2):
                sp.sem_inc(stored[k], 16)
                if last_half:
                    sp.sem_inc(old_stored[k], 16)

            def load(j, s):
                sp.wait_ge(turned, j + 1)
                sp.dma_start(rows[s][:, :, :], rows_of(x_normed, j)).then_inc(rows_loaded[s], 16)

            def load_late(j, s):
                sp.wait_ge(summed, j + 1)
                sp.dma_start(xm[s][:, :, :], rows_of(x_mid, j)).then_inc(xm_loaded[s], 16)
                if last_half:
                    sp.wait_ge(old_partial, j + 1)
                    sp.dma_start(old_base[s][:, :, :], rows_of(base, j, 0)).then_inc(base_loaded[s], 16)

            def store(j, s):
                if last_half:
                    sp.wait_ge(old_finished, j + 1)
                    sp.dma_start(rows_of(out, j, 0), old_total[s][:, :, :]).then_inc(old_stored[s], 16)
                    sp.wait_ge(finished, j + 1)
                else:
                    sp.wait_ge(summed, j + 3)
                sp.dma_start(rows_of(out if last_half else base, j), total[s][:, :, :]).then_inc(stored[s], 16)

            if not last_half:
                def load_weights(n):
                    sp.dma_start(stage[n][:, :, :], w[n].rearrange("(p c) n -> p c n", p=P)).then_inc(w_loaded[n], 16)

                route["load_bias"](sp)
                load_weights(0)
            load(0, 0)
            if not last_half:
                load_weights(1)
            load(1, 1)
            if not last_half:
                load_weights(2)
            load_late(0, 0)
            load(2, 0)

            def body(j, s):
                load(j + 3, 1 - s)
                load_late(j + 1, 1 - s)
                store(j, s)

            tiles(sp, 0, NT - 4, body)
            load(NT - 1, 1)
            for j in range(NT - 4, NT):
                if j + 1 < NT:
                    load_late(j + 1, (j + 1) % 2)
                store(j, j % 2)
            for k in range(2):
                sp.wait_ge(stored[k], 16 * (NT // 2 + 1))
                if last_half:
                    sp.wait_ge(old_stored[k], 16 * (NT // 2 + 1))

        @block.gpsimd
        def _(pool):
            if not last_half:
                def fetch(t):
                    if t >= NB:
                        pool.wait_ge(sent[t % NB], 32 * (t // NB))
                    pool.dma_start(row[t % NB][:, :], x_normed[t * P:(t + 1) * P, :]).then_inc(row_loaded[t % NB], 16)

                for n in range(1, len(w)):
                    pool.wait_ge(w_hi_done, n + 1)
                    nc.gpsimd.tensor_tensor(w_lo[n][:, :, :], stage[n][:, :, :], f32(w_hi[n][:, :, :]), ALU.subtract).then_inc(w_lo_done[n], 1)
                    if n == 1:
                        route["constants"](pool)
                for t in range(2):
                    fetch(t)
                pool.wait_ge(slots_ready, 1)
                for t in range(sh.TT):
                    if t + 2 < sh.TT:
                        fetch(t + 2)
                    pool.wait_ge(row_loaded[t % NB], 16 * (t // NB + 1))
                    for k in range(2):
                        pool.indirect_dma_start(out=gathered, out_offset=bass.IndirectOffsetOnAxis(ap=slots[:, k, t:t + 1], axis=0),
                                                in_=row[t % NB][:, :], in_offset=None).then_inc(sent[t % NB], 16)
                for k in range(NB):
                    pool.wait_ge(sent[k], 32 * (sh.TT // NB))
            else:
                for j in range(NT):
                    for y, loaded, read, t0 in ((old_res, old_loaded, old_finished, 0), (res, res_loaded, finished, TH)):
                        if j >= 2:
                            pool.wait_ge(read, j - 1)
                        for r in range(RT):
                            for k in range(2):
                                at = slots[:, k, t0 + j * RT + r:t0 + j * RT + r + 1]
                                pool.indirect_dma_start(out=y[j % 2][:, 2 * r + k, :], out_offset=None, in_=results,
                                                        in_offset=bass.IndirectOffsetOnAxis(ap=at, axis=0)).then_inc(loaded[j % 2], 16)

        @block.scalar
        def _(act):
            act.sem_inc(silu_done, 1)

            def high(j, s):
                act.wait_ge(turned, j + 3)
                nc.scalar.activation(xhi[s][:, :, :], psT[:, :, :], ACT.Copy).then_inc(x_hi, 1)

            def hidden(j, s):
                act.wait_ge(up_done, j + 1)
                nc.scalar.activation(gate[s][:, :], psU[:, :], ACT.Silu).then_inc(silu_done, 1)
                act.wait_ge(h_done, j + 2)
                nc.scalar.activation(hhi[s][:, :], h[s][:, :], ACT.Copy).then_inc(h_hi, 1)

            if last_half:
                high(0, 0)
                high(1, 1)
            else:
                for n in range(len(w)):
                    act.wait_ge(w_loaded[n], 16)
                    nc.scalar.activation(w_hi[n][:, :, :], stage[n][:, :, :], ACT.Copy).then_inc(w_hi_done, 1)
                    if n < 2:
                        high(n, n)
            hidden(0, 0)

            def body(j, s):
                high(j + 2, s)
                hidden(j + 1, 1 - s)

            first = 0
            if not last_half:
                first = 2
                body(0, 0)
                body(1, 1)
                route["exponentials"](act)
            tiles(act, first, NT - 2, body)
            hidden(NT - 1, 1)

        @block.vector
        def _(dve):
            dve.sem_inc(h_done, 1)
            dve.sem_inc(x_lo, 1)
            dve.sem_inc(summed, 2)
            if last_half:
                dve.sem_inc(old_partial, 2)

            def low(j, s):
                dve.wait_ge(x_hi, j + 1)
                nc.vector.tensor_tensor(xlo[s][:, :, :], psT[:, :, :], f32(xhi[s][:, :, :]), ALU.subtract).then_inc(x_lo, 1)

            def hidden(j, s):
                dve.wait_ge(silu_done, j + 2)
                dve.wait_ge(gate_done, j + 1)
                nc.vector.tensor_tensor(h[s][:, :], psG[:, :], gate[s][:, :], ALU.mult).then_inc(h_done, 1)
                dve.wait_ge(h_hi, j + 1)
                nc.vector.tensor_tensor(hlo[s][:, :], h[s][:, :], f32(hhi[s][:, :]), ALU.subtract).then_inc(h_lo, 1)

            def add_result(dst, src, y, k, t, done):
                for r in range(RT):
                    last = nc.vector.scalar_tensor_tensor(out=dst[:, r, :], in0=y[:, 2 * r + k, :], scalar=weights[:, k, bass.ds(t + r, 1)],
                                                          in1=src[:, r, :], op0=ALU.mult, op1=ALU.add)
                last.then_inc(done, 1)

            def old_rows(j, s):
                dve.wait_ge(base_loaded[s], (j - s) * 8 + 16)
                dve.wait_ge(old_loaded[s], (j - s) * (8 * 2 * RT) + 16 * 2 * RT)
                add_result(old_acc, old_base[s], old_res[s], 0, j * RT, old_partial)
                dve.wait_ge(old_partial, j + 3)
                dve.wait_ge(old_stored[s], (j - s) * 8 + 16)
                add_result(old_total[s], old_acc, old_res[s], 1, j * RT, old_finished)

            def add_results(j, s):
                dve.wait_ge(xm_loaded[s], (j - s) * 8 + 16)
                dve.wait_ge(res_loaded[s], (j - s) * (8 * 2 * RT) + 16 * 2 * RT)
                add_result(acc, xm[s], res[s], 0, j * RT + TH, partial)
                dve.wait_ge(partial, j + 1)
                add_result(acc, acc, res[s], 1, j * RT + TH, both_added)

            def sums(j, s):
                dve.wait_ge(down_done, j + 1)
                dve.wait_ge(stored[s], (j - s) * 8 + 16)
                if last_half:
                    dve.wait_ge(both_added, j + 1)
                    nc.vector.tensor_tensor(total[s][:, :, :], psY[:, :, :], acc[:, :, :], ALU.add).then_inc(summed, 1)
                    dve.wait_ge(summed, j + 3)
                    dve.sem_inc(finished, 1)
                else:
                    dve.wait_ge(xm_loaded[s], (j - s) * 8 + 16)
                    nc.vector.tensor_tensor(total[s][:, :, :], psY[:, :, :], xm[s][:, :, :], ALU.add).then_inc(summed, 1)

            if not last_half:
                dve.wait_ge(w_hi_done, 1)
                nc.vector.tensor_tensor(w_lo[0][:, :, :], stage[0][:, :, :], f32(w_hi[0][:, :, :]), ALU.subtract).then_inc(w_lo_done[0], 1)
            low(0, 0)
            low(1, 1)
            if not last_half:
                route["choose"](dve)
            hidden(0, 0)

            def body(j, s):
                low(j + 2, s)
                if last_half:
                    old_rows(j, s)
                    add_results(j, s)
                hidden(j + 1, 1 - s)
                sums(j, s)

            first = 0
            if not last_half:
                first = 2
                route["read_counts"](dve)
                route["rank_tokens"](dve)
                body(0, 0)
                route["name_tiles"](dve)
                body(1, 1)
                route["weigh"](dve)
            tiles(dve, first, NT - 2, body)
            if last_half:
                old_rows(NT - 2, 0)
                add_results(NT - 2, 0)
            hidden(NT - 1, 1)
            sums(NT - 2, 0)
            if last_half:
                old_rows(NT - 1, 1)
                add_results(NT - 1, 1)
            sums(NT - 1, 1)

        @block.tensor
        def _(pe):
            pe.sem_inc(turned, 2)

            def turn(j, s):
                pe.wait_ge(rows_loaded[s], (j - s) * 8 + 16)
                pe.wait_ge(x_lo, j + 1)
                for r in range(RT):
                    for c in range(LC):
                        last = nc.tensor.transpose(psT[:, c, r * P:(r + 1) * P], rows[s][:, r, c::LC], ident[:, :])
                last.then_inc(turned, 1)

            def up(j, s):
                pe.wait_ge(x_lo, j + 2)
                for n, (bank, done) in enumerate(((psU, up_done), (psG, gate_done))):
                    if not last_half:
                        pe.wait_ge(w_lo_done[n], 1)
                    pe.wait_ge((silu_done, h_done)[n], j + 1)
                    for fc in range(FC):
                        f = slice(fc, FS, FC)
                        for c in range(LC):
                            last = three_passes(nc, bank[:, fc * R:(fc + 1) * R], w_hi[n][:, c, f], w_lo[n][:, c, f],
                                                xhi[s][:, c, :], xlo[s][:, c, :], c == 0, c == LC - 1)
                    last.then_inc(done, 1)

            def down(j, s):
                if not last_half:
                    pe.wait_ge(w_lo_done[2], 1)
                pe.wait_ge(h_lo, j + 1)
                pe.wait_ge(summed, j + 2)
                for r in range(RT):
                    for fc in range(FC):
                        col = slice(fc * R + r * P, fc * R + (r + 1) * P)
                        last = three_passes(nc, psY[:, r, :], hhi[s][:, col], hlo[s][:, col],
                                            w_hi[2][:, fc, :], w_lo[2][:, fc, :], fc == 0, fc == FC - 1)
                last.then_inc(down_done, 1)

            turn(0, 0)
            turn(1, 1)
            up(0, 0)

            def body(j, s):
                turn(j + 2, s)
                up(j + 1, 1 - s)
                down(j, s)

            first = 0
            if not last_half:
                first = 2
                turn(2, 0)
                route["count_tokens"](pe)
                up(1, 1)
                pe.wait_ge(counts_read, 2)
                down(0, 0)
                body(1, 1)
            tiles(pe, first, NT - 2, body)
            up(NT - 1, 1)
            down(NT - 2, 0)
            down(NT - 1, 1)


def program(nc, x, context, taps, skip, router, bias, wu, wg, wd, su, sg, sd, out):
    sh = Shapes(x, taps, router, wu)
    rows, context_rows = x.rearrange("b s l -> (b s) l"), context.rearrange("b s l -> (b s) l")

    out = out.rearrange("b s l -> (b s) l")

    def dram(name, shape):
        return nc.dram_tensor(name, shape, F32).ap()

    taps_rev = dram("taps_rev", (sh.H, sh.RB))
    x_mid, x_normed, base = dram("x_mid", (sh.T, sh.L)), dram("x_mid_normed", (sh.T, sh.L)), dram("base", (sh.T // 2, sh.L))
    gathered, results = dram("gathered", (sh.GR, sh.L)), dram("results", (sh.NT * P, sh.L))
    with ExitStack() as ctx:
        def sb(name, shape, dt=F32, scope=ctx):
            return scope.enter_context(nc.sbuf_tensor(name, shape, dt))

        ident, eps, router_T = sb("identity", [P, P]), sb("eps", [P, 1]), sb("router_T", [P, sh.LC, sh.E])
        logits = sb("logits", [P, sh.TT * sh.E])
        prepare(nc, sh, taps, skip, router, taps_rev, router_T, ident, eps)
        slots, weights, tile_turn = sb("slots", [P, 2, sh.TT], U32), sb("weights", [P, 2, sh.TT]), sb("tile_turn", [1, sh.NT], I32)
        turn_expert, turn_end = sb("turn_expert", [1, sh.E], I32), sb("turn_end", [1, sh.E], I32)
        shared = (su[0], sg[0], sd[0])
        with ExitStack() as attention:
            cT, qT0, qT1 = (sb(name, [P, sh.LC * sh.HB * sh.H * sh.CE], F32, attention) for name in ("cT", "qT0", "qT1"))
            for leaving, entering, oT, qT in ((None, 0, None, qT0), (0, 1, qT0, qT1), (1, None, qT1, None)):
                change_rows(nc, sh, leaving, entering, rows, context_rows, cT, qT, oT, x_mid, x_normed, router_T, logits, ident, eps)
                if entering is not None:
                    long_convolution(nc, sh, entering, taps_rev, cT, qT, gathered)
        s_hi, s_lo = ([sb(f"shared_{part}{n}", [P, w.shape[0] // P, w.shape[1]], F32R) for n, w in enumerate(shared)] for part in ("hi", "lo"))
        for half in range(2):
            shared_half(nc, sh, half, x_mid, x_normed, shared, s_hi, s_lo, base, gathered, results, logits, bias, slots, weights, tile_turn, turn_expert, turn_end, out, ident)
            if half == 0:
                experts(nc, sh, gathered, results, tile_turn, turn_expert, turn_end, wu, wg, wd, ident)


_INS = ['x', 'ctx_2048', 'L0_xattn_ssm_kernel', 'L0_xattn_D', 'L0_ffn_router_w', 'L0_ffn_router_bias',
        'L0_ffn_Wu', 'L0_ffn_Wg', 'L0_ffn_Wd', 'L0_ffn_Su', 'L0_ffn_Sg', 'L0_ffn_Sd']


def kernel(**inputs):
    import numpy as _np
    import concourse.bacc as _bacc
    from concourse import mybir as _mybir
    from concourse.bass_utils import run_bass_kernel_spmd as _run

    nc = _bacc.Bacc("TRN2", target_bir_lowering=False, num_devices=1)
    arrays, args = {}, []
    for name in _INS:
        a = _np.ascontiguousarray(inputs[name])
        arrays[f"in_{name}"] = a
        args.append(nc.dram_tensor(f"in_{name}", a.shape, _mybir.dt.from_np(a.dtype), kind="ExternalInput").ap())
    out = nc.dram_tensor("out", inputs["x"].shape, _mybir.dt.from_np(_np.dtype("float32")), kind="ExternalOutput").ap()
    program(nc, *args, out)
    r = _run(nc, [arrays], core_ids=[0])
    return r.results[0]["out"]
```
